# Optimizing a Trainium2 kernel written in Bass

```python
import numpy as np
import jax
import jax.numpy as jnp

def _softmax(x, axis=-1):
    return jax.nn.softmax(x, axis=axis)

def _gelu(x):
    return jax.nn.gelu(x, approximate=True)

def _silu(x):
    return jax.nn.silu(x)

def _sigmoid(x):
    return jax.nn.sigmoid(x)

def _layernorm(x, axis=-1, eps=1e-05):
    m = jnp.mean(x, axis=axis, keepdims=True)
    v = jnp.var(x, axis=axis, keepdims=True)
    return (x - m) / jnp.sqrt(v + eps)

def _scatter_add(tgt, idx, src, axis=0):
    return tgt.at[idx].add(src)

def _segment_sum(src, seg, n):
    return jax.ops.segment_sum(src, seg, n)
kernel_name = 'mk_gnn_resnorm_d4_gnn_r8_297adb'

def setup_inputs(seed: int=0):
    np.random.seed(seed)
    _w = jnp.asarray

    def _rec_inputs():
        import jax
        import jax.numpy as jnp
        _gk = jax.random.key(seed)
        x = -0.000202 + 1 * jax.random.normal(jax.random.fold_in(_gk, 1), (6250, 128), jnp.float32)
        src = jax.random.randint(jax.random.fold_in(_gk, 2), (100000,), 0, 6250, jnp.int32)
        dst = jax.random.randint(jax.random.fold_in(_gk, 3), (100000,), 0, 6250, jnp.int32)
        _o = jnp.argsort(dst, stable=True)
        src = src[_o]
        dst = dst[_o]
        edge_attr_128 = -5.16925e-05 + 1.00005 * jax.random.normal(jax.random.fold_in(_gk, 12), (100000, 128), jnp.float32)
        edge_type_16 = jax.random.randint(jax.random.fold_in(_gk, 14), (100000,), 0, 16, jnp.int32)
        edge_type_4 = jax.random.randint(jax.random.fold_in(_gk, 15), (100000,), 0, 4, jnp.int32)
        edge_weight = jax.random.uniform(jax.random.fold_in(_gk, 16), (100000,), jnp.float32, 0.0, 1)
        return (x, src, dst, edge_attr_128, edge_type_16, edge_type_4, edge_weight)
    x, src, dst, edge_attr_128, edge_type_16, edge_type_4, edge_weight = _rec_inputs()

    def _L0_gnn_setup():
        import jax, jax.numpy as jnp
        import numpy as np
        N, E, IN_DIM, OUT_DIM, HEADS = (6250, 100000, 128, 32, 4)

        def _linear_params(key, fan_in, fan_out, bias=True):
            kw, kb = jax.random.split(key)
            s = 1.0 / np.sqrt(fan_in)
            W = jax.random.uniform(kw, (fan_in, fan_out), jnp.float32, -s, s)
            b = jax.random.uniform(kb, (fan_out,), jnp.float32, -s, s) if bias else None
            return (W, b)

        def _transformer_conv(x, src, dst, ea, Wq, bq, Wk, bk, Wv, bv, We, Ws, bs, H, C):
            n = x.shape[0]
            q = (x @ Wq + bq).reshape(n, H, C)
            k = (x @ Wk + bk).reshape(n, H, C)
            v = (x @ Wv + bv).reshape(n, H, C)
            e = (ea @ We).reshape(-1, H, C)
            kj = k[src] + e
            vj = v[src] + e
            alpha = jnp.einsum('ehc,ehc->eh', q[dst], kj) / jnp.sqrt(jnp.asarray(C, x.dtype))
            amax = jax.ops.segment_max(alpha, dst, num_segments=n)
            p = jnp.exp(alpha - amax[dst])
            denom = jax.ops.segment_sum(p, dst, num_segments=n)
            w = p / denom[dst]
            msg = (vj * w[..., None]).reshape(-1, H * C)
            out = jax.ops.segment_sum(msg, dst, num_segments=n)
            return out + x @ Ws + bs
        key = jax.random.key(seed)
        ks = jax.random.split(key, 24)
        H, C = (HEADS, OUT_DIM)
        inp = {'x': jax.random.normal(ks[0], (N, IN_DIM), jnp.float32), 'edge_weight': jax.random.uniform(ks[1], (E,), jnp.float32)}
        for li, fan_in in ((1, IN_DIM), (2, H * C)):
            base = 2 + (li - 1) * 10
            inp[f'Wq{li}'], inp[f'bq{li}'] = _linear_params(ks[base + 0], fan_in, H * C)
            inp[f'Wk{li}'], inp[f'bk{li}'] = _linear_params(ks[base + 1], fan_in, H * C)
            inp[f'Wv{li}'], inp[f'bv{li}'] = _linear_params(ks[base + 2], fan_in, H * C)
            We, _ = _linear_params(ks[base + 3], 1, H * C, bias=False)
            inp[f'We{li}'] = We
            inp[f'Ws{li}'], inp[f'bs{li}'] = _linear_params(ks[base + 4], fan_in, H * C)
        inp['edge_index'] = jax.random.randint(ks[22], (2, E), 0, N, jnp.int64)
        return inp
    _L0_gnn_all = _L0_gnn_setup()
    _L0_gnn_in = {k: v for k, v in _L0_gnn_all.items() if k in ('Wq1', 'bq1', 'Wk1', 'bk1', 'Wv1', 'bv1', 'We1', 'Ws1', 'bs1', 'Wq2', 'bq2', 'Wk2', 'bk2', 'Wv2', 'bv2', 'We2', 'Ws2', 'bs2')}
    del _L0_gnn_all

    def _L1_gnn_setup():
        import jax, jax.numpy as jnp
        import numpy as np
        N_NODES = 6250
        N_EDGES = 100000
        D = 128

        def _layer_norm(h, gamma, beta, eps=1e-05):
            mu = jnp.mean(h, axis=-1, keepdims=True)
            var = jnp.mean(jnp.square(h - mu), axis=-1, keepdims=True)
            return (h - mu) * jax.lax.rsqrt(var + eps) * gamma + beta
        key = jax.random.key(seed)
        ks = jax.random.split(key, 6)
        s1 = 1.0 / np.sqrt(2 * D)
        s2 = 1.0 / np.sqrt(2 * D)
        return {'x': jax.random.normal(ks[0], (N_NODES, D), dtype=jnp.float32), 'edge_index': jax.random.randint(ks[1], (2, N_EDGES), 0, N_NODES, dtype=jnp.int32), 'edge_attr': jax.random.normal(ks[2], (N_EDGES, D), dtype=jnp.float32), 'W1': jax.random.normal(ks[3], (2 * D, 2 * D), dtype=jnp.float32) * s1, 'b1': jnp.zeros((2 * D,), dtype=jnp.float32), 'W2': jax.random.normal(ks[4], (2 * D, D), dtype=jnp.float32) * s2, 'b2': jnp.zeros((D,), dtype=jnp.float32), 'ln_gamma': jnp.ones((D,), dtype=jnp.float32), 'ln_beta': jnp.zeros((D,), dtype=jnp.float32)}
    _L1_gnn_all = _L1_gnn_setup()
    _L1_gnn_in = {k: v for k, v in _L1_gnn_all.items() if k in ('W1', 'b1', 'W2', 'b2', 'ln_gamma', 'ln_beta')}
    del _L1_gnn_all

    def _L2_gnn_setup():
        import jax, jax.numpy as jnp
        import numpy as np
        N, R, D, RD, B, E = (6250, 16, 128, 32, 8, 100000)
        IN = 2 * D + RD
        key = jax.random.key(seed)
        ks = jax.random.split(key, 11)
        return {'node_emb': jax.random.normal(ks[0], (N, D), jnp.float32), 'edge_embeddings': jax.random.normal(ks[1], (R, RD), jnp.float32) * 0.1, 'basis_s': jax.random.normal(ks[2], (B, IN), jnp.float32) * 0.05, 'coef_s': jax.random.normal(ks[3], (R, B), jnp.float32) * 0.3, 'b_s': jax.random.normal(ks[4], (R,), jnp.float32) * 0.1, 'basis_r': jax.random.normal(ks[5], (B, IN), jnp.float32) * 0.05, 'coef_r': jax.random.normal(ks[6], (R, B), jnp.float32) * 0.3, 'b_r': jax.random.normal(ks[7], (R,), jnp.float32) * 0.1, 'src': jax.random.randint(ks[8], (E,), 0, N, jnp.int32), 'dst': jax.random.randint(ks[9], (E,), 0, N, jnp.int32), 'etype': jax.random.randint(ks[10], (E,), 0, R, jnp.int32)}
    _L2_gnn_all = _L2_gnn_setup()
    _L2_gnn_in = {k: v for k, v in _L2_gnn_all.items() if k in ('edge_embeddings', 'basis_s', 'coef_s', 'b_s', 'basis_r', 'coef_r', 'b_r')}
    del _L2_gnn_all

    def _L3_gnn_setup():
        import jax, jax.numpy as jnp
        import numpy as np
        NUM_RELATIONS = 4
        N_NODES = 2500
        N_EDGES = 40000
        F_IN = 128
        HID = 128
        EMB = 128

        def _rgcn_conv(x, src, dst, edge_type, edge_weight, W, root, bias):
            xj = x[src]
            m = jnp.zeros((xj.shape[0], W.shape[2]), dtype=x.dtype)
            for r in range(W.shape[0]):
                mask = (edge_type == r).astype(x.dtype)[:, None]
                m = m + mask * (xj @ W[r])
            m = m * edge_weight[:, None]
            out = jax.ops.segment_sum(m, dst, num_segments=x.shape[0])
            return out + x @ root + bias
        key = jax.random.key(seed)
        ks = jax.random.split(key, 10)
        return {'x': jax.random.normal(ks[0], (N_NODES, F_IN), dtype=jnp.float32), 'edge_index': jax.random.randint(ks[1], (2, N_EDGES), 0, N_NODES, dtype=jnp.int64 if jax.config.jax_enable_x64 else jnp.int32).astype(jnp.int32), 'edge_type': jax.random.randint(ks[2], (N_EDGES,), 0, NUM_RELATIONS).astype(jnp.int32), 'edge_weight': jax.random.uniform(ks[3], (N_EDGES,), dtype=jnp.float32), 'W1': jax.random.normal(ks[4], (NUM_RELATIONS, F_IN, HID), dtype=jnp.float32) * 0.05, 'root1': jax.random.normal(ks[5], (F_IN, HID), dtype=jnp.float32) * 0.05, 'b1': jax.random.normal(ks[6], (HID,), dtype=jnp.float32) * 0.05, 'W2': jax.random.normal(ks[7], (NUM_RELATIONS, HID, EMB), dtype=jnp.float32) * 0.05, 'root2': jax.random.normal(ks[8], (HID, EMB), dtype=jnp.float32) * 0.05, 'b2': jax.random.normal(ks[9], (EMB,), dtype=jnp.float32) * 0.05}
    _L3_gnn_all = _L3_gnn_setup()
    _L3_gnn_in = {k: v for k, v in _L3_gnn_all.items() if k in ('W1', 'root1', 'b1', 'W2', 'root2', 'b2')}
    del _L3_gnn_all
    return {'x': x, 'src': src, 'dst': dst, 'edge_attr_128': edge_attr_128, 'edge_type_16': edge_type_16, 'edge_type_4': edge_type_4, 'edge_weight': edge_weight, 'L0_gnn_Wq1': _L0_gnn_in['Wq1'], 'L0_gnn_bq1': _L0_gnn_in['bq1'], 'L0_gnn_Wk1': _L0_gnn_in['Wk1'], 'L0_gnn_bk1': _L0_gnn_in['bk1'], 'L0_gnn_Wv1': _L0_gnn_in['Wv1'], 'L0_gnn_bv1': _L0_gnn_in['bv1'], 'L0_gnn_We1': _L0_gnn_in['We1'], 'L0_gnn_Ws1': _L0_gnn_in['Ws1'], 'L0_gnn_bs1': _L0_gnn_in['bs1'], 'L0_gnn_Wq2': _L0_gnn_in['Wq2'], 'L0_gnn_bq2': _L0_gnn_in['bq2'], 'L0_gnn_Wk2': _L0_gnn_in['Wk2'], 'L0_gnn_bk2': _L0_gnn_in['bk2'], 'L0_gnn_Wv2': _L0_gnn_in['Wv2'], 'L0_gnn_bv2': _L0_gnn_in['bv2'], 'L0_gnn_We2': _L0_gnn_in['We2'], 'L0_gnn_Ws2': _L0_gnn_in['Ws2'], 'L0_gnn_bs2': _L0_gnn_in['bs2'], 'L1_gnn_W1': _L1_gnn_in['W1'], 'L1_gnn_b1': _L1_gnn_in['b1'], 'L1_gnn_W2': _L1_gnn_in['W2'], 'L1_gnn_b2': _L1_gnn_in['b2'], 'L1_gnn_ln_gamma': _L1_gnn_in['ln_gamma'], 'L1_gnn_ln_beta': _L1_gnn_in['ln_beta'], 'L2_gnn_edge_embeddings': _L2_gnn_in['edge_embeddings'], 'L2_gnn_basis_s': _L2_gnn_in['basis_s'], 'L2_gnn_coef_s': _L2_gnn_in['coef_s'], 'L2_gnn_b_s': _L2_gnn_in['b_s'], 'L2_gnn_basis_r': _L2_gnn_in['basis_r'], 'L2_gnn_coef_r': _L2_gnn_in['coef_r'], 'L2_gnn_b_r': _L2_gnn_in['b_r'], 'L3_gnn_W1': _L3_gnn_in['W1'], 'L3_gnn_root1': _L3_gnn_in['root1'], 'L3_gnn_b1': _L3_gnn_in['b1'], 'L3_gnn_W2': _L3_gnn_in['W2'], 'L3_gnn_root2': _L3_gnn_in['root2'], 'L3_gnn_b2': _L3_gnn_in['b2']}

def reference(x, src, dst, edge_attr_128, edge_type_16, edge_type_4, edge_weight, L0_gnn_Wq1, L0_gnn_bq1, L0_gnn_Wk1, L0_gnn_bk1, L0_gnn_Wv1, L0_gnn_bv1, L0_gnn_We1, L0_gnn_Ws1, L0_gnn_bs1, L0_gnn_Wq2, L0_gnn_bq2, L0_gnn_Wk2, L0_gnn_bk2, L0_gnn_Wv2, L0_gnn_bv2, L0_gnn_We2, L0_gnn_Ws2, L0_gnn_bs2, L1_gnn_W1, L1_gnn_b1, L1_gnn_W2, L1_gnn_b2, L1_gnn_ln_gamma, L1_gnn_ln_beta, L2_gnn_edge_embeddings, L2_gnn_basis_s, L2_gnn_coef_s, L2_gnn_b_s, L2_gnn_basis_r, L2_gnn_coef_r, L2_gnn_b_r, L3_gnn_W1, L3_gnn_root1, L3_gnn_b1, L3_gnn_W2, L3_gnn_root2, L3_gnn_b2):
    import jax
    import jax.numpy as jnp

    def _L0_gnn_ref(x, edge_weight, Wq1, bq1, Wk1, bk1, Wv1, bv1, We1, Ws1, bs1, Wq2, bq2, Wk2, bk2, Wv2, bv2, We2, Ws2, bs2, edge_index):
        import jax, jax.numpy as jnp
        import numpy as np
        N, E, IN_DIM, OUT_DIM, HEADS = (6250, 100000, 128, 32, 4)

        def _linear_params(key, fan_in, fan_out, bias=True):
            kw, kb = jax.random.split(key)
            s = 1.0 / np.sqrt(fan_in)
            W = jax.random.uniform(kw, (fan_in, fan_out), jnp.float32, -s, s)
            b = jax.random.uniform(kb, (fan_out,), jnp.float32, -s, s) if bias else None
            return (W, b)

        def _transformer_conv(x, src, dst, ea, Wq, bq, Wk, bk, Wv, bv, We, Ws, bs, H, C):
            n = x.shape[0]
            q = (x @ Wq + bq).reshape(n, H, C)
            k = (x @ Wk + bk).reshape(n, H, C)
            v = (x @ Wv + bv).reshape(n, H, C)
            e = (ea @ We).reshape(-1, H, C)
            kj = k[src] + e
            vj = v[src] + e
            alpha = jnp.einsum('ehc,ehc->eh', q[dst], kj) / jnp.sqrt(jnp.asarray(C, x.dtype))
            amax = jax.ops.segment_max(alpha, dst, num_segments=n)
            p = jnp.exp(alpha - amax[dst])
            denom = jax.ops.segment_sum(p, dst, num_segments=n)
            w = p / denom[dst]
            msg = (vj * w[..., None]).reshape(-1, H * C)
            out = jax.ops.segment_sum(msg, dst, num_segments=n)
            return out + x @ Ws + bs
        src, dst = (edge_index[0], edge_index[1])
        ea = edge_weight[:, None]
        h = _transformer_conv(x, src, dst, ea, Wq1, bq1, Wk1, bk1, Wv1, bv1, We1, Ws1, bs1, HEADS, OUT_DIM)
        out = _transformer_conv(h, src, dst, ea, Wq2, bq2, Wk2, bk2, Wv2, bv2, We2, Ws2, bs2, HEADS, OUT_DIM)
        return out

    def _L1_gnn_ref(x, edge_index, edge_attr, W1, b1, W2, b2, ln_gamma, ln_beta):
        import jax, jax.numpy as jnp
        import numpy as np
        N_NODES = 6250
        N_EDGES = 100000
        D = 128

        def _layer_norm(h, gamma, beta, eps=1e-05):
            mu = jnp.mean(h, axis=-1, keepdims=True)
            var = jnp.mean(jnp.square(h - mu), axis=-1, keepdims=True)
            return (h - mu) * jax.lax.rsqrt(var + eps) * gamma + beta
        j = edge_index[1]
        agg = jax.ops.segment_sum(edge_attr, j, num_segments=x.shape[0])
        out = jnp.concatenate([x, agg], axis=-1)
        h = jax.nn.silu(out @ W1 + b1)
        h = h @ W2 + b2
        h = _layer_norm(h, ln_gamma, ln_beta)
        return x + h

    def _L2_gnn_ref(node_emb, edge_embeddings, basis_s, coef_s, b_s, basis_r, coef_r, b_r, src, dst, etype):
        import jax, jax.numpy as jnp
        import numpy as np
        N, R, D, RD, B, E = (6250, 16, 128, 32, 8, 100000)
        IN = 2 * D + RD
        n, d = node_emb.shape
        r = edge_embeddings.shape[0]
        w_s = coef_s @ basis_s
        ws_src, ws_dst, ws_rel = (w_s[:, :d], w_s[:, d:2 * d], w_s[:, 2 * d:])
        S_src = node_emb @ ws_src.T
        S_dst = node_emb @ ws_dst.T
        s_rel = jnp.sum(edge_embeddings * ws_rel, axis=-1) + b_s
        score = S_src[src, etype] + S_dst[dst, etype] + s_rel[etype]
        seg = dst * r + etype
        seg_max = jax.ops.segment_max(score, seg, num_segments=n * r)
        seg_max = jnp.where(jnp.isfinite(seg_max), seg_max, 0.0)
        ex = jnp.exp(score - seg_max[seg])
        denom = jax.ops.segment_sum(ex, seg, num_segments=n * r)
        alpha = ex / denom[seg]
        dst_msg = node_emb[dst]
        aggr = jax.ops.segment_sum(alpha[:, None] * dst_msg, seg, num_segments=n * r).reshape(n, r, d)
        cnt = jax.ops.segment_sum(jnp.ones_like(score), seg, num_segments=n * r).reshape(n, r)
        w_r = coef_r @ basis_r
        wr_n, wr_m, wr_e = (w_r[:, :d], w_r[:, d:2 * d], w_r[:, 2 * d:])
        rel_score = node_emb @ wr_n.T + jnp.einsum('nrd,rd->nr', aggr, wr_m) + jnp.sum(edge_embeddings * wr_e, axis=-1) + b_r
        rel_score = jnp.where(cnt > 0, rel_score, -10000000000.0)
        attn = jax.nn.softmax(rel_score, axis=1)
        new_emb = jnp.einsum('nr,nrd->nd', attn, aggr)
        return node_emb + new_emb

    def _L3_gnn_ref(x, edge_index, edge_type, edge_weight, W1, root1, b1, W2, root2, b2):
        import jax, jax.numpy as jnp
        import numpy as np
        NUM_RELATIONS = 4
        N_NODES = 2500
        N_EDGES = 40000
        F_IN = 128
        HID = 128
        EMB = 128

        def _rgcn_conv(x, src, dst, edge_type, edge_weight, W, root, bias):
            xj = x[src]
            m = jnp.zeros((xj.shape[0], W.shape[2]), dtype=x.dtype)
            for r in range(W.shape[0]):
                mask = (edge_type == r).astype(x.dtype)[:, None]
                m = m + mask * (xj @ W[r])
            m = m * edge_weight[:, None]
            out = jax.ops.segment_sum(m, dst, num_segments=x.shape[0])
            return out + x @ root + bias
        src, dst = (edge_index[0], edge_index[1])
        ew = (edge_weight - edge_weight.min()) / (edge_weight.max() - edge_weight.min() + 1e-08)
        h = jax.nn.relu(_rgcn_conv(x, src, dst, edge_type, ew, W1, root1, b1))
        h = _rgcn_conv(h, src, dst, edge_type, ew, W2, root2, b2)
        return h
    edge_index = jnp.stack([src, dst])
    x = _layernorm(x + _L0_gnn_ref(x, edge_weight, L0_gnn_Wq1, L0_gnn_bq1, L0_gnn_Wk1, L0_gnn_bk1, L0_gnn_Wv1, L0_gnn_bv1, L0_gnn_We1, L0_gnn_Ws1, L0_gnn_bs1, L0_gnn_Wq2, L0_gnn_bq2, L0_gnn_Wk2, L0_gnn_bk2, L0_gnn_Wv2, L0_gnn_bv2, L0_gnn_We2, L0_gnn_Ws2, L0_gnn_bs2, edge_index), axis=-1)
    x = _layernorm(x + _L1_gnn_ref(x, edge_index, edge_attr_128, L1_gnn_W1, L1_gnn_b1, L1_gnn_W2, L1_gnn_b2, L1_gnn_ln_gamma, L1_gnn_ln_beta), axis=-1)
    x = _layernorm(x + _L2_gnn_ref(x, L2_gnn_edge_embeddings, L2_gnn_basis_s, L2_gnn_coef_s, L2_gnn_b_s, L2_gnn_basis_r, L2_gnn_coef_r, L2_gnn_b_r, src, dst, edge_type_16), axis=-1)
    x = _layernorm(x + _L3_gnn_ref(x, edge_index, edge_type_4, edge_weight, L3_gnn_W1, L3_gnn_root1, L3_gnn_b1, L3_gnn_W2, L3_gnn_root2, L3_gnn_b2), axis=-1)
    return x

_drawn_inputs = setup_inputs


def setup_inputs(seed=0):
    import zlib

    import numpy as np

    out = dict(_drawn_inputs(seed))
    spreads = {'L1_gnn_b1': (0.0, 0.449),
     'L1_gnn_b2': (0.0, 0.1),
     'L1_gnn_ln_gamma': (1.0, 0.2),
     'L1_gnn_ln_beta': (0.0, 0.1)}
    factors = {'L0_gnn_Wq1': 3.194,
     'L0_gnn_bq1': 8.0,
     'L0_gnn_Wk1': 3.35,
     'L0_gnn_bk1': 8.0,
     'L0_gnn_Wq2': 5.019,
     'L0_gnn_bq2': 8.0,
     'L0_gnn_Wk2': 7.392,
     'L0_gnn_bk2': 8.0,
     'L2_gnn_edge_embeddings': 8.0,
     'L2_gnn_basis_s': 8.0,
     'L2_gnn_coef_s': 8.0,
     'L2_gnn_b_s': 8.0,
     'L2_gnn_basis_r': 8.0,
     'L2_gnn_coef_r': 8.0,
     'L2_gnn_b_r': 8.0}
    for name, (base, spread) in spreads.items():
        noise = np.random.default_rng([zlib.crc32(name.encode()), seed]).standard_normal(out[name].shape)
        drawn = base * np.exp(spread * noise) if base else spread * noise
        out[name] = jnp.asarray(drawn.astype(out[name].dtype))
    for name, factor in factors.items():
        out[name] = (out[name] * factor).astype(out[name].dtype)
    return out
```

```python
from contextlib import ExitStack

import concourse.bass as bass
import numpy as np
from concourse import mybir

F32, BF16, I32 = mybir.dt.float32, mybir.dt.bfloat16, mybir.dt.int32
ALU, ACT, AX = mybir.AluOpType, mybir.ActivationFunctionType, mybir.AxisListType

P = 128
N, E, D = 6250, 100000, 128
H, C = 4, 32
R16, R4, RD, NBASIS = 16, 4, 32, 8
NW = -(-N // P)
NPAD = NW * P
NT = -(-E // P)
NTP = -(-NT // 2)
STEPS = NTP + NW - 1
SLOTS = 2 * STEPS
SB = -(-SLOTS // P)
SP = SB * P
CB = 20
CP = CB // 2
NCH = -(-SLOTS // CB)
NCH += NCH % 2
NPAIR = NCH // 2
assert NCH * CB <= SP and CB % 4 == 0
TC = -(-NTP // P)
G = 7
NG = NW // G
BIG = 1e30
NOWHERE = 1000000
KC = C + 1
KVW = D + H * KC
QW = H * KC
ACCW = D + 2 * H
EPS = 1e-5
INT_TABLES = ("dst", "before", "after", "src", "et16", "et4")


FROM_ONE = ("np_turned", "np_made", "np_xt", "np_added", "np_out", "sc_summed0", "sc_summed1", "sc_qe_used", "sc_out0",
            "sc_out1", "sc_st0", "sc_st1", "rs_st0", "rs_st1", "ag_read0", "ag_read1", "ag_added", "cs_pv_made0", "cs_pv_made1", "ml_turned", "ml_hidden",
            "ml_made", "ml_xt", "ml_silued", "ml_added", "rs_summed0", "rs_summed1", "rs_de_made")


class Signal:

    def __init__(self, sem, base):
        self.sem, self.base = sem, base

    def at(self, n):
        return self.base + n


def gnn_program(nc, a, out):
    ctx = ExitStack()
    signals = {}
    used = {}

    def signal(name):
        if name not in signals:
            signals[name] = Signal(ctx.enter_context(nc.semaphore(name)), 1 if name in FROM_ONE else 0)
        return signals[name]

    def stage_end(**counts):
        for name, n in counts.items():
            signals[name].base += n

    def dram(name, shape, dt):
        return nc.dram_tensor(name, shape, dt).ap()

    def chain(engine, sig, base=0):
        count = [0]

        def link(ins):
            count[0] += 1
            ins.then_inc(sig.sem, 1)
            engine.wait_ge(sig.sem, sig.at(base + count[0]))
        link.count = count
        return link

    kv_table = dram("kv_table", (NPAD, KVW), F32)
    v_steps = dram("v_steps", (P, NCH * CB * D), F32)
    skip_rows = dram("skip_rows", (P, NW * D), F32)
    agg_rows = dram("agg_rows", (P, NW * D), F32)
    dloc_slots = dram("dloc_slots", (1, SP * P), BF16)
    score_table = dram("score_table", (NPAD, R16), F32)
    rel_table = dram("rel_table", (NPAD, R4 * D), F32)

    with ctx:
        def sb(stack, name, shape, dt=F32):
            used[name] = used.get(name, 0) + 1
            return stack.enter_context(nc.sbuf_tensor(f"{name}_{used[name]}", shape, dt))

        def pb(stack, name, shape, dt=F32):
            used[name] = used.get(name, 0) + 1
            return stack.enter_context(nc.psum_tensor(f"{name}_{used[name]}", shape, dt))

        x = sb(ctx, "x", [P, NW * D])
        ident = sb(ctx, "ident", [P, P])
        iota_row = sb(ctx, "iota_row", [P, P])
        iota_col = sb(ctx, "iota_col", [P, 1])
        ones = sb(ctx, "ones", [P, P])
        window_of = sb(ctx, "window_of", [1, SP // 2], I32)
        pair_of = sb(ctx, "pair_of", [1, SP // 2], I32)
        dloc_e = sb(ctx, "dloc_e", [P, SP])
        ew_e = sb(ctx, "ew_e", [P, SP])
        et16_e = sb(ctx, "et16_e", [P, SP])
        src_i = sb(ctx, "src_i", [P, SP], I32)
        src16_i = sb(ctx, "src16_i", [P, SP], I32)
        src4_i = sb(ctx, "src4_i", [P, SP], I32)
        ewn_e = sb(ctx, "ewn_e", [P, SP])
        reset_t = sb(ctx, "reset_t", [P, SP])
        close_t = sb(ctx, "close_t", [P, SP])
        cumreset_t = sb(ctx, "cumreset_t", [P, SP])
        cumclose_t = sb(ctx, "cumclose_t", [P, SP])
        amask_t = sb(ctx, "amask_t", [P, SP])
        et16_t = sb(ctx, "et16_t", [P, SP])

        def tables():
            done = ExitStack()
            with done:
                ones_b = sb(done, "ones_b", [P, P], BF16)
                steps_row = sb(done, "steps_row", [P, SP])
                pair_no = sb(done, "pair_no", [P, TC])
                odd_t = sb(done, "odd_t", [P, SB])
                step_t = sb(done, "step_t", [P, SB])
                last_i = sb(done, "last_i", [P, TC], I32)
                lastw_i = sb(done, "lastw_i", [P, TC], I32)
                last = sb(done, "last", [P, TC])
                cmp = sb(done, "cmp", [P, TC * SP], BF16)
                pair_t = sb(done, "pair_t", [P, SB])
                tile_t = sb(done, "tile_t", [P, SB])
                tile_t_i = sb(done, "tile_t_i", [P, SB], I32)
                negw_t = sb(done, "negw_t", [P, SB])
                tile_row = sb(done, "tile_row", [1, SP])
                win_row = sb(done, "win_row", [1, SP])
                packed = sb(done, "packed", [P, SB * 6 * P], I32)
                ew_t = sb(done, "ew_t", [P, SP])
                dl = sb(done, "dl", [P, SP])
                act = sb(done, "act", [P, SP])
                tmp = sb(done, "tmp", [P, SP])
                src_t = sb(done, "src_t", [P, SP])
                dl_b = sb(done, "dl_b", [P, SP], BF16)
                src16_t = sb(done, "src16_t", [P, SP])
                src4_t = sb(done, "src4_t", [P, SP])
                ext = sb(done, "ext", [P, 2])
                ext2 = sb(done, "ext2", [2, 1])
                ext_d = sb(done, "ext_d", [2, 2])
                ext_b = sb(done, "ext_b", [P, 4])
                ps_row = pb(done, "ps_row", [P, 1024])
                ps_t = pb(done, "ps_t", [P, 512])
                ps_e = pb(done, "ps_e", [P, 2 * 1024])
                loaded, gathered, chained, counted, turned, copied, stored, ext_s = (
                    signal(n) for n in ("tb_loaded", "tb_gathered", "tb_chain", "tb_counted",
                                        "tb_turned", "tb_copied", "tb_stored", "tb_ext"))
                idx_ready = signal("tb_idx_ready")
                cmp_v = cmp[:, :].rearrange("p (c s) -> p c s", c=TC)
                pk = packed[:, :].rearrange("p (b f e) -> p b f e", b=SB, f=6)
                blocked = lambda t: t[:, :].rearrange("p (b e) -> p b e", b=SB)
                to_turn = [(dl, dloc_e), (ew_t, ew_e), (et16_t, et16_e), (src_t, src_i),
                           (src16_t, src16_i), (src4_t, src4_i)]
                half = SP // 2
                with nc.Block() as block:
                    @block.sync
                    def _(sp):
                        for name in FROM_ONE:
                            sp.sem_inc(signal(name).sem, 1)
                        loads = [(x[:, :], a["x"]), (ident[:, :], a["c_ident"]), (iota_row[:, :], a["c_iota_row"]),
                                 (iota_col[:, :], a["c_iota_col"]), (steps_row[:, :], a["c_steps_row"]),
                                 (pair_no[:, :], a["c_pair_no"]), (step_t[:, :], a["c_step_t"]),
                                 (odd_t[:, :], a["c_odd_t"]),
                                 (last_i[:, :], a["pair_last"])]
                        for to, of in loads:
                            sp.dma_start(to, of).then_inc(loaded.sem, 16)
                        sp.wait_ge(chained.sem, 100)
                        sp.dma_start(dloc_slots.rearrange("o (p e) -> (o p) e", p=P), dl_b[:, :]).then_inc(stored.sem, 16)
                        sp.wait_ge(stored.sem, 16)

                    @block.vector
                    def _(dve):
                        link = chain(dve, chained)
                        link(dve.memset(ones[:, :], 1.0))
                        link(dve.memset(ones_b[:, :], 1.0))
                        dve.wait_ge(loaded.sem, 16 * 9)
                        link(dve.tensor_scalar(lastw_i[:, :], last_i[:, :], 7, None, ALU.arith_shift_right))
                        link(dve.tensor_copy(last[:, :], lastw_i[:, :]))
                        link(dve.scalar_tensor_tensor(last[:, :], last[:, :], float(NW - 1), pair_no[:, :], ALU.min, ALU.add))
                        for c in range(TC):
                            dve.tensor_scalar(cmp_v[:, c, :], steps_row[:, :], last[:, c:c + 1], None,
                                              ALU.is_gt).then_inc(counted.sem, 1)
                        dve.wait_ge(turned.sem, 1)
                        link(dve.tensor_copy(pair_t[:, :], ps_t[:, 0:SB]))
                        link(dve.scalar_tensor_tensor(tile_t[:, :], pair_t[:, :], 2.0, odd_t[:, :], ALU.mult, ALU.add))
                        dve.tensor_copy(tile_t_i[:, :], tile_t[:, :]).then_inc(idx_ready.sem, 1)
                        link(dve.tensor_tensor(negw_t[:, :], step_t[:, :], pair_t[:, :], ALU.subtract))
                        link(dve.tensor_scalar(negw_t[:, :], negw_t[:, :], float(NW - 1), -float(P), ALU.min, ALU.mult))
                        for h in range(2):
                            dve.tensor_copy(tile_row[:, h * half:(h + 1) * half], ps_row[0:1, h * 512:h * 512 + half])\
                               .then_inc(chained.sem, 1)
                            link.count[0] += 1
                        dve.wait_ge(chained.sem, link.count[0])
                        link(dve.tensor_copy(pair_of[:, :], tile_row[:, 0::2]))
                        link(dve.tensor_tensor(win_row[:, :], steps_row[0:1, :], tile_row[:, :], ALU.subtract))
                        link(dve.tensor_scalar(win_row[:, :], win_row[:, :], float(NW - 1), None, ALU.min))
                        link(dve.tensor_copy(window_of[:, :], win_row[:, 0::2]))
                        dve.wait_ge(gathered.sem, 16 * 2 * SB)
                        for b in range(SB):
                            link(dve.tensor_scalar(blocked(dl)[:, b, :], pk[:, b, 0, :], negw_t[:, b:b + 1], None, ALU.add))
                        link(dve.tensor_scalar(tmp[:, :], dl[:, :], 0.0, None, ALU.is_ge))
                        link(dve.scalar_tensor_tensor(act[:, :], dl[:, :], P - 0.5, tmp[:, :], ALU.is_le, ALU.mult))
                        link(dve.tensor_scalar(amask_t[:, :], act[:, :], -1.0, BIG, ALU.add, ALU.mult))
                        for other, flag in ((1, reset_t), (2, close_t)):
                            link(dve.tensor_tensor(blocked(tmp), pk[:, :, 0, :], pk[:, :, other, :], ALU.not_equal))
                            link(dve.scalar_tensor_tensor(flag[:, :], tmp[:, :], -BIG, act[:, :], ALU.mult, ALU.mult))
                        link(dve.memset(tmp[:, :], 0.0))
                        link(dve.tensor_tensor_scan(cumreset_t[:, :], tmp[:, :], reset_t[:, :], 0.0, ALU.add, ALU.add))
                        link(dve.tensor_tensor_scan(cumclose_t[:, ::-1], tmp[:, :], close_t[:, ::-1], 0.0, ALU.add, ALU.add))
                        link(dve.scalar_tensor_tensor(dl[:, :], dl[:, :], 1.0, act[:, :], ALU.add, ALU.mult))
                        link(dve.tensor_scalar(dl[:, :], dl[:, :], -1.0, None, ALU.add))
                        link(dve.tensor_copy(dl_b[:, :], dl[:, :]))
                        link(dve.tensor_copy(blocked(src_t), pk[:, :, 3, :]))
                        link(dve.tensor_copy(blocked(et16_t), pk[:, :, 4, :]))
                        link(dve.scalar_tensor_tensor(blocked(src16_t), blocked(src_t), float(R16), pk[:, :, 4, :], ALU.mult, ALU.add))
                        link(dve.scalar_tensor_tensor(blocked(src4_t), blocked(src_t), float(R4), pk[:, :, 5, :], ALU.mult, ALU.add))
                        link(dve.tensor_reduce(ext[:, 0:1], ew_t[:, :], AX.X, ALU.max))
                        link(dve.tensor_reduce(ext[:, 1:2], ew_t[:, :], AX.X, ALU.min))
                        link(dve.tensor_scalar(ext[:, 1:2], ext[:, 1:2], -1.0, None, ALU.mult))
                        dve.sem_inc(chained.sem, 100 - link.count[0])
                        link.count[0] = 100
                        dve.wait_ge(ext_s.sem, 1)
                        link(dve.tensor_reduce(ext2[:, :], ps_t[0:2, 128:256], AX.X, ALU.max))
                        dve.tensor_scalar(ext_d[:, :], ident[0:2, 0:2], ext2[:, :], None, ALU.mult).then_inc(counted.sem, 1)
                        dve.wait_ge(ext_s.sem, 2)
                        link(dve.tensor_copy(ext_b[:, 0:2], ps_t[:, 256:258]))
                        link(dve.tensor_tensor(ext_b[:, 2:3], ext_b[:, 0:1], ext_b[:, 1:2], ALU.add))
                        link(dve.tensor_scalar(ext_b[:, 2:3], ext_b[:, 2:3], 1e-8, None, ALU.add))
                        link(dve.reciprocal(ext_b[:, 3:4], ext_b[:, 2:3]))
                        dve.wait_ge(copied.sem, 2)
                        link(dve.tensor_scalar(ewn_e[:, :], ew_e[:, :], ext_b[:, 1:2], ext_b[:, 3:4], ALU.add, ALU.mult))

                    @block.tensor
                    def _(pe):
                        pe.wait_ge(counted.sem, TC)
                        for h in range(2):
                            for c in range(TC):
                                pe.matmul(ps_row[:, h * 512:h * 512 + half], ones_b[:, :],
                                          cmp_v[:, c, h * half:(h + 1) * half], start=(c == 0), stop=(c == TC - 1))
                        for b in range(SB):
                            for c in range(TC):
                                last_mm = pe.matmul(ps_t[:, b:b + 1], cmp_v[:, c, b::SB], ones_b[:, 0:1],
                                                    start=(c == 0), stop=(c == TC - 1))
                        last_mm.then_inc(turned.sem, 1)
                        pe.wait_ge(chained.sem, 100)
                        pe.transpose(ps_t[0:2, 128:256], ext[:, :], ident[:, :]).then_inc(ext_s.sem, 1)
                        pe.wait_ge(counted.sem, TC + 1)
                        pe.matmul(ps_t[:, 256:258], ones[0:2, :], ext_d[:, :], start=True, stop=True).then_inc(ext_s.sem, 1)
                        for n, (of, _) in enumerate(to_turn):
                            if n >= 2:
                                pe.wait_ge(copied.sem, n - 1)
                            for b in range(SB):
                                at = n % 2 * 1024 + b * P
                                last_mm = pe.transpose(ps_e[:, at:at + P], blocked(of)[:, b, :], ident[:, :])
                            last_mm.then_inc(turned.sem, 1)

                    @block.scalar
                    def _(act_e):
                        for n, (_, to) in enumerate(to_turn):
                            act_e.wait_ge(turned.sem, n + 2)
                            at = n % 2 * 1024
                            act_e.copy(to[:, :].rearrange("e (p b) -> e b p", b=SB),
                                       ps_e[:, at:at + SP].rearrange("e (b p) -> e b p", b=SB)).then_inc(copied.sem, 1)

                    @block.gpsimd
                    def _(pool):
                        pool.wait_ge(idx_ready.sem, 1)
                        for b in range(SB):
                            at = bass.IndirectOffsetOnAxis(ap=tile_t_i[:, b:b + 1], axis=0)
                            pool.indirect_dma_start(pk[:, b, :, :].rearrange("p f e -> p (f e)"), None,
                                                    a["int_rows"], at).then_inc(gathered.sem, 16)
                            pool.indirect_dma_start(blocked(ew_t)[:, b, :], None, a["ew_rows"], at)\
                                .then_inc(gathered.sem, 16)

        def project(src, w_all, cols, load, n_loads, stores, window, group, n_links, first=None):
            done = ExitStack()
            with done:
                slots = 4 if cols <= 512 else 2
                wide = 2048 // slots
                xg = sb(done, "xg", [P, G * D])
                xt = sb(done, "xt", [P, G * D])
                ps_x = pb(done, "ps_x", [P, 1024])
                ps_y = pb(done, "ps_y", [P, 2048])
                loaded, got, turned, xt_ready, made, added, rows, stored, chained = (
                    signal(n) for n in ("np_loaded", "np_got", "np_turned", "np_xt", "np_made",
                                        "np_added", "np_rows", "np_stored", "np_chain"))
                rows_out = signal("np_out")
                n_stores = len(stores(0))
                pre = [0]
                with nc.Block() as block:
                    @block.sync
                    def _(sp):
                        load(sp, loaded)
                        with sp.Fori(0, NG) as g:
                            sp.wait_ge(rows.sem, rows.at(g + 1))
                            for to, of in stores(g):
                                sp.dma_start(to, of).then_inc(stored.sem, 16)
                            sp.wait_ge(stored.sem, stored.at((g + 1) * (16 * n_stores)))
                            sp.sem_inc(rows_out.sem, 1)

                    @block.scalar
                    def _(act_e):
                        with act_e.Fori(0, NG) as g:
                            act_e.wait_ge(turned.sem, turned.at(g))
                            act_e.copy(xg[:, :], src[:, bass.ds(g * (G * D), G * D)]).then_inc(got.sem, 1)
                            act_e.wait_ge(turned.sem, turned.at(g + 1))
                            act_e.wait_ge(made.sem, made.at(g * G))
                            act_e.copy(xt[:, :], ps_x[:, 0:G * D]).then_inc(xt_ready.sem, 1)

                    @block.tensor
                    def _(pe):
                        pe.wait_ge(loaded.sem, loaded.at(16 * n_loads))
                        with pe.Fori(0, NG) as g:
                            pe.wait_ge(got.sem, got.at(g + 1))
                            pe.wait_ge(xt_ready.sem, xt_ready.at(g))
                            for j in range(G):
                                last_mm = pe.transpose(ps_x[:, j * D:(j + 1) * D], xg[:, j * D:(j + 1) * D], ident[:, :])
                            last_mm.then_inc(turned.sem, 1)
                            pe.wait_ge(xt_ready.sem, xt_ready.at(g + 1))
                            for j in range(G):
                                pe.wait_ge(added.sem, added.at(g * G + max(j - slots + 1, 0)))
                                for c in range(0, cols, 512):
                                    n = min(512, cols - c)
                                    at = j % slots * wide + c
                                    last_mm = pe.matmul(ps_y[:, at:at + n], xt[:, j * D:(j + 1) * D], w_all[:, c:c + n],
                                                        start=True, stop=True)
                                last_mm.then_inc(made.sem, 1)

                    @block.vector
                    def _(dve):
                        dve.wait_ge(loaded.sem, loaded.at(16 * n_loads))
                        if first:
                            link = chain(dve, chained)
                            first(dve, link)
                            pre[0] = link.count[0]
                        with dve.Fori(0, NG) as g:
                            dve.wait_ge(rows_out.sem, rows_out.at(g))
                            for j in range(G):
                                dve.wait_ge(made.sem, made.at(g * G + j + 1))
                                at = j % slots * wide
                                window(dve, ps_y[:, at:at + cols], j).then_inc(added.sem, 1)
                            dve.wait_ge(added.sem, added.at((g + 1) * G))
                            link = chain(dve, chained, g * n_links + pre[0])
                            group(dve, g, link)
                            assert link.count[0] == n_links
                            dve.sem_inc(rows.sem, 1)
                stage_end(np_loaded=16 * n_loads, np_got=NG, np_turned=NG, np_xt=NG, np_made=NW, np_added=NW,
                          np_rows=NG, np_out=NG, np_stored=16 * n_stores * NG, np_chain=pre[0] + n_links * NG)

        def split3(dve, link, value, part, rest, to):
            link(dve.tensor_copy(part[:, :], value[:, :]))
            link(dve.tensor_copy(to(0), grouped(part)))
            link(dve.tensor_tensor(rest[:, :], value[:, :], part[:, :], ALU.subtract))
            link(dve.tensor_copy(part[:, :], rest[:, :]))
            link(dve.tensor_copy(to(1), grouped(part)))
            link(dve.tensor_tensor(rest[:, :], rest[:, :], part[:, :], ALU.subtract))
            link(dve.tensor_copy(to(2), grouped(rest)))

        def grouped(t):
            return t[:, :].rearrange("p (g c) -> p g c", g=G)

        def in_heads(ap):
            return ap.rearrange("p (h c) -> p h c", h=H)

        def conv_project(src, layer, qsplit):
            done = ExitStack()
            with done:
                w_all = sb(done, "w_all", [P, 4 * D])
                b_all = sb(done, "b_all", [P, 4 * D])
                we_b = sb(done, "we_b", [P, D])
                kv_out = sb(done, "kv_out", [P, G * KVW])
                sq_out = sb(done, "sq_out", [P, G * 2 * D])
                qx = sb(done, "qx", [P, G * QW])
                rest = sb(done, "rest", [P, G * QW])
                part = sb(done, "part", [P, G * QW], BF16)
                tmp = sb(done, "tmp", [P, G * D])
                kv3, sq3 = grouped(kv_out), grouped(sq_out)
                qx4 = qx[:, :].rearrange("p (g h c) -> p g h c", g=G, h=H)
                tmp4 = tmp[:, :].rearrange("p (g h c) -> p g h c", g=G, h=H)
                q3 = qsplit[:, :].rearrange("p (w k c) -> p w k c", k=3, c=QW)

                def load(sp, sig):
                    for n, k in enumerate(("v", "s", "q", "k")):
                        sp.dma_start(w_all[:, n * D:(n + 1) * D], a[f"L0_gnn_W{k}{layer}"]).then_inc(sig.sem, 16)
                        sp.dma_start(b_all[:, n * D:(n + 1) * D],
                                     a[f"L0_gnn_b{k}{layer}"].partition_broadcast(P)).then_inc(sig.sem, 16)
                    sp.dma_start(we_b[:, :], a[f"L0_gnn_We{layer}"][0, :].partition_broadcast(P)).then_inc(sig.sem, 16)

                def first(dve, link):
                    link(dve.memset(kv_out[:, :], 0.0))

                def window(dve, y, j):
                    dve.tensor_tensor(kv3[:, j, 0:D], y[:, 0:D], b_all[:, 0:D], ALU.add)
                    dve.tensor_tensor(sq3[:, j, :], y[:, D:3 * D], b_all[:, D:3 * D], ALU.add)
                    return dve.tensor_tensor(in_heads(kv3[:, j, D:KVW])[:, :, 0:C], in_heads(y[:, 3 * D:4 * D]),
                                             in_heads(b_all[:, 3 * D:4 * D]), ALU.add)

                def group(dve, g, link):
                    for h in range(H):
                        link(dve.tensor_scalar(qx4[:, :, h, 0:C], sq3[:, :, D + h * C:D + (h + 1) * C],
                                               float(C) ** -0.5, None, ALU.mult))
                        link(dve.tensor_tensor(tmp4[:, :, h, :], qx4[:, :, h, 0:C],
                                               we_b[:, h * C:(h + 1) * C].unsqueeze(1).to_broadcast([P, G, C]), ALU.mult))
                        link(dve.tensor_reduce(qx4[:, :, h, C], tmp4[:, :, h, :], AX.X, ALU.add))
                    split3(dve, link, qx, part, rest, lambda k: q3[:, bass.ds(g * G, G), k, :])

                def stores(g):
                    return [(kv_table.rearrange("(w p) c -> p w c", p=P)[:, bass.ds(g * G, G), :], kv3),
                            (skip_rows.rearrange("p (w c) -> p w c", c=D)[:, bass.ds(g * G, G), :], sq3[:, :, 0:D])]
                project(src, w_all, 4 * D, load, 9, stores, window, group, 3 * H + 7, first)

        def conv_scores(qsplit, alpha):
            done = ExitStack()
            with done:
                kv = sb(done, "kv", [P, 2 * CB * KVW])
                idx = sb(done, "idx", [P, 2 * CB], I32)
                dl_row = sb(done, "dl_row", [P, 2 * CB * P], BF16)
                st = sb(done, "st", [P, 2 * CB * P], BF16)
                prod = sb(done, "prod", [P, CB * QW])
                ps_q = pb(done, "ps_q", [P, 2 * 1024])
                idx_ready, ew_in, qe_made, qe_used = (
                    signal(n) for n in ("sc_idx", "sc_ew_in", "sc_qe_made", "sc_qe_used"))
                st_made = (signal("sc_st0"), signal("sc_st1"))
                issuing = signal("issuing")
                values_out = (signal("sc_out0"), signal("sc_out1"))
                gathered, dl_in, spilled, summed = (
                    (signal(n + "0"), signal(n + "1")) for n in ("sc_gathered", "sc_dl_in", "sc_spilled", "sc_summed"))
                kv4 = kv[:, :].rearrange("p (k s c) -> p k s c", k=2, s=CB)
                st4 = st[:, :].rearrange("p (k s e) -> p k s e", k=2, s=CB)
                dl3 = dl_row[:, :].rearrange("p (k n) -> p k n", k=2)
                prod3 = prod[:, :].rearrange("p (s c) -> p s c", s=CB)
                ps4 = ps_q[:, :].rearrange("p (b s c) -> p b s c", b=2, s=4)
                al3 = alpha[:, :].rearrange("p (s h) -> p s h", h=H)
                q_of = lambda w, part: qsplit[:, bass.ds(w * (3 * QW) + part * QW, QW)]
                GQ = CB // 4
                with nc.Block() as block:
                    @block.gpsimd
                    def _(pool):
                        with pool.Fori(0, NPAIR) as i:
                            for k in range(2):
                                pool.wait_ge(summed[k].sem, summed[k].at(i))
                                pool.wait_ge(values_out[k].sem, values_out[k].at(i))
                                pool.tensor_copy(idx[:, k * CB:(k + 1) * CB], src_i[:, bass.ds((i * 2 + k) * CB, CB)])\
                                    .then_inc(idx_ready.sem, 1)
                                pool.wait_ge(idx_ready.sem, idx_ready.at(i * 2 + k + 1))
                                pool.sem_inc(issuing.sem, 1)
                                for s in range(CB):
                                    pool.indirect_dma_start(
                                        kv4[:, k, s, :], None, kv_table,
                                        bass.IndirectOffsetOnAxis(ap=idx[:, k * CB + s:k * CB + s + 1], axis=0))\
                                        .then_inc(gathered[k].sem, 16)

                    @block.sync
                    def _(sp):
                        with sp.Fori(0, NPAIR) as i:
                            for k in range(2):
                                sp.wait_ge(gathered[k].sem, gathered[k].at((i + 1) * (16 * CB)))
                                sp.dma_start(v_steps.rearrange("p (s c) -> p s c", c=D)[:, bass.ds((i * 2 + k) * CB, CB), :],
                                             kv4[:, k, :, 0:D]).then_inc(spilled[k].sem, 16)
                                sp.wait_ge(spilled[k].sem, spilled[k].at((i + 1) * 16))
                                sp.sem_inc(values_out[k].sem, 1)

                    @block.scalar
                    def _(act_e):
                        with act_e.Fori(0, NPAIR) as i:
                            for k in range(2):
                                act_e.wait_ge(st_made[k].sem, st_made[k].at(i))
                                act_e.dma_start(dl3[:, k, :], dloc_slots[0, bass.ds((i * 2 + k) * (CB * P), CB * P)]
                                                .partition_broadcast(P)).then_inc(dl_in[k].sem, 16)
                            for k in range(2):
                                act_e.wait_ge(gathered[k].sem, gathered[k].at((i + 1) * (16 * CB)))
                                act_e.copy(kv4[:, k, :, D:KVW].rearrange("p s (h c) -> p s h c", h=H)[:, :, :, C],
                                           ew_e[:, bass.ds((i * 2 + k) * CB, CB)].unsqueeze(2).to_broadcast([P, CB, H]))\
                                    .then_inc(ew_in.sem, 1)

                    @block.tensor
                    def _(pe):
                        with pe.Fori(0, NPAIR) as i:
                            for k in range(2):
                                pe.wait_ge(st_made[k].sem, st_made[k].at(i + 1))
                                _, ws = nc.values_load_multi_w_load_instructions(
                                    window_of[0:1, bass.ds((i * 2 + k) * CP, CP)],
                                    engines=(mybir.EngineType.PE,), min_val=0, max_val=NW - 1)
                                for q in range(GQ):
                                    n = 2 * GQ * i + k * GQ + q
                                    if k * GQ + q >= 2:
                                        pe.wait_ge(qe_used.sem, qe_used.at(n - 1))
                                    else:
                                        pe.wait_ge(qe_used.sem, qe_used.at(2 * GQ * i))
                                    for s in range(4):
                                        for part in range(3):
                                            last_mm = pe.matmul(ps4[:, (k * GQ + q) % 2, s, 0:QW], st4[:, k, q * 4 + s, :],
                                                                q_of(ws[(q * 4 + s) // 2], part), start=(part == 0), stop=(part == 2))
                                    last_mm.then_inc(qe_made.sem, 1)

                    @block.vector
                    def _(dve):
                        dve.memset(alpha[:, NCH * CB * H:], 0.0)
                        with dve.Fori(0, NPAIR) as i:
                            for k in range(2):
                                dve.wait_ge(dl_in[k].sem, dl_in[k].at((i + 1) * 16))
                                dve.wait_ge(qe_used.sem, qe_used.at(2 * GQ * i))
                                dve.tensor_scalar(st4[:, k].rearrange("p s e -> p (s e)"), dl3[:, k, :], iota_col[:, :],
                                                  None, ALU.is_equal).then_inc(st_made[k].sem, 1)
                                dve.wait_ge(ew_in.sem, ew_in.at(i * 2 + k + 1))
                                dve.wait_ge(summed[1 - k].sem, summed[1 - k].at(i + k))
                                for q in range(GQ):
                                    dve.wait_ge(qe_made.sem, qe_made.at(2 * GQ * i + k * GQ + q + 1))
                                    dve.tensor_tensor(prod3[:, q * 4:q * 4 + 4, :], ps4[:, (k * GQ + q) % 2, :, 0:QW],
                                                      kv4[:, k, q * 4:q * 4 + 4, D:KVW], ALU.mult).then_inc(qe_used.sem, 1)
                                dve.wait_ge(qe_used.sem, qe_used.at(2 * GQ * i + (k + 1) * GQ))
                                dve.tensor_reduce(al3[:, bass.ds((i * 2 + k) * CB, CB), :],
                                                  prod3.rearrange("p s (h c) -> p s h c", h=H),
                                                  AX.X, ALU.add).then_inc(summed[k].sem, 1)
                stage_end(sc_idx=NCH, sc_gathered0=16 * CB * NPAIR, sc_gathered1=16 * CB * NPAIR, sc_ew_in=NCH,
                          sc_dl_in0=16 * NPAIR, sc_dl_in1=16 * NPAIR, sc_st0=NPAIR, sc_st1=NPAIR, sc_qe_made=NCH * GQ,
                          sc_qe_used=NCH * GQ, sc_summed0=NPAIR, sc_summed1=NPAIR, sc_out0=NPAIR, sc_out1=NPAIR, sc_spilled0=16 * NPAIR, sc_spilled1=16 * NPAIR)

        def edge_softmax(score, lanes):
            done = ExitStack()
            by_relation = lanes == R16
            heads = 1 if by_relation else H
            with done:
                a_t = sb(done, "a_t", [P, heads * SP])
                f_t = sb(done, "f_t", [P, lanes * SP])
                lane_t = sb(done, "lane_t", [P, SP])
                eq_t = sb(done, "eq_t", [P, SP])
                back_t = sb(done, "back_t", [P, SP])
                m_t = sb(done, "m_t", [P, SP])
                ends = sb(done, "ends", [P, lanes])
                totals = sb(done, "totals", [P, lanes])
                ends_r = sb(done, "ends_r", [lanes, P])
                tot_r = sb(done, "tot_r", [lanes, P])
                carry_r = sb(done, "carry_r", [lanes, P + 1])
                carry = sb(done, "carry", [P, lanes])
                ps_a = pb(done, "ps_a", [P, 2 * 1024])
                ps_c = pb(done, "ps_c", [P, 512])
                turned_in, taken, chained, turned, out_turned, out_copied, weighed = (
                    signal(n) for n in ("sm_turned_in", "sm_taken", "sm_chain", "sm_turned", "sm_out_turned",
                                        "sm_out_copied", "sm_weighed"))
                ready = signal("sm_ready")
                s3 = score[:, :].rearrange("e (s h) -> e s h", h=heads)
                a3 = a_t[:, :].rearrange("p (h s) -> p h s", h=heads)
                lane_of = lambda t, r: t[:, bass.ds(r * SP, SP)]
                with nc.Block() as block:
                    @block.tensor
                    def _(pe):
                        for h in range(heads):
                            if h >= 2:
                                pe.wait_ge(taken.sem, taken.at(h - 1))
                            for b in range(SB):
                                at = h % 2 * 1024 + b * P
                                last_mm = pe.transpose(ps_a[:, at:at + P], s3[:, b::SB, h], ident[:, :])
                            last_mm.then_inc(turned_in.sem, 1)
                        for back in range(2):
                            pe.wait_ge(ready.sem, ready.at(2 * back + 1))
                            pe.transpose(ps_c[0:lanes, 0:P], ends[:, :], ident[:, :])
                            pe.transpose(ps_c[0:lanes, P:2 * P], totals[:, :], ident[:, :]).then_inc(turned.sem, 1)
                            pe.wait_ge(ready.sem, ready.at(2 * back + 2))
                            lo = 1 if back else 0
                            pe.transpose(ps_c[:, 2 * P:2 * P + lanes], carry_r[:, lo:lo + P], ident[0:lanes, 0:lanes])\
                              .then_inc(turned.sem, 1)
                        for h in range(heads):
                            pe.wait_ge(weighed.sem, weighed.at(h + 1))
                            if h >= 2:
                                pe.wait_ge(out_copied.sem, out_copied.at(h - 1))
                            for b in range(SB):
                                at = h % 2 * 1024 + b * P
                                last_mm = pe.transpose(ps_a[:, at:at + P], a3[:, h, b * P:(b + 1) * P], ident[:, :])
                            last_mm.then_inc(out_turned.sem, 1)

                    @block.vector
                    def _(dve):
                        count = [0]

                        def link(ins):
                            count[0] += 1
                            ins.then_inc(chained.sem, 1)
                            dve.wait_ge(chained.sem, chained.at(count[0]))

                        def lane_loop(per_lane, body):
                            start = count[0]
                            with dve.Fori(0, lanes) as r:
                                n = [0]

                                def step(ins):
                                    n[0] += 1
                                    ins.then_inc(chained.sem, 1)
                                    dve.wait_ge(chained.sem, chained.at(r * per_lane + (start + n[0])))
                                body(r, step)
                                assert n[0] == per_lane
                            count[0] = start + per_lane * lanes

                        for h in range(heads):
                            dve.wait_ge(turned_in.sem, turned_in.at(h + 1))
                            dve.tensor_tensor(a3[:, h, :], ps_a[:, h % 2 * 1024:h % 2 * 1024 + SP], amask_t[:, :], ALU.add)\
                               .then_inc(taken.sem, 1)
                        dve.wait_ge(taken.sem, taken.at(heads))

                        def lane_scores(r, step):
                            if not by_relation:
                                return lane_of(a_t, r)
                            step(dve.tensor_scalar(eq_t[:, :], et16_t[:, :], iota_row[:, bass.ds(r, 1)], -BIG,
                                                   ALU.not_equal, ALU.mult))
                            step(dve.tensor_tensor(lane_t[:, :], eq_t[:, :], a_t[:, :], ALU.add))
                            return lane_t[:, :]

                        def forward(r, step):
                            step(dve.tensor_tensor_scan(lane_of(f_t, r), reset_t[:, :], lane_scores(r, step), -BIG,
                                                        ALU.add, ALU.max))
                        lane_loop(3 if by_relation else 1, forward)

                        def carries(back, cum):
                            f3 = f_t[:, :].rearrange("p (l s) -> p l s", l=lanes)
                            edge = 0 if back else SP - 1
                            link(dve.tensor_copy(ends[:, :], f3[:, :, edge]))
                            link(dve.tensor_copy(totals[:, :], cum[:, edge:edge + 1].to_broadcast([P, lanes])))
                            dve.sem_inc(ready.sem, 1)
                            dve.wait_ge(turned.sem, turned.at(2 * back + 1))
                            link(dve.tensor_copy(ends_r[:, :], ps_c[0:lanes, 0:P]))
                            link(dve.tensor_copy(tot_r[:, :], ps_c[0:lanes, P:2 * P]))
                            link(dve.memset(carry_r[:, :], -BIG))
                            if back:
                                link(dve.tensor_tensor_scan(carry_r[:, 0:P][:, ::-1], tot_r[:, ::-1], ends_r[:, ::-1], -BIG,
                                                            ALU.add, ALU.max))
                            else:
                                link(dve.tensor_tensor_scan(carry_r[:, 1:P + 1], tot_r[:, :], ends_r[:, :], -BIG,
                                                            ALU.add, ALU.max))
                            dve.sem_inc(ready.sem, 1)
                            dve.wait_ge(turned.sem, turned.at(2 * back + 2))
                            link(dve.tensor_copy(carry[:, :], ps_c[:, 2 * P:2 * P + lanes]))

                        carries(0, cumreset_t)

                        def backward(r, step):
                            f = lane_of(f_t, r)
                            step(dve.scalar_tensor_tensor(lane_t[:, :], cumreset_t[:, :], carry[:, bass.ds(r, 1)], f,
                                                          ALU.add, ALU.max))
                            step(dve.tensor_tensor_scan(back_t[:, ::-1], close_t[:, ::-1], lane_t[:, ::-1], -BIG,
                                                        ALU.add, ALU.max))
                            step(dve.tensor_scalar(f, back_t[:, :], 0.0, None, ALU.add))
                        lane_loop(3, backward)
                        carries(1, cumclose_t)
                        if by_relation:
                            link(dve.memset(m_t[:, :], 0.0))

                            def pick(r, step):
                                f = lane_of(f_t, r)
                                step(dve.scalar_tensor_tensor(f, cumclose_t[:, :], carry[:, bass.ds(r, 1)], f, ALU.add, ALU.max))
                                step(dve.scalar_tensor_tensor(lane_t[:, :], et16_t[:, :], iota_row[:, bass.ds(r, 1)], f,
                                                              ALU.is_equal, ALU.mult))
                                step(dve.tensor_tensor(m_t[:, :], m_t[:, :], lane_t[:, :], ALU.add))
                            lane_loop(3, pick)
                            link(dve.tensor_tensor(a_t[:, :], a_t[:, :], m_t[:, :], ALU.subtract))
                        else:
                            def subtract(r, step):
                                f = lane_of(f_t, r)
                                step(dve.scalar_tensor_tensor(f, cumclose_t[:, :], carry[:, bass.ds(r, 1)], f, ALU.add, ALU.max))
                                step(dve.tensor_tensor(lane_of(a_t, r), lane_of(a_t, r), f, ALU.subtract))
                            lane_loop(2, subtract)
                        link(dve.tensor_scalar(a_t[:, :], a_t[:, :], 0.0, None, ALU.min))
                        dve.sem_inc(ready.sem, 1)
                        edge_softmax.linked = count[0]

                    @block.scalar
                    def _(act_e):
                        act_e.wait_ge(ready.sem, ready.at(5))
                        for h in range(heads):
                            act_e.activation(a3[:, h, :], a3[:, h, :], ACT.Exp).then_inc(weighed.sem, 1)
                        for h in range(heads):
                            act_e.wait_ge(out_turned.sem, out_turned.at(h + 1))
                            act_e.copy(s3.rearrange("e (p b) h -> e b p h", b=SB)[:, :, :, h],
                                       ps_a[:, h % 2 * 1024:h % 2 * 1024 + SP].rearrange("e (b p) -> e b p", b=SB))\
                                 .then_inc(out_copied.sem, 1)
                stage_end(sm_turned_in=heads, sm_taken=heads, sm_chain=edge_softmax.linked, sm_turned=4,
                          sm_out_turned=heads, sm_out_copied=heads, sm_weighed=heads, sm_ready=5)

        def aggregate(acc, width, rhs, fill, scale=None, extra=None, extra_width=0, clear=True):
            done = ExitStack()
            with done:
                RING, AHEAD = 4, 3
                onehot = sb(done, "onehot", [P, RING * 2 * P])
                ps_s = pb(done, "ps_s", [P, RING * 512])
                hot, added, cleared = signal("ag_hot"), signal("ag_added"), signal("ag_cleared")
                read = (signal("ag_read0"), signal("ag_read1"))
                total = width + extra_width
                one = lambda m, j: onehot[:, (m % RING * 2 + j) * P:(m % RING * 2 + j + 1) * P]
                with nc.Block() as block:
                    filled = fill(block, read)

                    @block.tensor
                    def _(pe):
                        with pe.Fori(0, NPAIR) as i:
                            for n in range(2 * CP):
                                k, m = divmod(n, CP)
                                g = i * (2 * CP) + n
                                if m == 0:
                                    for sig, per in filled:
                                        pe.wait_ge(sig[k].sem, sig[k].at((i + 1) * per))
                                pe.wait_ge(hot.sem, hot.at(g + 1))
                                pe.wait_ge(added.sem, added.at(i * (2 * CP) + max(n - RING + 1, 0)))
                                to = ps_s[:, n % RING * 512:n % RING * 512 + total]
                                if extra:
                                    for j in range(2):
                                        pe.matmul(to[:, width:total], one(n, j), extra(k, 2 * m + j),
                                                  start=(j == 0), stop=(j == 1))
                                for j in range(2):
                                    last_mm = pe.matmul(to[:, 0:width], one(n, j), rhs(k, 2 * m + j),
                                                        start=(j == 0), stop=(j == 1))
                                last_mm.then_inc(read[k].sem, 1)

                    @block.vector
                    def _(dve):
                        def make_onehots(g, n):
                            for j in range(2):
                                cell = bass.ds(g * 2 + j, 1)
                                if scale is None:
                                    last = dve.tensor_scalar(one(n, j), iota_row[:, :], dloc_e[:, cell], None, ALU.is_equal)
                                else:
                                    last = dve.tensor_scalar(one(n, j), iota_row[:, :], dloc_e[:, cell], scale[:, cell],
                                                             ALU.is_equal, ALU.mult)
                            last.then_inc(hot.sem, 1)
                        for n in range(AHEAD):
                            make_onehots(n, n)
                        if clear:
                            dve.memset(acc[:, :], 0.0).then_inc(cleared.sem, 1)
                            dve.wait_ge(cleared.sem, cleared.at(1))
                        with dve.Fori(0, NPAIR) as i:
                            for n in range(2 * CP):
                                k, m = divmod(n, CP)
                                if m == 0:
                                    _, ws = nc.values_load_multi_w_load_instructions(
                                        window_of[0:1, bass.ds(i * (2 * CP) + n, CP)],
                                        engines=(mybir.EngineType.DVE,), min_val=0, max_val=NW - 1)
                                if n == 0:
                                    dve.wait_ge(read[1].sem, read[1].at(i * CP))
                                else:
                                    dve.wait_ge(read[(n - 1) // CP].sem, read[(n - 1) // CP].at(i * CP + (n - 1) % CP + 1))
                                make_onehots(i * (2 * CP) + n + AHEAD, n + AHEAD)
                                dve.wait_ge(read[k].sem, read[k].at(i * CP + m + 1))
                                dve.wait_ge(added.sem, added.at(i * (2 * CP) + n))
                                at = acc[:, bass.ds(ws[m] * total, total)]
                                dve.tensor_tensor(at, at, ps_s[:, n % RING * 512:n % RING * 512 + total], ALU.add)\
                                   .then_inc(added.sem, 1)
                steps = NCH * CP
                stage_end(ag_hot=steps + AHEAD, ag_read0=NPAIR * CP, ag_read1=NPAIR * CP, ag_added=steps,
                          ag_cleared=1 if clear else 0)

        def conv_sums(acc, weight, with_edges):
            done = ExitStack()
            with done:
                vb = sb(done, "vb", [P, 2 * CB * D])
                pv = sb(done, "pv", [P, 2 * CB * ACCW])
                eb = sb(done, "eb", [P, 2 * CB * D]) if with_edges else None
                v_in, pv_made, e_in = ((signal(n + "0"), signal(n + "1")) for n in ("cs_v_in", "cs_pv_made", "cs_e_in"))
                vb4 = vb[:, :].rearrange("p (k s c) -> p k s c", k=2, s=CB)
                pv4 = pv[:, :].rearrange("p (k s c) -> p k s c", k=2, s=CB)
                eb4 = eb[:, :].rearrange("p (k s c) -> p k s c", k=2, s=CB) if with_edges else None
                w3 = weight[:, :].rearrange("p (s h) -> p s h", h=H)
                per_pv = 6

                def fill(block, read):
                    @block.sync
                    def _(sp):
                        with sp.Fori(0, NPAIR) as i:
                            for k in range(2):
                                sp.wait_ge(pv_made[k].sem, pv_made[k].at(i * per_pv))
                                sp.dma_start(vb4[:, k], v_steps.rearrange("p (s c) -> p s c", c=D)
                                             [:, bass.ds((i * 2 + k) * CB, CB), :]).then_inc(v_in[k].sem, 16)
                                if with_edges:
                                    sp.wait_ge(read[k].sem, read[k].at(i * CP))
                                    _, ts = nc.values_load_multi_w_load_instructions(
                                        pair_of[0:1, bass.ds((i * 2 + k) * CP, CP)],
                                        engines=(mybir.EngineType.SP,), min_val=0, max_val=NTP)
                                    for m in range(CP):
                                        sp.dma_start(eb4[:, k, 2 * m:2 * m + 2, :],
                                                     a["edge_attr"][bass.ds(ts[m] * (2 * P), 2 * P), :]
                                                     .rearrange("(j e) c -> e j c", j=2)).then_inc(e_in[k].sem, 16)

                    @block.gpsimd
                    def _(pool):
                        with pool.Fori(0, NPAIR) as i:
                            for k in range(2):
                                pool.wait_ge(read[k].sem, read[k].at(i * CP))
                                pool.wait_ge(v_in[k].sem, v_in[k].at((i + 1) * 16))
                                chunk = bass.ds((i * 2 + k) * CB, CB)
                                for h in range(H):
                                    pool.tensor_tensor(pv4[:, k, :, h * C:(h + 1) * C], vb4[:, k, :, h * C:(h + 1) * C],
                                                       w3[:, chunk, h:h + 1].to_broadcast([P, CB, C]), ALU.mult)\
                                        .then_inc(pv_made[k].sem, 1)
                                pool.tensor_copy(pv4[:, k, :, D:D + H], w3[:, chunk, :]).then_inc(pv_made[k].sem, 1)
                                pool.tensor_tensor(pv4[:, k, :, D + H:ACCW], w3[:, chunk, :],
                                                   ew_e[:, chunk].unsqueeze(2).to_broadcast([P, CB, H]), ALU.mult)\
                                    .then_inc(pv_made[k].sem, 1)
                    return [(pv_made, per_pv)] + ([(e_in, 16 * CP)] if with_edges else [])

                aggregate(acc, ACCW, lambda k, s: pv4[:, k, s, :], fill,
                          extra=(lambda k, s: eb4[:, k, s, :]) if with_edges else None, extra_width=D if with_edges else 0)
                stage_end(cs_v_in0=16 * NPAIR, cs_v_in1=16 * NPAIR, cs_pv_made0=per_pv * NPAIR,
                          cs_pv_made1=per_pv * NPAIR)
                if with_edges:
                    stage_end(cs_e_in0=16 * CP * NPAIR, cs_e_in1=16 * CP * NPAIR)

        def conv_finish(acc, total, y, layer, residual):
            done = ExitStack()
            with done:
                we_b = sb(done, "we_b", [P, D])
                rec = sb(done, "rec", [P, NW * H])
                pe_ = sb(done, "pe_", [P, NW * H])
                loaded, chained, stored = signal("cf_loaded"), signal("cf_chain"), signal("cf_stored")
                acc3 = acc[:, :].rearrange("p (w c) -> p w c", w=NW)
                y3 = y[:, :].rearrange("p (w c) -> p w c", w=NW)
                rec3 = rec[:, :].rearrange("p (w h) -> p w h", h=H)
                pe3 = pe_[:, :].rearrange("p (w h) -> p w h", h=H)
                counts = {}
                with nc.Block() as block:
                    @block.sync
                    def _(sp):
                        sp.dma_start(we_b[:, :], a[f"L0_gnn_We{layer}"][0, :].partition_broadcast(P)).then_inc(loaded.sem, 16)
                        sp.dma_start(y[:, :], skip_rows).then_inc(loaded.sem, 16)
                        if total > ACCW:
                            sp.dma_start(agg_rows.rearrange("p (w c) -> p w c", w=NW), acc3[:, :, ACCW:total])\
                              .then_inc(stored.sem, 16)
                            sp.wait_ge(stored.sem, stored.at(16))

                    @block.vector
                    def _(dve):
                        link = chain(dve, chained)
                        link(dve.tensor_scalar(rec3, acc3[:, :, D:D + H], 1e-30, None, ALU.max))
                        link(dve.reciprocal(rec[:, :], rec[:, :]))
                        link(dve.tensor_tensor(pe3, acc3[:, :, D + H:ACCW], rec3, ALU.mult))
                        dve.wait_ge(loaded.sem, loaded.at(32))
                        for h in range(H):
                            part, to = acc3[:, :, h * C:(h + 1) * C], y3[:, :, h * C:(h + 1) * C]
                            link(dve.tensor_tensor(part, part, rec3[:, :, h:h + 1].to_broadcast([P, NW, C]), ALU.mult))
                            link(dve.tensor_tensor(to, to, part, ALU.add))
                            link(dve.tensor_tensor(part, pe3[:, :, h:h + 1].to_broadcast([P, NW, C]),
                                                   we_b[:, h * C:(h + 1) * C].unsqueeze(1).to_broadcast([P, NW, C]), ALU.mult))
                            link(dve.tensor_tensor(to, to, part, ALU.add))
                        if residual:
                            link(dve.tensor_tensor(y[:, :], y[:, :], x[:, :], ALU.add))
                        counts["chain"] = link.count[0]
                stage_end(cf_loaded=32, cf_chain=counts["chain"], cf_stored=16 if total > ACCW else 0)

        def norm_steps(dve, link, scratch, y, to, std_needed, std_ready):
            sq, mean, var = scratch
            y3, sq3, to3 = (t[:, :].rearrange("p (w c) -> p w c", w=NW) for t in (y, sq, to))
            over = lambda t: t[:, :].unsqueeze(2).to_broadcast([P, NW, D])
            link(dve.tensor_reduce(mean[:, :], y3, AX.X, ALU.add))
            link(dve.tensor_scalar(mean[:, :], mean[:, :], 1.0 / D, None, ALU.mult))
            link(dve.tensor_tensor(y3, y3, over(mean), ALU.subtract))
            link(dve.tensor_tensor(sq3, y3, y3, ALU.mult))
            link(dve.tensor_reduce(var[:, :], sq3, AX.X, ALU.add))
            link(dve.tensor_scalar(var[:, :], var[:, :], 1.0 / D, EPS, ALU.mult, ALU.add))
            dve.sem_inc(std_needed.sem, 1)
            dve.wait_ge(std_ready.sem, std_ready.at(norm_steps.count + 1))
            norm_steps.count += 1
            link(dve.reciprocal(var[:, :], var[:, :]))
            link(dve.tensor_tensor(to3, y3, over(var), ALU.mult))

        def norm_roots(act_e, scratch, n, std_needed, std_ready):
            for i in range(n):
                act_e.wait_ge(std_needed.sem, std_needed.at(i + 1))
                act_e.activation(scratch[2][:, :], scratch[2][:, :], ACT.Sqrt).then_inc(std_ready.sem, 1)

        def norm_scratch(stack):
            return (sb(stack, "ln_sq", [P, NW * D]), sb(stack, "ln_mean", [P, NW]), sb(stack, "ln_var", [P, NW]))

        def layer_norm(y):
            done = ExitStack()
            with done:
                scratch = norm_scratch(done)
                chained, needed, ready = signal("ln_chain"), signal("ln_needed"), signal("ln_ready")
                counts = {}
                norm_steps.count = 0
                with nc.Block() as block:
                    @block.vector
                    def _(dve):
                        link = chain(dve, chained)
                        norm_steps(dve, link, scratch, y, x, needed, ready)
                        counts["chain"] = link.count[0]

                    @block.scalar
                    def _(act_e):
                        norm_roots(act_e, scratch, 1, needed, ready)
                stage_end(ln_chain=counts["chain"], ln_needed=1, ln_ready=1)

        def mlp_layer():
            done = ExitStack()
            with done:
                agg = sb(done, "agg", [P, NW * D])
                y = sb(done, "y", [P, NW * D])
                w1 = sb(done, "w1", [P, 2 * 2 * D])
                w2 = sb(done, "w2", [P, 2 * D])
                b1 = sb(done, "b1", [P, 2])
                b2_b = sb(done, "b2_b", [P, D])
                gamma_b = sb(done, "gamma_b", [P, D])
                beta_b = sb(done, "beta_b", [P, D])
                xg = sb(done, "xg", [P, 2 * G * D])
                xt = sb(done, "xt", [P, 2 * G * D])
                ht = sb(done, "ht", [P, 2 * G * D])
                scratch = norm_scratch(done)
                ps_x = pb(done, "ps_x", [P, 1024])
                ps_h = pb(done, "ps_h", [P, 4 * 512])
                ps_y = pb(done, "ps_y", [P, 1024])
                (loaded, got, turned, xt_ready, hidden, silued, made, added, chained, needed, ready) = (
                    signal(n) for n in ("ml_loaded", "ml_got", "ml_turned", "ml_xt", "ml_hidden", "ml_silued",
                                        "ml_made", "ml_added", "ml_chain", "ln_needed", "ln_ready"))
                counts = {}
                norm_steps.count = 0
                GD = G * D
                HALF = GD // 2
                with nc.Block() as block:
                    @block.sync
                    def _(sp):
                        loads = [(agg[:, :], agg_rows), (w1[:, 0:2 * D], a["L1_gnn_W1"][0:D, :]),
                                 (w1[:, 2 * D:4 * D], a["L1_gnn_W1"][D:2 * D, :]), (w2[:, 0:D], a["L1_gnn_W2"][0:D, :]),
                                 (w2[:, D:2 * D], a["L1_gnn_W2"][D:2 * D, :]), (b1[:, :], a["L1_gnn_b1"]),
                                 (b2_b[:, :], a["L1_gnn_b2"].partition_broadcast(P)),
                                 (gamma_b[:, :], a["L1_gnn_ln_gamma"].partition_broadcast(P)),
                                 (beta_b[:, :], a["L1_gnn_ln_beta"].partition_broadcast(P))]
                        for to, of in loads:
                            sp.dma_start(to, of).then_inc(loaded.sem, 16)

                    @block.scalar
                    def _(act_e):
                        act_e.wait_ge(loaded.sem, 16 * 9)
                        with act_e.Fori(0, NG) as g:
                            act_e.wait_ge(turned.sem, turned.at(g * 2))
                            for n, t in enumerate((x, agg)):
                                act_e.copy(xg[:, n * GD:(n + 1) * GD], t[:, bass.ds(g * GD, GD)]).then_inc(got.sem, 1)
                            for n in range(2):
                                act_e.wait_ge(turned.sem, turned.at(g * 2 + n + 1))
                                act_e.wait_ge(hidden.sem, hidden.at(g * 4))
                                act_e.copy(xt[:, n * GD:(n + 1) * GD], ps_x[:, 0:GD]).then_inc(xt_ready.sem, 1)
                            for n in range(4):
                                j, half = divmod(n, 2)
                                act_e.wait_ge(hidden.sem, hidden.at(g * 4 + n + 1))
                                act_e.wait_ge(made.sem, made.at(g))
                                act_e.activation(ht[:, j * GD + half * HALF:j * GD + (half + 1) * HALF],
                                                 ps_h[:, n * 512:n * 512 + HALF], ACT.Silu, bias=b1[:, j:j + 1])\
                                     .then_inc(silued.sem, 1)
                        norm_roots(act_e, scratch, 2, needed, ready)

                    @block.tensor
                    def _(pe):
                        pe.wait_ge(loaded.sem, 16 * 9)
                        with pe.Fori(0, NG) as g:
                            for n in range(2):
                                pe.wait_ge(got.sem, got.at(g * 2 + n + 1))
                                pe.wait_ge(xt_ready.sem, xt_ready.at(g * 2 + n))
                                for j in range(G):
                                    at = n * GD + j * D
                                    last_mm = pe.transpose(ps_x[:, j * D:(j + 1) * D], xg[:, at:at + D], ident[:, :])
                                last_mm.then_inc(turned.sem, 1)
                            pe.wait_ge(xt_ready.sem, xt_ready.at(g * 2 + 2))
                            pe.wait_ge(silued.sem, silued.at(g * 4))
                            for n in range(4):
                                j, half = divmod(n, 2)
                                for k in range(2):
                                    last_mm = pe.matmul(ps_h[:, n * 512:n * 512 + HALF],
                                                        w1[:, k * 2 * D + j * D:k * 2 * D + (j + 1) * D],
                                                        xt[:, k * GD + half * HALF:k * GD + (half + 1) * HALF],
                                                        start=(k == 0), stop=(k == 1))
                                last_mm.then_inc(hidden.sem, 1)
                            pe.wait_ge(silued.sem, silued.at(g * 4 + 4))
                            pe.wait_ge(added.sem, added.at(g))
                            for w in range(G):
                                for j in range(2):
                                    last_mm = pe.matmul(ps_y[:, w * D:(w + 1) * D], ht[:, j * GD + w * D:j * GD + (w + 1) * D],
                                                        w2[:, j * D:(j + 1) * D], start=(j == 0), stop=(j == 1))
                            last_mm.then_inc(made.sem, 1)

                    @block.vector
                    def _(dve):
                        dve.wait_ge(loaded.sem, 16 * 9)
                        with dve.Fori(0, NG) as g:
                            dve.wait_ge(made.sem, made.at(g + 1))
                            dve.tensor_tensor(grouped_at(y, g), ps_y[:, 0:GD].rearrange("p (g c) -> p g c", g=G),
                                              b2_b[:, :].unsqueeze(1).to_broadcast([P, G, D]), ALU.add)\
                               .then_inc(added.sem, 1)
                        dve.wait_ge(added.sem, added.at(NG))
                        link = chain(dve, chained)
                        norm_steps(dve, link, scratch, y, y, needed, ready)
                        y3 = y[:, :].rearrange("p (w c) -> p w c", w=NW)
                        every = lambda t: t[:, :].unsqueeze(1).to_broadcast([P, NW, D])
                        link(dve.tensor_tensor(y3, y3, every(gamma_b), ALU.mult))
                        link(dve.tensor_tensor(y3, y3, every(beta_b), ALU.add))
                        link(dve.tensor_tensor(y[:, :], y[:, :], x[:, :], ALU.add))
                        link(dve.tensor_tensor(y[:, :], y[:, :], x[:, :], ALU.add))
                        norm_steps(dve, link, scratch, y, x, needed, ready)
                        counts["chain"] = link.count[0]
                stage_end(ml_loaded=0, ln_needed=2, ln_ready=2)

        def grouped_at(t, g):
            return t[:, bass.ds(g * (G * D), G * D)].rearrange("p (g c) -> p g c", g=G)

        def relation_weights(wrel, rel_b):
            done = ExitStack()
            with done:
                basis = sb(done, "basis", [NBASIS, 2 * (2 * D + RD)])
                coef = sb(done, "coef", [NBASIS, 2 * R16])
                emb = sb(done, "emb", [RD, R16])
                bias_b = sb(done, "bias_b", [P, 2 * R16])
                prod = sb(done, "prod", [RD, 2 * R16])
                ps_w = pb(done, "ps_w", [P, 512])
                ps_r = pb(done, "ps_r", [P, 512])
                loaded, made, chained = signal("rw_loaded"), signal("rw_made"), signal("rw_chain")
                IN = 2 * D + RD
                with nc.Block() as block:
                    @block.sync
                    def _(sp):
                        loads = [(emb[:, :], a["edge_embeddings_t"])]
                        for n, k in enumerate("sr"):
                            loads += [(basis[:, n * IN:(n + 1) * IN], a[f"L2_gnn_basis_{k}"]),
                                      (coef[:, n * R16:(n + 1) * R16], a[f"coef_{k}_t"]),
                                      (bias_b[:, n * R16:(n + 1) * R16], a[f"L2_gnn_b_{k}"].partition_broadcast(P))]
                        for to, of in loads:
                            sp.dma_start(to, of).then_inc(loaded.sem, 16)

                    @block.tensor
                    def _(pe):
                        pe.wait_ge(loaded.sem, 16 * 7)
                        for n in range(2):
                            c = coef[:, n * R16:(n + 1) * R16]
                            for m in range(2):
                                at = (2 * n + m) * R16
                                pe.matmul(ps_w[:, at:at + R16], basis[:, n * IN + m * D:n * IN + (m + 1) * D], c,
                                          start=True, stop=True)
                            last_mm = pe.matmul(ps_r[0:RD, n * R16:(n + 1) * R16], basis[:, n * IN + 2 * D:(n + 1) * IN], c,
                                                start=True, stop=True)
                        last_mm.then_inc(made.sem, 1)
                        pe.wait_ge(chained.sem, 3)
                        pe.matmul(ps_w[:, 256:256 + 2 * R16], ones[0:RD, :], prod[:, :], start=True, stop=True)\
                          .then_inc(made.sem, 1)

                    @block.vector
                    def _(dve):
                        link = chain(dve, chained)
                        dve.wait_ge(made.sem, 1)
                        link(dve.tensor_copy(wrel[:, :], ps_w[:, 0:4 * R16]))
                        for n in range(2):
                            link(dve.tensor_tensor(prod[:, n * R16:(n + 1) * R16], ps_r[0:RD, n * R16:(n + 1) * R16],
                                                   emb[:, :], ALU.mult))
                        dve.wait_ge(made.sem, 2)
                        link(dve.tensor_tensor(rel_b[:, :], ps_w[:, 256:256 + 2 * R16], bias_b[:, :], ALU.add))

        def relation_project(wrel, rel_b, dsplit, xnm):
            done = ExitStack()
            with done:
                s_out = sb(done, "s_out", [P, G * R16])
                d_out = sb(done, "d_out", [P, G * R16])
                nm_out = sb(done, "nm_out", [P, G * 2 * R16])
                rest = sb(done, "rest", [P, G * R16])
                part = sb(done, "part", [P, G * R16], BF16)
                d3 = dsplit[:, :].rearrange("p (w k c) -> p w k c", k=3, c=R16)

                def window(dve, y, j):
                    dve.tensor_copy(grouped(s_out)[:, j, :], y[:, 0:R16])
                    dve.tensor_tensor(grouped(d_out)[:, j, :], y[:, R16:2 * R16], rel_b[:, 0:R16], ALU.add)
                    return dve.tensor_copy(grouped(nm_out)[:, j, :], y[:, 2 * R16:4 * R16])

                def group(dve, g, link):
                    split3(dve, link, d_out, part, rest, lambda k: d3[:, bass.ds(g * G, G), k, :])
                    link(dve.tensor_copy(xnm[:, bass.ds(g * (G * 2 * R16), G * 2 * R16)], nm_out[:, :]))

                def stores(g):
                    return [(score_table.rearrange("(w p) c -> p w c", p=P)[:, bass.ds(g * G, G), :], grouped(s_out))]
                project(x, wrel, 4 * R16, lambda sp, sig: None, 0, stores, window, group, 8)

        def relation_scores(dsplit, score, typed):
            done = ExitStack()
            with done:
                idx = sb(done, "idx", [P, 2 * CB], I32)
                from_src = sb(done, "from_src", [P, 2 * CB])
                dl_row = sb(done, "dl_row", [P, 2 * CB * P], BF16)
                st = sb(done, "st", [P, 2 * CB * P], BF16)
                picked = sb(done, "picked", [P, CB * R16])
                total = sb(done, "total", [P, CB])
                ps_d = pb(done, "ps_d", [P, 2 * 512])
                idx_ready, de_made, chained = (signal(n) for n in ("rs_idx", "rs_de_made", "rs_chain"))
                st_made = (signal("rs_st0"), signal("rs_st1"))
                issuing = signal("issuing")
                gathered, dl_in, summed = ((signal(n + "0"), signal(n + "1")) for n in ("rs_gathered", "rs_dl_in", "rs_summed"))
                st4 = st[:, :].rearrange("p (k s e) -> p k s e", k=2, s=CB)
                dl3 = dl_row[:, :].rearrange("p (k n) -> p k n", k=2)
                r3 = lambda t: t[:, :].rearrange("p (s r) -> p s r", r=R16)
                ps4 = ps_d[:, :].rearrange("p (k c) -> p k c", k=2)[:, :, 0:CB * R16]
                flat_scores = score_table.rearrange("n (r o) -> (n r) o", o=1)
                with nc.Block() as block:
                    @block.gpsimd
                    def _(pool):
                        with pool.Fori(0, NPAIR) as i:
                            for k in range(2):
                                pool.wait_ge(summed[k].sem, summed[k].at(i))
                                pool.tensor_copy(idx[:, k * CB:(k + 1) * CB], src16_i[:, bass.ds((i * 2 + k) * CB, CB)])\
                                    .then_inc(idx_ready.sem, 1)
                                pool.wait_ge(idx_ready.sem, idx_ready.at(i * 2 + k + 1))
                                pool.sem_inc(issuing.sem, 1)
                                for s in range(CB):
                                    pool.indirect_dma_start(
                                        from_src[:, k * CB + s:k * CB + s + 1], None, flat_scores,
                                        bass.IndirectOffsetOnAxis(ap=idx[:, k * CB + s:k * CB + s + 1], axis=0))\
                                        .then_inc(gathered[k].sem, 16)

                    @block.scalar
                    def _(act_e):
                        with act_e.Fori(0, NPAIR) as i:
                            for k in range(2):
                                act_e.wait_ge(st_made[k].sem, st_made[k].at(i))
                                act_e.dma_start(dl3[:, k, :], dloc_slots[0, bass.ds((i * 2 + k) * (CB * P), CB * P)]
                                                .partition_broadcast(P)).then_inc(dl_in[k].sem, 16)

                    @block.tensor
                    def _(pe):
                        with pe.Fori(0, NPAIR) as i:
                            for k in range(2):
                                pe.wait_ge(st_made[k].sem, st_made[k].at(i + 1))
                                pe.wait_ge(summed[k].sem, summed[k].at(i))
                                _, ws = nc.values_load_multi_w_load_instructions(
                                    window_of[0:1, bass.ds((i * 2 + k) * CP, CP)],
                                    engines=(mybir.EngineType.PE,), min_val=0, max_val=NW - 1)
                                for s in range(CB):
                                    for part in range(3):
                                        last_mm = pe.matmul(ps4[:, k, s * R16:(s + 1) * R16], st4[:, k, s, :],
                                                            dsplit[:, bass.ds(ws[s // 2] * (3 * R16) + part * R16, R16)],
                                                            start=(part == 0), stop=(part == 2))
                                last_mm.then_inc(de_made.sem, 1)

                    @block.vector
                    def _(dve):
                        dve.memset(score[:, NCH * CB:], 0.0)
                        L = 4
                        with dve.Fori(0, NPAIR) as i:
                            for k in range(2):
                                link = chain(dve, chained, i * (2 * L) + k * L)
                                chunk = bass.ds((i * 2 + k) * CB, CB)
                                dve.wait_ge(dl_in[k].sem, dl_in[k].at((i + 1) * 16))
                                dve.wait_ge(de_made.sem, de_made.at(i * 2))
                                dve.tensor_scalar(st4[:, k].rearrange("p s e -> p (s e)"), dl3[:, k, :], iota_col[:, :],
                                                  None, ALU.is_equal).then_inc(st_made[k].sem, 1)
                                link(dve.tensor_tensor(r3(typed)[:, chunk, :], et16_e[:, chunk].unsqueeze(2).to_broadcast([P, CB, R16]),
                                                       iota_row[:, 0:R16].unsqueeze(1).to_broadcast([P, CB, R16]),
                                                       ALU.is_equal))
                                dve.wait_ge(de_made.sem, de_made.at(i * 2 + k + 1))
                                link(dve.tensor_tensor(picked[:, :], ps4[:, k, :], typed[:, bass.ds((i * 2 + k) * (CB * R16), CB * R16)],
                                                       ALU.mult))
                                link(dve.tensor_reduce(total[:, :], r3(picked), AX.X, ALU.add))
                                dve.wait_ge(gathered[k].sem, gathered[k].at((i + 1) * (16 * CB)))
                                link(dve.tensor_tensor(score[:, chunk], total[:, :], from_src[:, k * CB:(k + 1) * CB], ALU.add))
                                dve.sem_inc(summed[k].sem, 1)

        def relation_sums(acc, weight, typed):
            done = ExitStack()
            with done:
                wb = sb(done, "wb", [P, 2 * CB * R16])
                made = (signal("rr_made0"), signal("rr_made1"))
                t3 = typed[:, :].rearrange("p (s r) -> p s r", r=R16)
                w4 = wb[:, :].rearrange("p (k s r) -> p k s r", k=2, s=CB)

                def fill(block, read):
                    @block.gpsimd
                    def _(pool):
                        with pool.Fori(0, NPAIR) as i:
                            for k in range(2):
                                chunk = bass.ds((i * 2 + k) * CB, CB)
                                pool.wait_ge(read[k].sem, read[k].at(i * CP))
                                pool.tensor_tensor(w4[:, k], t3[:, chunk, :], weight[:, chunk].unsqueeze(2)
                                                   .to_broadcast([P, CB, R16]), ALU.mult).then_inc(made[k].sem, 1)
                    return [(made, 1)]
                aggregate(acc, R16, lambda k, s: w4[:, k, s, :], fill)

        def relation_finish(acc, rel_b, xnm):
            done = ExitStack()
            with done:
                y = sb(done, "y", [P, NW * D])
                scratch = norm_scratch(done)
                share, present, rel, tmp = (sb(done, n, [P, NW * R16]) for n in ("share", "present", "rel", "tmp"))
                top = sb(done, "top", [P, NW])
                chained, needed, ready = signal("rf_chain"), signal("ln_needed"), signal("ln_ready")
                exp_needed, exp_ready = signal("rf_exp_needed"), signal("rf_exp_ready")
                norm_steps.count = 0
                xnm3 = xnm[:, :].rearrange("p (w c) -> p w c", w=NW)
                r3 = lambda t: t[:, :].rearrange("p (w r) -> p w r", w=NW)
                over = lambda t, n: t[:, :].unsqueeze(2).to_broadcast([P, NW, n])
                with nc.Block() as block:
                    @block.vector
                    def _(dve):
                        link = chain(dve, chained)
                        link(dve.tensor_scalar(present[:, :], acc[:, :], 0.5, None, ALU.is_gt))
                        link(dve.tensor_scalar(share[:, :], acc[:, :], 1e-30, None, ALU.max))
                        link(dve.reciprocal(share[:, :], share[:, :]))
                        link(dve.tensor_tensor(share[:, :], share[:, :], acc[:, :], ALU.mult))
                        link(dve.tensor_tensor(r3(rel), r3(share), xnm3[:, :, R16:2 * R16], ALU.mult))
                        link(dve.tensor_tensor(r3(rel), r3(rel), xnm3[:, :, 0:R16], ALU.add))
                        link(dve.tensor_tensor(r3(rel), r3(rel), rel_b[:, R16:2 * R16].unsqueeze(1)
                                               .to_broadcast([P, NW, R16]), ALU.add))
                        link(dve.tensor_tensor(rel[:, :], rel[:, :], present[:, :], ALU.mult))
                        link(dve.tensor_scalar(tmp[:, :], present[:, :], -1.0, 1e10, ALU.add, ALU.mult))
                        link(dve.tensor_tensor(rel[:, :], rel[:, :], tmp[:, :], ALU.add))
                        link(dve.tensor_reduce(top[:, :], r3(rel), AX.X, ALU.max))
                        link(dve.tensor_tensor(r3(rel), r3(rel), over(top, R16), ALU.subtract))
                        dve.sem_inc(exp_needed.sem, 1)
                        dve.wait_ge(exp_ready.sem, 1)
                        link(dve.tensor_reduce(top[:, :], r3(rel), AX.X, ALU.add))
                        link(dve.reciprocal(top[:, :], top[:, :]))
                        link(dve.tensor_tensor(rel[:, :], rel[:, :], share[:, :], ALU.mult))
                        link(dve.tensor_tensor(r3(rel), r3(rel), over(top, R16), ALU.mult))
                        link(dve.tensor_reduce(top[:, :], r3(rel), AX.X, ALU.add))
                        link(dve.tensor_scalar(top[:, :], top[:, :], 2.0, None, ALU.add))
                        link(dve.tensor_tensor(y[:, :].rearrange("p (w c) -> p w c", w=NW),
                                               x[:, :].rearrange("p (w c) -> p w c", w=NW), over(top, D), ALU.mult))
                        norm_steps(dve, link, scratch, y, x, needed, ready)

                    @block.scalar
                    def _(act_e):
                        act_e.wait_ge(exp_needed.sem, 1)
                        act_e.activation(rel[:, :], rel[:, :], ACT.Exp).then_inc(exp_ready.sem, 1)
                        norm_roots(act_e, scratch, 1, needed, ready)
                stage_end(ln_needed=1, ln_ready=1)

        def rgcn_project(src, layer, acc):
            done = ExitStack()
            with done:
                w_all = sb(done, "w_all", [P, (R4 + 1) * D])
                b_b = sb(done, "b_b", [P, D])
                y_out = sb(done, "y_out", [P, G * R4 * D])
                root = sb(done, "root", [P, G * D])

                def load(sp, sig):
                    for r in range(R4):
                        sp.dma_start(w_all[:, r * D:(r + 1) * D], a[f"L3_gnn_W{layer}"][r]).then_inc(sig.sem, 16)
                    sp.dma_start(w_all[:, R4 * D:], a[f"L3_gnn_root{layer}"]).then_inc(sig.sem, 16)
                    sp.dma_start(b_b[:, :], a[f"L3_gnn_b{layer}"].partition_broadcast(P)).then_inc(sig.sem, 16)

                def window(dve, y, j):
                    dve.tensor_copy(grouped(y_out)[:, j, :], y[:, 0:R4 * D])
                    return dve.tensor_tensor(grouped(root)[:, j, :], y[:, R4 * D:], b_b[:, :], ALU.add)

                def group(dve, g, link):
                    link(dve.tensor_copy(grouped_at(acc, g), grouped(root)))

                def stores(g):
                    return [(rel_table.rearrange("(w p) c -> p w c", p=P)[:, bass.ds(g * G, G), :], grouped(y_out))]
                project(src, w_all, (R4 + 1) * D, load, R4 + 2, stores, window, group, 1)

        def rgcn_sums(acc):
            done = ExitStack()
            with done:
                idx = sb(done, "idx", [P, 2 * CB], I32)
                yb = sb(done, "yb", [P, 2 * CB * D])
                idx_ready, issuing = signal("rg_idx"), signal("issuing")
                gathered = (signal("rg_gathered0"), signal("rg_gathered1"))
                yb4 = yb[:, :].rearrange("p (k s c) -> p k s c", k=2, s=CB)
                rows = rel_table.rearrange("n (r c) -> (n r) c", c=D)

                def fill(block, read):
                    @block.gpsimd
                    def _(pool):
                        with pool.Fori(0, NPAIR) as i:
                            for k in range(2):
                                pool.wait_ge(read[k].sem, read[k].at(i * CP))
                                pool.tensor_copy(idx[:, k * CB:(k + 1) * CB], src4_i[:, bass.ds((i * 2 + k) * CB, CB)])\
                                    .then_inc(idx_ready.sem, 1)
                                pool.wait_ge(idx_ready.sem, idx_ready.at(i * 2 + k + 1))
                                pool.sem_inc(issuing.sem, 1)
                                for s in range(CB):
                                    pool.indirect_dma_start(
                                        yb4[:, k, s, :], None, rows,
                                        bass.IndirectOffsetOnAxis(ap=idx[:, k * CB + s:k * CB + s + 1], axis=0))\
                                        .then_inc(gathered[k].sem, 16)
                    return [(gathered, 16 * CB)]
                aggregate(acc, D, lambda k, s: yb4[:, k, s, :], fill, scale=ewn_e, clear=False)
                stage_end(rg_idx=NCH, rg_gathered0=16 * CB * NPAIR, rg_gathered1=16 * CB * NPAIR)

        def on_vector(emit):
            sig = signal("ov_chain")
            counts = {}
            with nc.Block() as block:
                @block.vector
                def _(dve):
                    link = chain(dve, sig)
                    emit(dve, link)
                    counts["n"] = link.count[0]
            stage_end(ov_chain=counts["n"])

        tables()
        h_rows = dram("h_rows", (P, NW * D), F32)
        if STOP == "T": return finish(nc, ctx, signal, x, out)

        def copy_rows(to, of):
            moved = signal("h_moved")
            with nc.Block() as block:
                @block.sync
                def _(sp):
                    sp.dma_start(to, of).then_inc(moved.sem, 16)
                    sp.wait_ge(moved.sem, moved.at(16))
            stage_end(h_moved=16)

        for layer in (1, 2):
            total = ACCW + (D if layer == 1 else 0)
            with ExitStack() as conv:
                alpha = sb(conv, "alpha", [P, SP * H])
                with ExitStack() as scoring:
                    qsplit = sb(scoring, "qsplit", [P, NW * 3 * QW], BF16)
                    if layer == 1:
                        conv_project(x, layer, qsplit)
                    else:
                        with ExitStack() as hidden:
                            h1 = sb(hidden, "h1", [P, NW * D])
                            copy_rows(h1[:, :], h_rows)
                            conv_project(h1, layer, qsplit)
                    conv_scores(qsplit, alpha)
                edge_softmax(alpha, H)
                acc = sb(conv, "acc", [P, NW * total])
                conv_sums(acc, alpha, with_edges=layer == 1)
                y = sb(conv, "y", [P, NW * D])
                conv_finish(acc, total, y, layer, residual=layer == 2)
                if layer == 1:
                    copy_rows(h_rows, y[:, :])
                else:
                    layer_norm(y)
        if STOP == "L0": return finish(nc, ctx, signal, x, out)
        mlp_layer()
        with ExitStack() as rel:
            rel_b = sb(rel, "rel_b", [P, 2 * R16])
            xnm = sb(rel, "xnm", [P, NW * 2 * R16])
            score = sb(rel, "score", [P, SP])
            acc = sb(rel, "acc", [P, NW * R16])
            typed = sb(rel, "typed", [P, SP * R16], BF16)
            with ExitStack() as scoring:
                wrel = sb(scoring, "wrel", [P, 4 * R16])
                dsplit = sb(scoring, "dsplit", [P, NW * 3 * R16], BF16)
                relation_weights(wrel, rel_b)
                relation_project(wrel, rel_b, dsplit, xnm)
                relation_scores(dsplit, score, typed)
            edge_softmax(score, R16)
            relation_sums(acc, score, typed)
            relation_finish(acc, rel_b, xnm)
        with ExitStack() as rgcn:
            acc1 = sb(rgcn, "acc1", [P, NW * D])
            acc2 = sb(rgcn, "acc2", [P, NW * D])
            rgcn_project(x, 1, acc1)
            rgcn_sums(acc1)
            on_vector(lambda dve, link: link(dve.tensor_scalar(acc1[:, :], acc1[:, :], 0.0, None, ALU.max)))
            rgcn_project(acc1, 2, acc2)
            rgcn_sums(acc2)
            on_vector(lambda dve, link: link(dve.tensor_tensor(acc2[:, :], acc2[:, :], x[:, :], ALU.add)))
            layer_norm(acc2)
        finish(nc, ctx, signal, x, out)


def finish(nc, ctx, signal, x, out):
    stored = signal("out_stored")
    full = N // P
    with nc.Block() as block:
        @block.sync
        def _(sp):
            sp.dma_start(out[0:full * P, :].rearrange("(w p) c -> p w c", p=P),
                         x[:, 0:full * D].rearrange("p (w c) -> p w c", c=D)).then_inc(stored.sem, 16)
            sp.dma_start(out[full * P:N, :], x[0:N - full * P, full * D:(full + 1) * D]).then_inc(stored.sem, 16)
            sp.wait_ge(stored.sem, 32)

STOP = None

def kernel(**inputs):
    import concourse.bacc as bacc
    from concourse.bass_utils import run_bass_kernel_spmd

    pad = 2 * NTP * P - E

    def by_tile(v, fill):
        v = np.asarray(v)
        return np.concatenate([v, np.full(pad + 2 * P, fill, v.dtype)]).reshape(2 * NTP + 2, P)

    arrays = {}
    xs = np.zeros((NPAD, D), np.float32)
    xs[:N] = np.asarray(inputs["x"])
    arrays["x"] = np.ascontiguousarray(xs.reshape(NW, P, D).transpose(1, 0, 2)).reshape(P, NW * D)
    dst = np.asarray(inputs["dst"])
    outside = np.full(1, NOWHERE, np.int32)
    ints = {"dst": by_tile(dst, NOWHERE), "before": by_tile(np.concatenate([outside, dst[:-1]]), NOWHERE),
            "after": by_tile(np.concatenate([dst[1:], outside]), NOWHERE), "src": by_tile(inputs["src"], 0),
            "et16": by_tile(inputs["edge_type_16"], 0), "et4": by_tile(inputs["edge_type_4"], 0)}
    arrays["int_rows"] = np.concatenate([ints[n] for n in INT_TABLES], axis=1)
    ew = np.asarray(inputs["edge_weight"])
    arrays["ew_rows"] = np.concatenate([ew, np.repeat(ew[-1:], pad + 2 * P)]).reshape(2 * NTP + 2, P)
    last = np.zeros(TC * P, np.int32)
    last[:NTP] = ints["dst"][1:2 * NTP:2, -1]
    arrays["pair_last"] = np.ascontiguousarray(last.reshape(TC, P).T)
    edge_attr = np.zeros(((2 * NTP + 2) * P, D), np.float32)
    edge_attr[:E] = np.asarray(inputs["edge_attr_128"])
    arrays["edge_attr"] = edge_attr
    number = np.full(TC * P, 4 * SP, np.float32)
    number[:NTP] = np.arange(NTP)
    arrays["c_pair_no"] = np.ascontiguousarray(number.reshape(TC, P).T)
    slot = np.arange(SP)
    arrays["c_step_t"] = (slot // 2).astype(np.float32).reshape(P, SB)
    arrays["c_odd_t"] = (slot % 2).astype(np.float32).reshape(P, SB)
    arrays["c_steps_row"] = np.ascontiguousarray(np.broadcast_to((slot // 2).astype(np.float32), (P, SP)))
    arrays["c_iota_row"] = np.ascontiguousarray(np.broadcast_to(np.arange(P, dtype=np.float32), (P, P)))
    arrays["c_iota_col"] = np.arange(P, dtype=np.float32).reshape(P, 1)
    arrays["c_ident"] = np.eye(P, dtype=np.float32)
    for name, v in inputs.items():
        if name.startswith("L"):
            arrays[name] = np.ascontiguousarray(np.asarray(v))
    arrays["L1_gnn_b1"] = np.ascontiguousarray(arrays["L1_gnn_b1"].reshape(2, D).T)
    arrays["edge_embeddings_t"] = np.ascontiguousarray(arrays.pop("L2_gnn_edge_embeddings").T)
    for k in "sr":
        arrays[f"coef_{k}_t"] = np.ascontiguousarray(arrays.pop(f"L2_gnn_coef_{k}").T)

    nc = bacc.Bacc("TRN2", target_bir_lowering=False, num_devices=1)
    a = {name: nc.dram_tensor(f"in_{name}", v.shape, mybir.dt.from_np(v.dtype), kind="ExternalInput").ap()
         for name, v in arrays.items()}
    out = nc.dram_tensor("out_x", (N, D), F32, kind="ExternalOutput").ap()
    gnn_program(nc, a, out)
    result = run_bass_kernel_spmd(nc, [{f"in_{name}": v for name, v in arrays.items()}], core_ids=[0])
    return result.results[0]["out_x"]
```

```python
from contextlib import ExitStack

import concourse.bass as bass
import numpy as np
from concourse import mybir

F32, BF16, I32 = mybir.dt.float32, mybir.dt.bfloat16, mybir.dt.int32
ALU, ACT, AX = mybir.AluOpType, mybir.ActivationFunctionType, mybir.AxisListType

P = 128
N, E, D = 6250, 100000, 128
H, C = 4, 32
R16, R4, RD, NBASIS = 16, 4, 32, 8
NW = -(-N // P)
NPAD = NW * P
NT = -(-E // P)
NTP = -(-NT // 2)
STEPS = NTP + NW - 1
SLOTS = 2 * STEPS
SB = -(-SLOTS // P)
SP = SB * P
CB = 20
CP = CB // 2
NCH = -(-SLOTS // CB)
NCH += NCH % 2
NPAIR = NCH // 2
assert NCH * CB <= SP and CB % 4 == 0
TC = -(-NTP // P)
G = 7
NG = NW // G
BIG = 1e30
NOWHERE = 1000000
KC = C + 1
KVW = D + H * KC
QW = H * KC
ACCW = D + 2 * H
EPS = 1e-5
INT_TABLES = ("dst", "before", "after", "src", "et16", "et4")


FROM_ONE = ("np_turned", "np_made", "np_xt", "np_added", "np_stored0", "np_stored1", "np_evacuated", "np_kept", "sc_summed0", "sc_summed1", "sc_qe_used", "sc_out0",
            "sc_out1", "sc_st0", "sc_st1", "rs_st0", "rs_st1", "ag_read0", "ag_read1", "ag_added", "cs_pv_made0", "cs_pv_made1", "ml_turned", "ml_hidden",
            "ml_made", "ml_xt", "ml_silued", "ml_added", "ml_normed", "ml_based", "rs_summed0", "rs_summed1", "rs_de_made", "rr_read0", "rr_read1")


class Signal:

    def __init__(self, sem, base):
        self.sem, self.base = sem, base

    def at(self, n):
        return self.base + n


def gnn_program(nc, a, out):
    ctx = ExitStack()
    signals = {}
    used = {}

    def signal(name):
        if name not in signals:
            signals[name] = Signal(ctx.enter_context(nc.semaphore(name)), 1 if name in FROM_ONE else 0)
        return signals[name]

    def stage_end(**counts):
        for name, n in counts.items():
            signals[name].base += n

    def dram(name, shape, dt):
        return nc.dram_tensor(name, shape, dt).ap()

    def chain(engine, sig, base=0):
        count = [0]

        def link(ins):
            count[0] += 1
            ins.then_inc(sig.sem, 1)
            engine.wait_ge(sig.sem, sig.at(base + count[0]))
        link.count = count
        return link

    kv_table = dram("kv_table", (NPAD, KVW), F32)
    v_steps = dram("v_steps", (P, NCH * CB * D), F32)
    skip_rows = dram("skip_rows", (P, NW * D), F32)
    agg_rows = dram("agg_rows", (P, NW * D), F32)
    dloc_slots = dram("dloc_slots", (1, SP * P), BF16)
    score_table = dram("score_table", (NPAD, R16), F32)
    rel_table = dram("rel_table", (NPAD, R4 * D), F32)

    with ctx:
        def sb(stack, name, shape, dt=F32):
            used[name] = used.get(name, 0) + 1
            return stack.enter_context(nc.sbuf_tensor(f"{name}_{used[name]}", shape, dt))

        def pb(stack, name, shape, dt=F32):
            used[name] = used.get(name, 0) + 1
            return stack.enter_context(nc.psum_tensor(f"{name}_{used[name]}", shape, dt))

        x = sb(ctx, "x", [P, NW * D])
        ident = sb(ctx, "ident", [P, P])
        iota_row = sb(ctx, "iota_row", [P, P])
        iota_col = sb(ctx, "iota_col", [P, 1])
        ones = sb(ctx, "ones", [P, P])
        window_of = sb(ctx, "window_of", [1, SP // 2], I32)
        pair_of = sb(ctx, "pair_of", [1, SP // 2], I32)
        dloc_e = sb(ctx, "dloc_e", [P, SP])
        ew_e = sb(ctx, "ew_e", [P, SP])
        et16_e = sb(ctx, "et16_e", [P, SP])
        src_i = sb(ctx, "src_i", [P, SP], I32)
        src16_i = sb(ctx, "src16_i", [P, SP], I32)
        src4_i = sb(ctx, "src4_i", [P, SP], I32)
        ewn_e = sb(ctx, "ewn_e", [P, SP])
        reset_t = sb(ctx, "reset_t", [P, SP])
        close_t = sb(ctx, "close_t", [P, SP])
        cumreset_t = sb(ctx, "cumreset_t", [P, SP])
        cumclose_t = sb(ctx, "cumclose_t", [P, SP])
        amask_t = sb(ctx, "amask_t", [P, SP])
        et16_t = sb(ctx, "et16_t", [P, SP])

        def tables():
            done = ExitStack()
            with done:
                ones_b = sb(done, "ones_b", [P, P], BF16)
                steps_row = sb(done, "steps_row", [P, SP])
                pair_no = sb(done, "pair_no", [P, TC])
                odd_t = sb(done, "odd_t", [P, SB])
                step_t = sb(done, "step_t", [P, SB])
                last_i = sb(done, "last_i", [P, TC], I32)
                lastw_i = sb(done, "lastw_i", [P, TC], I32)
                last = sb(done, "last", [P, TC])
                cmp = sb(done, "cmp", [P, TC * SP], BF16)
                pair_t = sb(done, "pair_t", [P, SB])
                tile_t = sb(done, "tile_t", [P, SB])
                tile_t_i = sb(done, "tile_t_i", [P, SB], I32)
                negw_t = sb(done, "negw_t", [P, SB])
                tile_row = sb(done, "tile_row", [1, SP])
                win_row = sb(done, "win_row", [1, SP])
                packed = sb(done, "packed", [P, SB * 6 * P], I32)
                ew_t = sb(done, "ew_t", [P, SP])
                dl = sb(done, "dl", [P, SP])
                act = sb(done, "act", [P, SP])
                tmp = sb(done, "tmp", [P, SP])
                src_t = sb(done, "src_t", [P, SP])
                dl_b = sb(done, "dl_b", [P, SP], BF16)
                src16_t = sb(done, "src16_t", [P, SP])
                src4_t = sb(done, "src4_t", [P, SP])
                ext = sb(done, "ext", [P, 2])
                ext2 = sb(done, "ext2", [2, 1])
                ext_d = sb(done, "ext_d", [2, 2])
                ext_b = sb(done, "ext_b", [P, 4])
                ps_row = pb(done, "ps_row", [P, 1024])
                ps_t = pb(done, "ps_t", [P, 512])
                ps_e = pb(done, "ps_e", [P, 2 * 1024])
                loaded, gathered, chained, counted, turned, copied, stored, ext_s = (
                    signal(n) for n in ("tb_loaded", "tb_gathered", "tb_chain", "tb_counted",
                                        "tb_turned", "tb_copied", "tb_stored", "tb_ext"))
                idx_ready = signal("tb_idx_ready")
                cmp_v = cmp[:, :].rearrange("p (c s) -> p c s", c=TC)
                pk = packed[:, :].rearrange("p (b f e) -> p b f e", b=SB, f=6)
                blocked = lambda t: t[:, :].rearrange("p (b e) -> p b e", b=SB)
                to_turn = [(dl, dloc_e), (ew_t, ew_e), (et16_t, et16_e), (src_t, src_i),
                           (src16_t, src16_i), (src4_t, src4_i)]
                half = SP // 2
                with nc.Block() as block:
                    @block.sync
                    def _(sp):
                        for name in FROM_ONE:
                            sp.sem_inc(signal(name).sem, 1)
                        loads = [(x[:, :], a["x"]), (ident[:, :], a["c_ident"]), (iota_row[:, :], a["c_iota_row"]),
                                 (iota_col[:, :], a["c_iota_col"]), (steps_row[:, :], a["c_steps_row"]),
                                 (pair_no[:, :], a["c_pair_no"]), (step_t[:, :], a["c_step_t"]),
                                 (odd_t[:, :], a["c_odd_t"]),
                                 (last_i[:, :], a["pair_last"])]
                        for to, of in loads:
                            sp.dma_start(to, of).then_inc(loaded.sem, 16)
                        sp.wait_ge(chained.sem, 100)
                        sp.dma_start(dloc_slots.rearrange("o (p e) -> (o p) e", p=P), dl_b[:, :]).then_inc(stored.sem, 16)
                        sp.wait_ge(stored.sem, 16)

                    @block.vector
                    def _(dve):
                        link = chain(dve, chained)
                        link(dve.memset(ones[:, :], 1.0))
                        link(dve.memset(ones_b[:, :], 1.0))
                        dve.wait_ge(loaded.sem, 16 * 9)
                        link(dve.tensor_scalar(lastw_i[:, :], last_i[:, :], 7, None, ALU.arith_shift_right))
                        link(dve.tensor_copy(last[:, :], lastw_i[:, :]))
                        link(dve.scalar_tensor_tensor(last[:, :], last[:, :], float(NW - 1), pair_no[:, :], ALU.min, ALU.add))
                        for c in range(TC):
                            dve.tensor_scalar(cmp_v[:, c, :], steps_row[:, :], last[:, c:c + 1], None,
                                              ALU.is_gt).then_inc(counted.sem, 1)
                        dve.wait_ge(turned.sem, 1)
                        link(dve.tensor_copy(pair_t[:, :], ps_t[:, 0:SB]))
                        link(dve.scalar_tensor_tensor(tile_t[:, :], pair_t[:, :], 2.0, odd_t[:, :], ALU.mult, ALU.add))
                        dve.tensor_copy(tile_t_i[:, :], tile_t[:, :]).then_inc(idx_ready.sem, 1)
                        link(dve.tensor_tensor(negw_t[:, :], step_t[:, :], pair_t[:, :], ALU.subtract))
                        link(dve.tensor_scalar(negw_t[:, :], negw_t[:, :], float(NW - 1), -float(P), ALU.min, ALU.mult))
                        for h in range(2):
                            dve.tensor_copy(tile_row[:, h * half:(h + 1) * half], ps_row[0:1, h * 512:h * 512 + half])\
                               .then_inc(chained.sem, 1)
                            link.count[0] += 1
                        dve.wait_ge(chained.sem, link.count[0])
                        link(dve.tensor_copy(pair_of[:, :], tile_row[:, 0::2]))
                        link(dve.tensor_tensor(win_row[:, :], steps_row[0:1, :], tile_row[:, :], ALU.subtract))
                        link(dve.tensor_scalar(win_row[:, :], win_row[:, :], float(NW - 1), None, ALU.min))
                        link(dve.tensor_copy(window_of[:, :], win_row[:, 0::2]))
                        dve.wait_ge(gathered.sem, 16 * 2 * SB)
                        for b in range(SB):
                            link(dve.tensor_scalar(blocked(dl)[:, b, :], pk[:, b, 0, :], negw_t[:, b:b + 1], None, ALU.add))
                        link(dve.tensor_scalar(tmp[:, :], dl[:, :], 0.0, None, ALU.is_ge))
                        link(dve.scalar_tensor_tensor(act[:, :], dl[:, :], P - 0.5, tmp[:, :], ALU.is_le, ALU.mult))
                        link(dve.tensor_scalar(amask_t[:, :], act[:, :], -1.0, BIG, ALU.add, ALU.mult))
                        for other, flag in ((1, reset_t), (2, close_t)):
                            link(dve.tensor_tensor(blocked(tmp), pk[:, :, 0, :], pk[:, :, other, :], ALU.not_equal))
                            link(dve.scalar_tensor_tensor(flag[:, :], tmp[:, :], -BIG, act[:, :], ALU.mult, ALU.mult))
                        link(dve.memset(tmp[:, :], 0.0))
                        link(dve.tensor_tensor_scan(cumreset_t[:, :], tmp[:, :], reset_t[:, :], 0.0, ALU.add, ALU.add))
                        link(dve.tensor_tensor_scan(cumclose_t[:, ::-1], tmp[:, :], close_t[:, ::-1], 0.0, ALU.add, ALU.add))
                        link(dve.scalar_tensor_tensor(dl[:, :], dl[:, :], 1.0, act[:, :], ALU.add, ALU.mult))
                        link(dve.tensor_scalar(dl[:, :], dl[:, :], -1.0, None, ALU.add))
                        link(dve.tensor_copy(dl_b[:, :], dl[:, :]))
                        link(dve.tensor_copy(blocked(src_t), pk[:, :, 3, :]))
                        link(dve.tensor_copy(blocked(et16_t), pk[:, :, 4, :]))
                        link(dve.scalar_tensor_tensor(blocked(src16_t), blocked(src_t), float(R16), pk[:, :, 4, :], ALU.mult, ALU.add))
                        link(dve.scalar_tensor_tensor(blocked(src4_t), blocked(src_t), float(R4), pk[:, :, 5, :], ALU.mult, ALU.add))
                        link(dve.tensor_reduce(ext[:, 0:1], ew_t[:, :], AX.X, ALU.max))
                        link(dve.tensor_reduce(ext[:, 1:2], ew_t[:, :], AX.X, ALU.min))
                        link(dve.tensor_scalar(ext[:, 1:2], ext[:, 1:2], -1.0, None, ALU.mult))
                        dve.sem_inc(chained.sem, 100 - link.count[0])
                        link.count[0] = 100
                        dve.wait_ge(ext_s.sem, 1)
                        link(dve.tensor_reduce(ext2[:, :], ps_t[0:2, 128:256], AX.X, ALU.max))
                        dve.tensor_scalar(ext_d[:, :], ident[0:2, 0:2], ext2[:, :], None, ALU.mult).then_inc(counted.sem, 1)
                        dve.wait_ge(ext_s.sem, 2)
                        link(dve.tensor_copy(ext_b[:, 0:2], ps_t[:, 256:258]))
                        link(dve.tensor_tensor(ext_b[:, 2:3], ext_b[:, 0:1], ext_b[:, 1:2], ALU.add))
                        link(dve.tensor_scalar(ext_b[:, 2:3], ext_b[:, 2:3], 1e-8, None, ALU.add))
                        link(dve.reciprocal(ext_b[:, 3:4], ext_b[:, 2:3]))
                        dve.wait_ge(copied.sem, 2)
                        link(dve.tensor_scalar(ewn_e[:, :], ew_e[:, :], ext_b[:, 1:2], ext_b[:, 3:4], ALU.add, ALU.mult))

                    @block.tensor
                    def _(pe):
                        pe.wait_ge(counted.sem, TC)
                        for h in range(2):
                            for c in range(TC):
                                pe.matmul(ps_row[:, h * 512:h * 512 + half], ones_b[:, :],
                                          cmp_v[:, c, h * half:(h + 1) * half], start=(c == 0), stop=(c == TC - 1))
                        for b in range(SB):
                            for c in range(TC):
                                last_mm = pe.matmul(ps_t[:, b:b + 1], cmp_v[:, c, b::SB], ones_b[:, 0:1],
                                                    start=(c == 0), stop=(c == TC - 1))
                        last_mm.then_inc(turned.sem, 1)
                        pe.wait_ge(chained.sem, 100)
                        pe.transpose(ps_t[0:2, 128:256], ext[:, :], ident[:, :]).then_inc(ext_s.sem, 1)
                        pe.wait_ge(counted.sem, TC + 1)
                        pe.matmul(ps_t[:, 256:258], ones[0:2, :], ext_d[:, :], start=True, stop=True).then_inc(ext_s.sem, 1)
                        for n, (of, _) in enumerate(to_turn):
                            if n >= 2:
                                pe.wait_ge(copied.sem, n - 1)
                            for b in range(SB):
                                at = n % 2 * 1024 + b * P
                                last_mm = pe.transpose(ps_e[:, at:at + P], blocked(of)[:, b, :], ident[:, :])
                            last_mm.then_inc(turned.sem, 1)

                    @block.scalar
                    def _(act_e):
                        for n, (_, to) in enumerate(to_turn):
                            act_e.wait_ge(turned.sem, n + 2)
                            at = n % 2 * 1024
                            act_e.copy(to[:, :].rearrange("e (p b) -> e b p", b=SB),
                                       ps_e[:, at:at + SP].rearrange("e (b p) -> e b p", b=SB)).then_inc(copied.sem, 1)

                    @block.gpsimd
                    def _(pool):
                        pool.wait_ge(idx_ready.sem, 1)
                        for b in range(SB):
                            at = bass.IndirectOffsetOnAxis(ap=tile_t_i[:, b:b + 1], axis=0)
                            pool.indirect_dma_start(pk[:, b, :, :].rearrange("p f e -> p (f e)"), None,
                                                    a["int_rows"], at).then_inc(gathered.sem, 16)
                            pool.indirect_dma_start(blocked(ew_t)[:, b, :], None, a["ew_rows"], at)\
                                .then_inc(gathered.sem, 16)

        def project(src, w_all, cols, load, n_loads, stores, window, group, n_links, first=None,
                    act_window=None, keep=None):
            done = ExitStack()
            with done:
                slots = 4 if cols <= 512 else 2
                wide = 2048 // slots
                xg = sb(done, "xg", [P, G * D])
                xt = sb(done, "xt", [P, G * D])
                ps_x = pb(done, "ps_x", [P, 1024])
                ps_y = pb(done, "ps_y", [P, 2048])
                loaded, got, turned, xt_ready, made, added, chained = (
                    signal(n) for n in ("np_loaded", "np_got", "np_turned", "np_xt", "np_made",
                                        "np_added", "np_chain"))
                evacuated, kept, issuing = signal("np_evacuated"), signal("np_kept"), signal("issuing")
                HALVES = ((0, 4), (4, G))
                starts = [lo for lo, _ in HALVES]
                stored = (signal("np_stored0"), signal("np_stored1"))
                results = signal("np_results")
                n_stores = len(stores(0, 0, 1))
                pre = [0]
                with nc.Block() as block:
                    @block.sync
                    def _(sp):
                        load(sp, loaded)
                        with sp.Fori(0, NG) as g:
                            for (lo, hi), sig in zip(HALVES, stored):
                                sp.wait_ge(added.sem, added.at(g * G + hi))
                                sp.sem_inc(issuing.sem, 1)
                                if act_window:
                                    sp.wait_ge(evacuated.sem, evacuated.at(g * G + hi))
                                    sp.sem_inc(issuing.sem, 1)
                                for to, of in stores(g, lo, hi):
                                    sp.dma_start(to, of).then_inc(sig.sem, 16)
                        for sig in stored:
                            sp.wait_ge(sig.sem, sig.at(NG * 16 * n_stores))

                    @block.scalar
                    def _(act_e):
                        def take(g):
                            act_e.wait_ge(turned.sem, turned.at(g + 1))
                            act_e.wait_ge(made.sem, made.at(g * G))
                            act_e.copy(xt[:, :], ps_x[:, 0:G * D]).then_inc(xt_ready.sem, 1)
                            if act_window:
                                for j in range(G):
                                    if j in starts:
                                        sig = stored[starts.index(j)]
                                        act_e.wait_ge(sig.sem, sig.at(g * (16 * n_stores)))
                                    act_e.wait_ge(made.sem, made.at(g * G + j + 1))
                                    at = j % slots * wide
                                    act_window(act_e, ps_y[:, at:at + cols], j).then_inc(evacuated.sem, 1)

                        def store_results(g):
                            if keep:
                                act_e.wait_ge(results.sem, results.at(g + 1))
                                keep(act_e, g).then_inc(kept.sem, 1)
                        take(0)
                        with act_e.Fori(1, NG) as g:
                            take(g)
                            store_results(g - 1)
                        store_results(NG - 1)

                    @block.gpsimd
                    def _(pool):
                        with pool.Fori(0, NG) as g:
                            pool.wait_ge(turned.sem, turned.at(g))
                            pool.tensor_copy(xg[:, :], src[:, bass.ds(g * (G * D), G * D)]).then_inc(got.sem, 1)

                    @block.tensor
                    def _(pe):
                        pe.wait_ge(loaded.sem, loaded.at(16 * n_loads))
                        with pe.Fori(0, NG) as g:
                            pe.wait_ge(got.sem, got.at(g + 1))
                            pe.wait_ge(xt_ready.sem, xt_ready.at(g))
                            for j in range(G):
                                last_mm = pe.transpose(ps_x[:, j * D:(j + 1) * D], xg[:, j * D:(j + 1) * D], ident[:, :])
                            last_mm.then_inc(turned.sem, 1)
                            pe.wait_ge(xt_ready.sem, xt_ready.at(g + 1))
                            for j in range(G):
                                pe.wait_ge(added.sem, added.at(g * G + max(j - slots + 1, 0)))
                                if act_window:
                                    pe.wait_ge(evacuated.sem, evacuated.at(g * G + max(j - slots + 1, 0)))
                                for c in range(0, cols, 512):
                                    n = min(512, cols - c)
                                    at = j % slots * wide + c
                                    last_mm = pe.matmul(ps_y[:, at:at + n], xt[:, j * D:(j + 1) * D], w_all[:, c:c + n],
                                                        start=True, stop=True)
                                last_mm.then_inc(made.sem, 1)

                    @block.vector
                    def _(dve):
                        dve.wait_ge(loaded.sem, loaded.at(16 * n_loads))
                        if first:
                            link = chain(dve, chained)
                            first(dve, link)
                            pre[0] = link.count[0]
                        with dve.Fori(0, NG) as g:
                            for j in range(G):
                                if j in starts:
                                    sig = stored[starts.index(j)]
                                    dve.wait_ge(sig.sem, sig.at(g * (16 * n_stores)))
                                dve.wait_ge(made.sem, made.at(g * G + j + 1))
                                at = j % slots * wide
                                window(dve, ps_y[:, at:at + cols], j).then_inc(added.sem, 1)
                            dve.wait_ge(added.sem, added.at((g + 1) * G))
                            if group:
                                if keep:
                                    dve.wait_ge(kept.sem, kept.at(g))
                                link = chain(dve, chained, g * n_links + pre[0])
                                group(dve, g, link)
                                assert link.count[0] == n_links
                                dve.sem_inc(results.sem, 1)
                stage_end(np_evacuated=NW if act_window else 0, np_results=NG if group else 0, np_kept=NG if keep else 0,
                          np_loaded=16 * n_loads, np_got=NG, np_turned=NG, np_xt=NG, np_made=NW, np_added=NW,
                          np_stored0=16 * n_stores * NG, np_stored1=16 * n_stores * NG, np_chain=pre[0] + n_links * NG)

        def split3(dve, link, value, rest, parts):
            p3 = parts[:, :].rearrange("p (k g c) -> p k g c", k=3, g=G)
            link(dve.tensor_copy(p3[:, 0], grouped(value)))
            link(dve.tensor_tensor(grouped(rest), grouped(value), p3[:, 0], ALU.subtract))
            link(dve.tensor_copy(p3[:, 1], grouped(rest)))
            link(dve.tensor_tensor(p3[:, 2], grouped(rest), p3[:, 1], ALU.subtract))

        def grouped(t):
            return t[:, :].rearrange("p (g c) -> p g c", g=G)

        def in_heads(ap):
            return ap.rearrange("p (h c) -> p h c", h=H)

        def conv_project(src, layer, qsplit):
            done = ExitStack()
            with done:
                w_all = sb(done, "w_all", [P, 4 * D])
                b_all = sb(done, "b_all", [P, 4 * D])
                we_b = sb(done, "we_b", [P, D])
                kv_out = sb(done, "kv_out", [P, G * KVW])
                sq_out = sb(done, "sq_out", [P, G * 2 * D])
                qx = sb(done, "qx", [P, G * QW])
                rest = sb(done, "rest", [P, G * QW])
                parts = sb(done, "parts", [P, 3 * G * QW], BF16)
                tmp = sb(done, "tmp", [P, G * D])
                kv3, sq3 = grouped(kv_out), grouped(sq_out)
                qx4 = qx[:, :].rearrange("p (g h c) -> p g h c", g=G, h=H)
                tmp4 = tmp[:, :].rearrange("p (g h c) -> p g h c", g=G, h=H)
                q3 = qsplit[:, :].rearrange("p (w k c) -> p w k c", k=3, c=QW)

                def load(sp, sig):
                    for n, k in enumerate(("v", "s", "q", "k")):
                        sp.dma_start(w_all[:, n * D:(n + 1) * D], a[f"L0_gnn_W{k}{layer}"]).then_inc(sig.sem, 16)
                        sp.dma_start(b_all[:, n * D:(n + 1) * D],
                                     a[f"L0_gnn_b{k}{layer}"].partition_broadcast(P)).then_inc(sig.sem, 16)
                    sp.dma_start(we_b[:, :], a[f"L0_gnn_We{layer}"][0, :].partition_broadcast(P)).then_inc(sig.sem, 16)

                def first(dve, link):
                    link(dve.memset(kv_out[:, :], 0.0))

                def window(dve, y, j):
                    dve.tensor_tensor(kv3[:, j, 0:D], y[:, 0:D], b_all[:, 0:D], ALU.add)
                    dve.tensor_tensor(sq3[:, j, :], y[:, D:3 * D], b_all[:, D:3 * D], ALU.add)
                    return dve.tensor_tensor(in_heads(kv3[:, j, D:KVW])[:, :, 0:C], in_heads(y[:, 3 * D:4 * D]),
                                             in_heads(b_all[:, 3 * D:4 * D]), ALU.add)

                def group(dve, g, link):
                    link(dve.tensor_scalar(qx4[:, :, :, 0:C], sq3[:, :, D:2 * D].rearrange("p g (h c) -> p g h c", h=H),
                                           float(C) ** -0.5, None, ALU.mult))
                    link(dve.tensor_tensor(tmp4, qx4[:, :, :, 0:C],
                                           in_heads(we_b[:, :]).unsqueeze(1).to_broadcast([P, G, H, C]), ALU.mult))
                    link(dve.tensor_reduce(qx4[:, :, :, C], tmp4, AX.X, ALU.add))
                    split3(dve, link, qx, rest, parts)

                def keep(act_e, g):
                    return act_e.copy(q3[:, bass.ds(g * G, G), :, :],
                                            parts[:, :].rearrange("p (k g c) -> p g k c", k=3, g=G))

                def stores(g, lo, hi):
                    return [(kv_table.rearrange("(w p) c -> p w c", p=P)[:, bass.ds(g * G + lo, hi - lo), :], kv3[:, lo:hi, :]),
                            (skip_rows.rearrange("p (w c) -> p w c", c=D)[:, bass.ds(g * G + lo, hi - lo), :],
                             sq3[:, lo:hi, 0:D])]
                project(src, w_all, 4 * D, load, 9, stores, window, group, 7, first, keep=keep)

        def conv_scores(qsplit, alpha):
            done = ExitStack()
            with done:
                kv = sb(done, "kv", [P, 2 * CB * KVW])
                idx = sb(done, "idx", [P, 2 * CB], I32)
                dl_row = sb(done, "dl_row", [P, 2 * CB * P], BF16)
                st = sb(done, "st", [P, 2 * CB * P], BF16)
                prod = sb(done, "prod", [P, CB * QW])
                ps_q = pb(done, "ps_q", [P, 2 * 1024])
                idx_ready, ew_in, qe_made, qe_used = (
                    signal(n) for n in ("sc_idx", "sc_ew_in", "sc_qe_made", "sc_qe_used"))
                st_made = (signal("sc_st0"), signal("sc_st1"))
                issuing = signal("issuing")
                values_out = (signal("sc_out0"), signal("sc_out1"))
                gathered, dl_in, spilled, summed = (
                    (signal(n + "0"), signal(n + "1")) for n in ("sc_gathered", "sc_dl_in", "sc_spilled", "sc_summed"))
                kv4 = kv[:, :].rearrange("p (k s c) -> p k s c", k=2, s=CB)
                st4 = st[:, :].rearrange("p (k s e) -> p k s e", k=2, s=CB)
                dl3 = dl_row[:, :].rearrange("p (k n) -> p k n", k=2)
                prod3 = prod[:, :].rearrange("p (s c) -> p s c", s=CB)
                ps4 = ps_q[:, :].rearrange("p (b s c) -> p b s c", b=2, s=4)
                al3 = alpha[:, :].rearrange("p (s h) -> p s h", h=H)
                q_of = lambda w, part: qsplit[:, bass.ds(w * (3 * QW) + part * QW, QW)]
                GQ = CB // 4
                with nc.Block() as block:
                    @block.gpsimd
                    def _(pool):
                        with pool.Fori(0, NPAIR) as i:
                            for k in range(2):
                                pool.wait_ge(summed[k].sem, summed[k].at(i))
                                pool.wait_ge(values_out[k].sem, values_out[k].at(i))
                                pool.tensor_copy(idx[:, k * CB:(k + 1) * CB], src_i[:, bass.ds((i * 2 + k) * CB, CB)])\
                                    .then_inc(idx_ready.sem, 1)
                                pool.wait_ge(idx_ready.sem, idx_ready.at(i * 2 + k + 1))
                                pool.sem_inc(issuing.sem, 1)
                                for s in range(CB):
                                    pool.indirect_dma_start(
                                        kv4[:, k, s, :], None, kv_table,
                                        bass.IndirectOffsetOnAxis(ap=idx[:, k * CB + s:k * CB + s + 1], axis=0))\
                                        .then_inc(gathered[k].sem, 16)

                    @block.sync
                    def _(sp):
                        with sp.Fori(0, NPAIR) as i:
                            for k in range(2):
                                sp.wait_ge(gathered[k].sem, gathered[k].at((i + 1) * (16 * CB)))
                                sp.dma_start(v_steps.rearrange("p (s c) -> p s c", c=D)[:, bass.ds((i * 2 + k) * CB, CB), :],
                                             kv4[:, k, :, 0:D]).then_inc(spilled[k].sem, 16)
                                sp.wait_ge(spilled[k].sem, spilled[k].at((i + 1) * 16))
                                sp.sem_inc(values_out[k].sem, 1)

                    @block.scalar
                    def _(act_e):
                        with act_e.Fori(0, NPAIR) as i:
                            for k in range(2):
                                act_e.wait_ge(st_made[k].sem, st_made[k].at(i))
                                act_e.dma_start(dl3[:, k, :], dloc_slots[0, bass.ds((i * 2 + k) * (CB * P), CB * P)]
                                                .partition_broadcast(P)).then_inc(dl_in[k].sem, 16)
                            for k in range(2):
                                act_e.wait_ge(gathered[k].sem, gathered[k].at((i + 1) * (16 * CB)))
                                act_e.copy(kv4[:, k, :, D:KVW].rearrange("p s (h c) -> p s h c", h=H)[:, :, :, C],
                                           ew_e[:, bass.ds((i * 2 + k) * CB, CB)].unsqueeze(2).to_broadcast([P, CB, H]))\
                                    .then_inc(ew_in.sem, 1)

                    @block.tensor
                    def _(pe):
                        with pe.Fori(0, NPAIR) as i:
                            for k in range(2):
                                pe.wait_ge(st_made[k].sem, st_made[k].at(i + 1))
                                _, ws = nc.values_load_multi_w_load_instructions(
                                    window_of[0:1, bass.ds((i * 2 + k) * CP, CP)],
                                    engines=(mybir.EngineType.PE,), min_val=0, max_val=NW - 1)
                                for q in range(GQ):
                                    n = 2 * GQ * i + k * GQ + q
                                    if k * GQ + q >= 2:
                                        pe.wait_ge(qe_used.sem, qe_used.at(n - 1))
                                    else:
                                        pe.wait_ge(qe_used.sem, qe_used.at(2 * GQ * i))
                                    for s in range(4):
                                        for part in range(3):
                                            last_mm = pe.matmul(ps4[:, (k * GQ + q) % 2, s, 0:QW], st4[:, k, q * 4 + s, :],
                                                                q_of(ws[(q * 4 + s) // 2], part), start=(part == 0), stop=(part == 2))
                                    last_mm.then_inc(qe_made.sem, 1)

                    @block.vector
                    def _(dve):
                        dve.memset(alpha[:, NCH * CB * H:], 0.0)
                        with dve.Fori(0, NPAIR) as i:
                            for k in range(2):
                                dve.wait_ge(dl_in[k].sem, dl_in[k].at((i + 1) * 16))
                                dve.wait_ge(qe_used.sem, qe_used.at(2 * GQ * i))
                                dve.tensor_scalar(st4[:, k].rearrange("p s e -> p (s e)"), dl3[:, k, :], iota_col[:, :],
                                                  None, ALU.is_equal).then_inc(st_made[k].sem, 1)
                                dve.wait_ge(ew_in.sem, ew_in.at(i * 2 + k + 1))
                                dve.wait_ge(summed[1 - k].sem, summed[1 - k].at(i + k))
                                for q in range(GQ):
                                    dve.wait_ge(qe_made.sem, qe_made.at(2 * GQ * i + k * GQ + q + 1))
                                    dve.tensor_tensor(prod3[:, q * 4:q * 4 + 4, :], ps4[:, (k * GQ + q) % 2, :, 0:QW],
                                                      kv4[:, k, q * 4:q * 4 + 4, D:KVW], ALU.mult).then_inc(qe_used.sem, 1)
                                dve.wait_ge(qe_used.sem, qe_used.at(2 * GQ * i + (k + 1) * GQ))
                                dve.tensor_reduce(al3[:, bass.ds((i * 2 + k) * CB, CB), :],
                                                  prod3.rearrange("p s (h c) -> p s h c", h=H),
                                                  AX.X, ALU.add).then_inc(summed[k].sem, 1)
                stage_end(sc_idx=NCH, sc_gathered0=16 * CB * NPAIR, sc_gathered1=16 * CB * NPAIR, sc_ew_in=NCH,
                          sc_dl_in0=16 * NPAIR, sc_dl_in1=16 * NPAIR, sc_st0=NPAIR, sc_st1=NPAIR, sc_qe_made=NCH * GQ,
                          sc_qe_used=NCH * GQ, sc_summed0=NPAIR, sc_summed1=NPAIR, sc_out0=NPAIR, sc_out1=NPAIR, sc_spilled0=16 * NPAIR, sc_spilled1=16 * NPAIR)

        def edge_softmax(score, lanes):
            done = ExitStack()
            by_relation = lanes == R16
            heads = 1 if by_relation else H
            with done:
                a_t = sb(done, "a_t", [P, heads * SP])
                f_t = sb(done, "f_t", [P, lanes * SP])
                lane_t = sb(done, "lane_t", [P, SP])
                eq_t = sb(done, "eq_t", [P, SP])
                back_t = sb(done, "back_t", [P, SP])
                m_t = sb(done, "m_t", [P, SP])
                ends = sb(done, "ends", [P, lanes])
                totals = sb(done, "totals", [P, lanes])
                ends_r = sb(done, "ends_r", [lanes, P])
                tot_r = sb(done, "tot_r", [lanes, P])
                carry_r = sb(done, "carry_r", [lanes, P + 1])
                carry = sb(done, "carry", [P, lanes])
                ps_a = pb(done, "ps_a", [P, 2 * 1024])
                ps_c = pb(done, "ps_c", [P, 512])
                turned_in, taken, chained, turned, out_turned, out_copied, weighed = (
                    signal(n) for n in ("sm_turned_in", "sm_taken", "sm_chain", "sm_turned", "sm_out_turned",
                                        "sm_out_copied", "sm_weighed"))
                ready = signal("sm_ready")
                s3 = score[:, :].rearrange("e (s h) -> e s h", h=heads)
                a3 = a_t[:, :].rearrange("p (h s) -> p h s", h=heads)
                lane_of = lambda t, r: t[:, bass.ds(r * SP, SP)]
                with nc.Block() as block:
                    @block.tensor
                    def _(pe):
                        for h in range(heads):
                            if h >= 2:
                                pe.wait_ge(taken.sem, taken.at(h - 1))
                            for b in range(SB):
                                at = h % 2 * 1024 + b * P
                                last_mm = pe.transpose(ps_a[:, at:at + P], s3[:, b::SB, h], ident[:, :])
                            last_mm.then_inc(turned_in.sem, 1)
                        for back in range(2):
                            pe.wait_ge(ready.sem, ready.at(2 * back + 1))
                            pe.transpose(ps_c[0:lanes, 0:P], ends[:, :], ident[:, :])
                            pe.transpose(ps_c[0:lanes, P:2 * P], totals[:, :], ident[:, :]).then_inc(turned.sem, 1)
                            pe.wait_ge(ready.sem, ready.at(2 * back + 2))
                            lo = 1 if back else 0
                            pe.transpose(ps_c[:, 2 * P:2 * P + lanes], carry_r[:, lo:lo + P], ident[0:lanes, 0:lanes])\
                              .then_inc(turned.sem, 1)
                        for h in range(heads):
                            pe.wait_ge(weighed.sem, weighed.at(h + 1))
                            if h >= 2:
                                pe.wait_ge(out_copied.sem, out_copied.at(h - 1))
                            for b in range(SB):
                                at = h % 2 * 1024 + b * P
                                last_mm = pe.transpose(ps_a[:, at:at + P], a3[:, h, b * P:(b + 1) * P], ident[:, :])
                            last_mm.then_inc(out_turned.sem, 1)

                    @block.vector
                    def _(dve):
                        count = [0]

                        def link(ins):
                            count[0] += 1
                            ins.then_inc(chained.sem, 1)
                            dve.wait_ge(chained.sem, chained.at(count[0]))

                        def lane_loop(per_lane, body):
                            start = count[0]
                            with dve.Fori(0, lanes) as r:
                                n = [0]

                                def step(ins):
                                    n[0] += 1
                                    ins.then_inc(chained.sem, 1)
                                    dve.wait_ge(chained.sem, chained.at(r * per_lane + (start + n[0])))
                                body(r, step)
                                assert n[0] == per_lane
                            count[0] = start + per_lane * lanes

                        for h in range(heads):
                            dve.wait_ge(turned_in.sem, turned_in.at(h + 1))
                            dve.tensor_tensor(a3[:, h, :], ps_a[:, h % 2 * 1024:h % 2 * 1024 + SP], amask_t[:, :], ALU.add)\
                               .then_inc(taken.sem, 1)
                        dve.wait_ge(taken.sem, taken.at(heads))

                        def lane_scores(r, step):
                            if not by_relation:
                                return lane_of(a_t, r)
                            step(dve.tensor_scalar(eq_t[:, :], et16_t[:, :], iota_row[:, bass.ds(r, 1)], -BIG,
                                                   ALU.not_equal, ALU.mult))
                            step(dve.tensor_tensor(lane_t[:, :], eq_t[:, :], a_t[:, :], ALU.add))
                            return lane_t[:, :]

                        def forward(r, step):
                            step(dve.tensor_tensor_scan(lane_of(f_t, r), reset_t[:, :], lane_scores(r, step), -BIG,
                                                        ALU.add, ALU.max))
                        lane_loop(3 if by_relation else 1, forward)

                        def carries(back, cum):
                            f3 = f_t[:, :].rearrange("p (l s) -> p l s", l=lanes)
                            edge = 0 if back else SP - 1
                            link(dve.tensor_copy(ends[:, :], f3[:, :, edge]))
                            link(dve.tensor_copy(totals[:, :], cum[:, edge:edge + 1].to_broadcast([P, lanes])))
                            dve.sem_inc(ready.sem, 1)
                            dve.wait_ge(turned.sem, turned.at(2 * back + 1))
                            link(dve.tensor_copy(ends_r[:, :], ps_c[0:lanes, 0:P]))
                            link(dve.tensor_copy(tot_r[:, :], ps_c[0:lanes, P:2 * P]))
                            link(dve.memset(carry_r[:, :], -BIG))
                            if back:
                                link(dve.tensor_tensor_scan(carry_r[:, 0:P][:, ::-1], tot_r[:, ::-1], ends_r[:, ::-1], -BIG,
                                                            ALU.add, ALU.max))
                            else:
                                link(dve.tensor_tensor_scan(carry_r[:, 1:P + 1], tot_r[:, :], ends_r[:, :], -BIG,
                                                            ALU.add, ALU.max))
                            dve.sem_inc(ready.sem, 1)
                            dve.wait_ge(turned.sem, turned.at(2 * back + 2))
                            link(dve.tensor_copy(carry[:, :], ps_c[:, 2 * P:2 * P + lanes]))

                        carries(0, cumreset_t)

                        def backward(r, step):
                            f = lane_of(f_t, r)
                            step(dve.scalar_tensor_tensor(lane_t[:, :], cumreset_t[:, :], carry[:, bass.ds(r, 1)], f,
                                                          ALU.add, ALU.max))
                            step(dve.tensor_tensor_scan(back_t[:, ::-1], close_t[:, ::-1], lane_t[:, ::-1], -BIG,
                                                        ALU.add, ALU.max))
                            step(dve.tensor_scalar(f, back_t[:, :], 0.0, None, ALU.add))
                        lane_loop(3, backward)
                        carries(1, cumclose_t)
                        if by_relation:
                            link(dve.memset(m_t[:, :], 0.0))

                            def pick(r, step):
                                f = lane_of(f_t, r)
                                step(dve.scalar_tensor_tensor(f, cumclose_t[:, :], carry[:, bass.ds(r, 1)], f, ALU.add, ALU.max))
                                step(dve.scalar_tensor_tensor(lane_t[:, :], et16_t[:, :], iota_row[:, bass.ds(r, 1)], f,
                                                              ALU.is_equal, ALU.mult))
                                step(dve.tensor_tensor(m_t[:, :], m_t[:, :], lane_t[:, :], ALU.add))
                            lane_loop(3, pick)
                            link(dve.tensor_tensor(a_t[:, :], a_t[:, :], m_t[:, :], ALU.subtract))
                        else:
                            def subtract(r, step):
                                f = lane_of(f_t, r)
                                step(dve.scalar_tensor_tensor(f, cumclose_t[:, :], carry[:, bass.ds(r, 1)], f, ALU.add, ALU.max))
                                step(dve.tensor_tensor(lane_of(a_t, r), lane_of(a_t, r), f, ALU.subtract))
                            lane_loop(2, subtract)
                        link(dve.tensor_scalar(a_t[:, :], a_t[:, :], 0.0, None, ALU.min))
                        dve.sem_inc(ready.sem, 1)
                        edge_softmax.linked = count[0]

                    @block.scalar
                    def _(act_e):
                        act_e.wait_ge(ready.sem, ready.at(5))
                        for h in range(heads):
                            act_e.activation(a3[:, h, :], a3[:, h, :], ACT.Exp).then_inc(weighed.sem, 1)
                        for h in range(heads):
                            act_e.wait_ge(out_turned.sem, out_turned.at(h + 1))
                            act_e.copy(s3.rearrange("e (p b) h -> e b p h", b=SB)[:, :, :, h],
                                       ps_a[:, h % 2 * 1024:h % 2 * 1024 + SP].rearrange("e (b p) -> e b p", b=SB))\
                                 .then_inc(out_copied.sem, 1)
                stage_end(sm_turned_in=heads, sm_taken=heads, sm_chain=edge_softmax.linked, sm_turned=4,
                          sm_out_turned=heads, sm_out_copied=heads, sm_weighed=heads, sm_ready=5)

        def aggregate(acc, width, rhs, fill, scale=None, extra=None, extra_width=0, clear=True):
            done = ExitStack()
            with done:
                RING, AHEAD = 4, 3
                onehot = sb(done, "onehot", [P, RING * 2 * P])
                ps_s = pb(done, "ps_s", [P, RING * 512])
                hot, added, cleared = signal("ag_hot"), signal("ag_added"), signal("ag_cleared")
                read = (signal("ag_read0"), signal("ag_read1"))
                total = width + extra_width
                one = lambda m, j: onehot[:, (m % RING * 2 + j) * P:(m % RING * 2 + j + 1) * P]
                with nc.Block() as block:
                    filled = fill(block, read)

                    @block.tensor
                    def _(pe):
                        with pe.Fori(0, NPAIR) as i:
                            for n in range(2 * CP):
                                k, m = divmod(n, CP)
                                g = i * (2 * CP) + n
                                if m == 0:
                                    for sig, per in filled:
                                        pe.wait_ge(sig[k].sem, sig[k].at((i + 1) * per))
                                pe.wait_ge(hot.sem, hot.at(g + 1))
                                pe.wait_ge(added.sem, added.at(i * (2 * CP) + max(n - RING + 1, 0)))
                                to = ps_s[:, n % RING * 512:n % RING * 512 + total]
                                if extra:
                                    for j in range(2):
                                        pe.matmul(to[:, width:total], one(n, j), extra(k, 2 * m + j),
                                                  start=(j == 0), stop=(j == 1))
                                for j in range(2):
                                    last_mm = pe.matmul(to[:, 0:width], one(n, j), rhs(k, 2 * m + j),
                                                        start=(j == 0), stop=(j == 1))
                                last_mm.then_inc(read[k].sem, 1)

                    @block.vector
                    def _(dve):
                        def make_onehots(g, n):
                            for j in range(2):
                                cell = bass.ds(g * 2 + j, 1)
                                if scale is None:
                                    last = dve.tensor_scalar(one(n, j), iota_row[:, :], dloc_e[:, cell], None, ALU.is_equal)
                                else:
                                    last = dve.tensor_scalar(one(n, j), iota_row[:, :], dloc_e[:, cell], scale[:, cell],
                                                             ALU.is_equal, ALU.mult)
                            last.then_inc(hot.sem, 1)
                        for n in range(AHEAD):
                            make_onehots(n, n)
                        if clear:
                            dve.memset(acc[:, :], 0.0).then_inc(cleared.sem, 1)
                            dve.wait_ge(cleared.sem, cleared.at(1))
                        with dve.Fori(0, NPAIR) as i:
                            for n in range(2 * CP):
                                k, m = divmod(n, CP)
                                if m == 0:
                                    _, ws = nc.values_load_multi_w_load_instructions(
                                        window_of[0:1, bass.ds(i * (2 * CP) + n, CP)],
                                        engines=(mybir.EngineType.DVE,), min_val=0, max_val=NW - 1)
                                if n == 0:
                                    dve.wait_ge(read[1].sem, read[1].at(i * CP))
                                else:
                                    dve.wait_ge(read[(n - 1) // CP].sem, read[(n - 1) // CP].at(i * CP + (n - 1) % CP + 1))
                                make_onehots(i * (2 * CP) + n + AHEAD, n + AHEAD)
                                dve.wait_ge(read[k].sem, read[k].at(i * CP + m + 1))
                                dve.wait_ge(added.sem, added.at(i * (2 * CP) + n))
                                at = acc[:, bass.ds(ws[m] * total, total)]
                                dve.tensor_tensor(at, at, ps_s[:, n % RING * 512:n % RING * 512 + total], ALU.add)\
                                   .then_inc(added.sem, 1)
                steps = NCH * CP
                stage_end(ag_hot=steps + AHEAD, ag_read0=NPAIR * CP, ag_read1=NPAIR * CP, ag_added=steps,
                          ag_cleared=1 if clear else 0)

        def conv_sums(acc, weight, with_edges, fetch):
            done = ExitStack()
            with done:
                vb = sb(done, "vb", [P, 2 * CB * D])
                pv = sb(done, "pv", [P, 2 * CB * ACCW])
                eb = sb(done, "eb", [P, 2 * CB * D]) if with_edges else None
                v_in, pv_made, e_in = ((signal(n + "0"), signal(n + "1")) for n in ("cs_v_in", "cs_pv_made", "cs_e_in"))
                vb4 = vb[:, :].rearrange("p (k s c) -> p k s c", k=2, s=CB)
                pv4 = pv[:, :].rearrange("p (k s c) -> p k s c", k=2, s=CB)
                eb4 = eb[:, :].rearrange("p (k s c) -> p k s c", k=2, s=CB) if with_edges else None
                w3 = weight[:, :].rearrange("p (s h) -> p s h", h=H)
                per_pv = 6
                fetched = signal("cs_fetched")

                def fill(block, read):
                    @block.sync
                    def _(sp):
                        with sp.Fori(0, NPAIR) as i:
                            for k in range(2):
                                sp.wait_ge(pv_made[k].sem, pv_made[k].at(i * per_pv))
                                sp.dma_start(vb4[:, k], v_steps.rearrange("p (s c) -> p s c", c=D)
                                             [:, bass.ds((i * 2 + k) * CB, CB), :]).then_inc(v_in[k].sem, 16)
                                if with_edges:
                                    sp.wait_ge(read[k].sem, read[k].at(i * CP))
                                    _, ts = nc.values_load_multi_w_load_instructions(
                                        pair_of[0:1, bass.ds((i * 2 + k) * CP, CP)],
                                        engines=(mybir.EngineType.SP,), min_val=0, max_val=NTP)
                                    for m in range(CP):
                                        sp.dma_start(eb4[:, k, 2 * m:2 * m + 2, :],
                                                     a["edge_attr"][bass.ds(ts[m] * (2 * P), 2 * P), :]
                                                     .rearrange("(j e) c -> e j c", j=2)).then_inc(e_in[k].sem, 16)

                    @block.scalar
                    def _(act_e):
                        for to, of in fetch:
                            act_e.dma_start(to, of).then_inc(fetched.sem, 16)
                        act_e.wait_ge(fetched.sem, fetched.at(16 * len(fetch)))

                    @block.gpsimd
                    def _(pool):
                        with pool.Fori(0, NPAIR) as i:
                            for k in range(2):
                                pool.wait_ge(read[k].sem, read[k].at(i * CP))
                                pool.wait_ge(v_in[k].sem, v_in[k].at((i + 1) * 16))
                                chunk = bass.ds((i * 2 + k) * CB, CB)
                                for h in range(H):
                                    pool.tensor_tensor(pv4[:, k, :, h * C:(h + 1) * C], vb4[:, k, :, h * C:(h + 1) * C],
                                                       w3[:, chunk, h:h + 1].to_broadcast([P, CB, C]), ALU.mult)\
                                        .then_inc(pv_made[k].sem, 1)
                                pool.tensor_copy(pv4[:, k, :, D:D + H], w3[:, chunk, :]).then_inc(pv_made[k].sem, 1)
                                pool.tensor_tensor(pv4[:, k, :, D + H:ACCW], w3[:, chunk, :],
                                                   ew_e[:, chunk].unsqueeze(2).to_broadcast([P, CB, H]), ALU.mult)\
                                    .then_inc(pv_made[k].sem, 1)
                    return [(pv_made, per_pv)] + ([(e_in, 16 * CP)] if with_edges else [])

                aggregate(acc, ACCW, lambda k, s: pv4[:, k, s, :], fill,
                          extra=(lambda k, s: eb4[:, k, s, :]) if with_edges else None, extra_width=D if with_edges else 0)
                stage_end(cs_v_in0=16 * NPAIR, cs_v_in1=16 * NPAIR, cs_pv_made0=per_pv * NPAIR,
                          cs_pv_made1=per_pv * NPAIR, cs_fetched=16 * len(fetch))
                if with_edges:
                    stage_end(cs_e_in0=16 * CP * NPAIR, cs_e_in1=16 * CP * NPAIR)

        def conv_finish(acc, total, y, layer, residual):
            done = ExitStack()
            with done:
                we_b = sb(done, "we_b", [P, D])
                rec = sb(done, "rec", [P, NW * H])
                pe_ = sb(done, "pe_", [P, NW * H])
                loaded, chained, stored = signal("cf_loaded"), signal("cf_chain"), signal("cf_stored")
                acc3 = acc[:, :].rearrange("p (w c) -> p w c", w=NW)
                y3 = y[:, :].rearrange("p (w c) -> p w c", w=NW)
                rec3 = rec[:, :].rearrange("p (w h) -> p w h", h=H)
                pe3 = pe_[:, :].rearrange("p (w h) -> p w h", h=H)
                counts = {}
                with nc.Block() as block:
                    @block.sync
                    def _(sp):
                        sp.dma_start(we_b[:, :], a[f"L0_gnn_We{layer}"][0, :].partition_broadcast(P)).then_inc(loaded.sem, 16)
                        if total > ACCW:
                            sp.dma_start(agg_rows.rearrange("p (w c) -> p w c", w=NW), acc3[:, :, ACCW:total])\
                              .then_inc(stored.sem, 16)
                            sp.wait_ge(stored.sem, stored.at(16))

                    @block.vector
                    def _(dve):
                        link = chain(dve, chained)
                        link(dve.tensor_scalar(rec3, acc3[:, :, D:D + H], 1e-30, None, ALU.max))
                        link(dve.reciprocal(rec[:, :], rec[:, :]))
                        link(dve.tensor_tensor(pe3, acc3[:, :, D + H:ACCW], rec3, ALU.mult))
                        dve.wait_ge(loaded.sem, loaded.at(16))
                        for h in range(H):
                            part, to = acc3[:, :, h * C:(h + 1) * C], y3[:, :, h * C:(h + 1) * C]
                            link(dve.tensor_tensor(part, part, rec3[:, :, h:h + 1].to_broadcast([P, NW, C]), ALU.mult))
                            link(dve.tensor_tensor(to, to, part, ALU.add))
                            link(dve.tensor_tensor(part, pe3[:, :, h:h + 1].to_broadcast([P, NW, C]),
                                                   we_b[:, h * C:(h + 1) * C].unsqueeze(1).to_broadcast([P, NW, C]), ALU.mult))
                            link(dve.tensor_tensor(to, to, part, ALU.add))
                        if residual:
                            link(dve.tensor_tensor(y[:, :], y[:, :], x[:, :], ALU.add))
                        counts["chain"] = link.count[0]
                stage_end(cf_loaded=16, cf_chain=counts["chain"], cf_stored=16 if total > ACCW else 0)

        def norm_steps(dve, link, scratch, y, to, centred, squared):
            _, mean, var, eps = scratch
            link(dve.memset(eps[:, :], EPS))
            for g in range(NG):
                ws = slice(g * G, (g + 1) * G)
                link(dve.tensor_reduce(mean[:, ws], y[:, g * G * D:(g + 1) * G * D].rearrange("p (w c) -> p w c", c=D),
                                       AX.X, ALU.add))
                link(dve.tensor_scalar(mean[:, ws], mean[:, ws], -1.0 / D, None, ALU.mult))
                dve.sem_inc(centred.sem, 1)
            for g in range(NG):
                ws = slice(g * G, (g + 1) * G)
                dve.wait_ge(squared.sem, squared.at(2 * (g + 1)))
                link(dve.reciprocal(var[:, ws], var[:, ws]))
                for w in range(g * G, (g + 1) * G):
                    last = dve.tensor_scalar(to[:, w * D:(w + 1) * D], y[:, w * D:(w + 1) * D], mean[:, w:w + 1],
                                             var[:, w:w + 1], ALU.add, ALU.mult)
                link(last)

        def norm_squares(act_e, scratch, y, centred, squared):
            sq, mean, var, eps = scratch
            for g in range(NG):
                act_e.wait_ge(centred.sem, centred.at(g + 1))
                for w in range(g * G, (g + 1) * G):
                    last = act_e.activation(sq[:, w * D:(w + 1) * D], y[:, w * D:(w + 1) * D], ACT.Square,
                                            bias=mean[:, w:w + 1], accum_out=var[:, w:w + 1])
                last.then_inc(squared.sem, 1)
                act_e.wait_ge(squared.sem, squared.at(2 * g + 1))
                ws = slice(g * G, (g + 1) * G)
                act_e.activation(var[:, ws], var[:, ws], ACT.Sqrt, bias=eps[:, :], scale=1.0 / D).then_inc(squared.sem, 1)

        def norm_scratch(stack):
            return (sb(stack, "ln_sq", [P, NW * D]), sb(stack, "ln_mean", [P, NW]), sb(stack, "ln_var", [P, NW]),
                    sb(stack, "ln_eps", [P, 1]))

        def norm_group(dve, link, y, sq, sums, squares, to, std_needed, std_ready, n):
            over = lambda t: t[:, :].unsqueeze(2).to_broadcast([P, G, D])
            link(dve.tensor_reduce(sums[:, :], y, AX.X, ALU.add))
            link(dve.scalar_tensor_tensor(y, over(sums), -1.0 / D, y, ALU.mult, ALU.add))
            link(dve.tensor_tensor(sq, y, y, ALU.mult))
            link(dve.tensor_reduce(squares[:, :], sq, AX.X, ALU.add))
            link(dve.tensor_scalar(squares[:, :], squares[:, :], 1.0 / D, EPS, ALU.mult, ALU.add))
            dve.sem_inc(std_needed.sem, 1)
            dve.wait_ge(std_ready.sem, std_ready.at(n))
            link(dve.reciprocal(squares[:, :], squares[:, :]))
            link(dve.tensor_tensor(to, y, over(squares), ALU.mult))

        def layer_norm(y):
            done = ExitStack()
            with done:
                scratch = norm_scratch(done)
                chained, centred, squared = signal("ln_chain"), signal("ln_centred"), signal("ln_squared")
                counts = {}
                with nc.Block() as block:
                    @block.vector
                    def _(dve):
                        link = chain(dve, chained)
                        norm_steps(dve, link, scratch, y, x, centred, squared)
                        counts["chain"] = link.count[0]

                    @block.scalar
                    def _(act_e):
                        norm_squares(act_e, scratch, y, centred, squared)
                stage_end(ln_chain=counts["chain"], ln_centred=NG, ln_squared=2 * NG)

        def mlp_layer():
            done = ExitStack()
            with done:
                w1 = sb(done, "w1", [P, 2 * 2 * D])
                w2 = sb(done, "w2", [P, 2 * D])
                b1 = sb(done, "b1", [P, 2])
                b2_b = sb(done, "b2_b", [P, D])
                gamma_b = sb(done, "gamma_b", [P, D])
                beta_b = sb(done, "beta_b", [P, D])
                xg = sb(done, "xg", [P, 2 * G * D])
                xt = sb(done, "xt", [P, 2 * G * D])
                ht = sb(done, "ht", [P, 2 * G * D])
                base = sb(done, "base", [P, G * D])
                y = sb(done, "y", [P, G * D])
                sq = sb(done, "sq", [P, G * D])
                sums, squares = sb(done, "sums", [P, G]), sb(done, "squares", [P, G])
                ps_x = pb(done, "ps_x", [P, 1024])
                ps_h = pb(done, "ps_h", [P, 4 * 512])
                ps_y = pb(done, "ps_y", [P, 1024])
                (loaded, got_x, got_agg, turned, xt_ready, hidden, silued, made, added, chained, based, normed) = (
                    signal(n) for n in ("ml_loaded", "ml_got_x", "ml_got_agg", "ml_turned", "ml_xt", "ml_hidden", "ml_silued",
                                        "ml_made", "ml_added", "ml_chain", "ml_based", "ml_normed"))
                needed, ready = signal("ln_needed"), signal("ln_ready")
                GD = G * D
                HALF = GD // 2
                LINKS = 16
                by_window = lambda t: t[:, :].unsqueeze(1).to_broadcast([P, G, D])
                with nc.Block() as block:
                    @block.sync
                    def _(sp):
                        loads = [(w1[:, 0:2 * D], a["L1_gnn_W1"][0:D, :]),
                                 (w1[:, 2 * D:4 * D], a["L1_gnn_W1"][D:2 * D, :]), (w2[:, 0:D], a["L1_gnn_W2"][0:D, :]),
                                 (w2[:, D:2 * D], a["L1_gnn_W2"][D:2 * D, :]), (b1[:, :], a["L1_gnn_b1"]),
                                 (b2_b[:, :], a["L1_gnn_b2"].partition_broadcast(P)),
                                 (gamma_b[:, :], a["L1_gnn_ln_gamma"].partition_broadcast(P)),
                                 (beta_b[:, :], a["L1_gnn_ln_beta"].partition_broadcast(P))]
                        for to, of in loads:
                            sp.dma_start(to, of).then_inc(loaded.sem, 16)
                        with sp.Fori(0, NG) as g:
                            sp.wait_ge(turned.sem, turned.at(g * 2))
                            sp.dma_start(xg[:, GD:2 * GD], agg_rows[:, bass.ds(g * GD, GD)]).then_inc(got_agg.sem, 16)

                    @block.gpsimd
                    def _(pool):
                        pool.wait_ge(loaded.sem, 16 * 8)
                        with pool.Fori(0, NG) as g:
                            pool.wait_ge(turned.sem, turned.at(g * 2))
                            pool.wait_ge(based.sem, based.at(g))
                            pool.tensor_copy(xg[:, 0:GD], x[:, bass.ds(g * GD, GD)]).then_inc(got_x.sem, 1)
                            pool.wait_ge(got_x.sem, got_x.at(g + 1))
                            pool.wait_ge(normed.sem, normed.at(g))
                            pool.tensor_tensor(grouped(base), xg[:, 0:GD].rearrange("p (g c) -> p g c", g=G),
                                               by_window(beta_b), ALU.add).then_inc(based.sem, 1)

                    @block.scalar
                    def _(act_e):
                        act_e.wait_ge(loaded.sem, 16 * 8)

                        def root(n):
                            act_e.wait_ge(needed.sem, needed.at(n))
                            act_e.activation(squares[:, :], squares[:, :], ACT.Sqrt).then_inc(ready.sem, 1)

                        def group(g, roots_too):
                            for n in range(2):
                                act_e.wait_ge(turned.sem, turned.at(g * 2 + n + 1))
                                act_e.wait_ge(hidden.sem, hidden.at(g * 4))
                                act_e.copy(xt[:, n * GD:(n + 1) * GD], ps_x[:, 0:GD]).then_inc(xt_ready.sem, 1)
                            if roots_too:
                                root(g * 2 - 1)
                            for n in range(4):
                                j, half = divmod(n, 2)
                                act_e.wait_ge(hidden.sem, hidden.at(g * 4 + n + 1))
                                act_e.wait_ge(made.sem, made.at(g))
                                act_e.activation(ht[:, j * GD + half * HALF:j * GD + (half + 1) * HALF],
                                                 ps_h[:, n * 512:n * 512 + HALF], ACT.Silu, bias=b1[:, j:j + 1])\
                                     .then_inc(silued.sem, 1)
                            if roots_too:
                                root(g * 2)
                        group(0, False)
                        with act_e.Fori(1, NG) as g:
                            group(g, True)
                        root(2 * NG - 1)
                        root(2 * NG)

                    @block.tensor
                    def _(pe):
                        def turn(g, n):
                            if n == 0:
                                pe.wait_ge(got_x.sem, got_x.at(g + 1))
                            else:
                                pe.wait_ge(got_agg.sem, got_agg.at((g + 1) * 16))
                            pe.wait_ge(xt_ready.sem, xt_ready.at(g * 2 + n))
                            for j in range(G):
                                at = n * GD + j * D
                                last_mm = pe.transpose(ps_x[:, j * D:(j + 1) * D], xg[:, at:at + D], ident[:, :])
                            last_mm.then_inc(turned.sem, 1)

                        def products(g, more):
                            pe.wait_ge(xt_ready.sem, xt_ready.at(g * 2 + 2))
                            pe.wait_ge(silued.sem, silued.at(g * 4))
                            for n in range(4):
                                j, half = divmod(n, 2)
                                for k in range(2):
                                    last_mm = pe.matmul(ps_h[:, n * 512:n * 512 + HALF],
                                                        w1[:, k * 2 * D + j * D:k * 2 * D + (j + 1) * D],
                                                        xt[:, k * GD + half * HALF:k * GD + (half + 1) * HALF],
                                                        start=(k == 0), stop=(k == 1))
                                last_mm.then_inc(hidden.sem, 1)
                            if more:
                                turn(g + 1, 0)
                            pe.wait_ge(silued.sem, silued.at(g * 4 + 4))
                            pe.wait_ge(added.sem, added.at(g))
                            for w in range(G):
                                for j in range(2):
                                    last_mm = pe.matmul(ps_y[:, w * D:(w + 1) * D], ht[:, j * GD + w * D:j * GD + (w + 1) * D],
                                                        w2[:, j * D:(j + 1) * D], start=(j == 0), stop=(j == 1))
                            last_mm.then_inc(made.sem, 1)
                            if more:
                                turn(g + 1, 1)
                        pe.wait_ge(loaded.sem, 16 * 8)
                        for n in range(2):
                            turn(0, n)
                        with pe.Fori(0, NG - 1) as g:
                            products(g, True)
                        products(NG - 1, False)

                    @block.vector
                    def _(dve):
                        dve.wait_ge(loaded.sem, 16 * 8)
                        with dve.Fori(0, NG) as g:
                            link = chain(dve, chained, g * LINKS)
                            dve.wait_ge(made.sem, made.at(g + 1))
                            dve.tensor_tensor(grouped(y), ps_y[:, 0:GD].rearrange("p (g c) -> p g c", g=G),
                                              by_window(b2_b), ALU.add).then_inc(added.sem, 1)
                            dve.wait_ge(added.sem, added.at(g + 1))
                            norm_group(dve, link, grouped(y), grouped(sq), sums, squares, grouped(y), needed, ready, g * 2 + 1)
                            link(dve.tensor_tensor(grouped(y), grouped(y), by_window(gamma_b), ALU.mult))
                            dve.wait_ge(based.sem, based.at(g + 1))
                            dve.tensor_tensor(y[:, :], y[:, :], base[:, :], ALU.add).then_inc(normed.sem, 1)
                            dve.wait_ge(normed.sem, normed.at(g + 1))
                            link(dve.tensor_tensor(y[:, :], y[:, :], x[:, bass.ds(g * GD, GD)], ALU.add))
                            norm_group(dve, link, grouped(y), grouped(sq), sums, squares, grouped_at(x, g), needed, ready,
                                       g * 2 + 2)
                            assert link.count[0] == LINKS
                stage_end(ln_needed=2 * NG, ln_ready=2 * NG)

        def grouped_at(t, g):
            return t[:, bass.ds(g * (G * D), G * D)].rearrange("p (g c) -> p g c", g=G)

        def relation_weights(wrel, rel_b):
            done = ExitStack()
            with done:
                basis = sb(done, "basis", [NBASIS, 2 * (2 * D + RD)])
                coef = sb(done, "coef", [NBASIS, 2 * R16])
                emb = sb(done, "emb", [RD, R16])
                bias_b = sb(done, "bias_b", [P, 2 * R16])
                prod = sb(done, "prod", [RD, 2 * R16])
                ps_w = pb(done, "ps_w", [P, 512])
                ps_r = pb(done, "ps_r", [P, 512])
                loaded, made, chained = signal("rw_loaded"), signal("rw_made"), signal("rw_chain")
                IN = 2 * D + RD
                with nc.Block() as block:
                    @block.sync
                    def _(sp):
                        loads = [(emb[:, :], a["edge_embeddings_t"])]
                        for n, k in enumerate("sr"):
                            loads += [(basis[:, n * IN:(n + 1) * IN], a[f"L2_gnn_basis_{k}"]),
                                      (coef[:, n * R16:(n + 1) * R16], a[f"coef_{k}_t"]),
                                      (bias_b[:, n * R16:(n + 1) * R16], a[f"L2_gnn_b_{k}"].partition_broadcast(P))]
                        for to, of in loads:
                            sp.dma_start(to, of).then_inc(loaded.sem, 16)

                    @block.tensor
                    def _(pe):
                        pe.wait_ge(loaded.sem, 16 * 7)
                        for n in range(2):
                            c = coef[:, n * R16:(n + 1) * R16]
                            for m in range(2):
                                at = (2 * n + m) * R16
                                pe.matmul(ps_w[:, at:at + R16], basis[:, n * IN + m * D:n * IN + (m + 1) * D], c,
                                          start=True, stop=True)
                            last_mm = pe.matmul(ps_r[0:RD, n * R16:(n + 1) * R16], basis[:, n * IN + 2 * D:(n + 1) * IN], c,
                                                start=True, stop=True)
                        last_mm.then_inc(made.sem, 1)
                        pe.wait_ge(chained.sem, 3)
                        pe.matmul(ps_w[:, 256:256 + 2 * R16], ones[0:RD, :], prod[:, :], start=True, stop=True)\
                          .then_inc(made.sem, 1)

                    @block.vector
                    def _(dve):
                        link = chain(dve, chained)
                        dve.wait_ge(made.sem, 1)
                        link(dve.tensor_copy(wrel[:, :], ps_w[:, 0:4 * R16]))
                        for n in range(2):
                            link(dve.tensor_tensor(prod[:, n * R16:(n + 1) * R16], ps_r[0:RD, n * R16:(n + 1) * R16],
                                                   emb[:, :], ALU.mult))
                        dve.wait_ge(made.sem, 2)
                        link(dve.tensor_tensor(rel_b[:, :], ps_w[:, 256:256 + 2 * R16], bias_b[:, :], ALU.add))

        def relation_project(wrel, rel_b, dsplit, xnm):
            done = ExitStack()
            with done:
                s_out = sb(done, "s_out", [P, G * R16])
                d_out = sb(done, "d_out", [P, G * R16])
                nm_out = sb(done, "nm_out", [P, G * 2 * R16])
                rest = sb(done, "rest", [P, G * R16])
                parts = sb(done, "parts", [P, 3 * G * R16], BF16)
                d3 = dsplit[:, :].rearrange("p (w k c) -> p w k c", k=3, c=R16)

                def window(dve, y, j):
                    dve.tensor_copy(grouped(s_out)[:, j, :], y[:, 0:R16])
                    dve.tensor_tensor(grouped(d_out)[:, j, :], y[:, R16:2 * R16], rel_b[:, 0:R16], ALU.add)
                    return dve.tensor_copy(grouped(nm_out)[:, j, :], y[:, 2 * R16:4 * R16])

                def group(dve, g, link):
                    split3(dve, link, d_out, rest, parts)
                    link(dve.tensor_copy(xnm[:, bass.ds(g * (G * 2 * R16), G * 2 * R16)], nm_out[:, :]))

                def keep(act_e, g):
                    return act_e.copy(d3[:, bass.ds(g * G, G), :, :],
                                            parts[:, :].rearrange("p (k g c) -> p g k c", k=3, g=G))

                def stores(g, lo, hi):
                    return [(score_table.rearrange("(w p) c -> p w c", p=P)[:, bass.ds(g * G + lo, hi - lo), :],
                             grouped(s_out)[:, lo:hi, :])]
                project(x, wrel, 4 * R16, lambda sp, sig: None, 0, stores, window, group, 5, keep=keep)

        def relation_scores(dsplit, score, typed):
            done = ExitStack()
            with done:
                idx = sb(done, "idx", [P, 2 * CB], I32)
                from_src = sb(done, "from_src", [P, 2 * CB])
                dl_row = sb(done, "dl_row", [P, 2 * CB * P], BF16)
                st = sb(done, "st", [P, 2 * CB * P], BF16)
                picked = sb(done, "picked", [P, CB * R16])
                total = sb(done, "total", [P, CB])
                ps_d = pb(done, "ps_d", [P, 2 * 512])
                idx_ready, de_made, chained = (signal(n) for n in ("rs_idx", "rs_de_made", "rs_chain"))
                st_made = (signal("rs_st0"), signal("rs_st1"))
                issuing = signal("issuing")
                gathered, dl_in, summed = ((signal(n + "0"), signal(n + "1")) for n in ("rs_gathered", "rs_dl_in", "rs_summed"))
                st4 = st[:, :].rearrange("p (k s e) -> p k s e", k=2, s=CB)
                dl3 = dl_row[:, :].rearrange("p (k n) -> p k n", k=2)
                r3 = lambda t: t[:, :].rearrange("p (s r) -> p s r", r=R16)
                ps4 = ps_d[:, :].rearrange("p (k c) -> p k c", k=2)[:, :, 0:CB * R16]
                flat_scores = score_table.rearrange("n (r o) -> (n r) o", o=1)
                with nc.Block() as block:
                    @block.gpsimd
                    def _(pool):
                        with pool.Fori(0, NPAIR) as i:
                            for k in range(2):
                                pool.wait_ge(summed[k].sem, summed[k].at(i))
                                pool.tensor_copy(idx[:, k * CB:(k + 1) * CB], src16_i[:, bass.ds((i * 2 + k) * CB, CB)])\
                                    .then_inc(idx_ready.sem, 1)
                                pool.wait_ge(idx_ready.sem, idx_ready.at(i * 2 + k + 1))
                                pool.sem_inc(issuing.sem, 1)
                                for s in range(CB):
                                    pool.indirect_dma_start(
                                        from_src[:, k * CB + s:k * CB + s + 1], None, flat_scores,
                                        bass.IndirectOffsetOnAxis(ap=idx[:, k * CB + s:k * CB + s + 1], axis=0))\
                                        .then_inc(gathered[k].sem, 16)

                    @block.scalar
                    def _(act_e):
                        with act_e.Fori(0, NPAIR) as i:
                            for k in range(2):
                                act_e.wait_ge(st_made[k].sem, st_made[k].at(i))
                                act_e.dma_start(dl3[:, k, :], dloc_slots[0, bass.ds((i * 2 + k) * (CB * P), CB * P)]
                                                .partition_broadcast(P)).then_inc(dl_in[k].sem, 16)

                    @block.tensor
                    def _(pe):
                        with pe.Fori(0, NPAIR) as i:
                            for k in range(2):
                                pe.wait_ge(st_made[k].sem, st_made[k].at(i + 1))
                                pe.wait_ge(summed[k].sem, summed[k].at(i))
                                _, ws = nc.values_load_multi_w_load_instructions(
                                    window_of[0:1, bass.ds((i * 2 + k) * CP, CP)],
                                    engines=(mybir.EngineType.PE,), min_val=0, max_val=NW - 1)
                                for s in range(CB):
                                    for part in range(3):
                                        last_mm = pe.matmul(ps4[:, k, s * R16:(s + 1) * R16], st4[:, k, s, :],
                                                            dsplit[:, bass.ds(ws[s // 2] * (3 * R16) + part * R16, R16)],
                                                            start=(part == 0), stop=(part == 2))
                                last_mm.then_inc(de_made.sem, 1)

                    @block.vector
                    def _(dve):
                        dve.memset(score[:, NCH * CB:], 0.0)
                        L = 4
                        with dve.Fori(0, NPAIR) as i:
                            for k in range(2):
                                link = chain(dve, chained, i * (2 * L) + k * L)
                                chunk = bass.ds((i * 2 + k) * CB, CB)
                                dve.wait_ge(dl_in[k].sem, dl_in[k].at((i + 1) * 16))
                                dve.wait_ge(de_made.sem, de_made.at(i * 2))
                                dve.tensor_scalar(st4[:, k].rearrange("p s e -> p (s e)"), dl3[:, k, :], iota_col[:, :],
                                                  None, ALU.is_equal).then_inc(st_made[k].sem, 1)
                                link(dve.tensor_tensor(r3(typed)[:, chunk, :], et16_e[:, chunk].unsqueeze(2).to_broadcast([P, CB, R16]),
                                                       iota_row[:, 0:R16].unsqueeze(1).to_broadcast([P, CB, R16]),
                                                       ALU.is_equal))
                                dve.wait_ge(de_made.sem, de_made.at(i * 2 + k + 1))
                                link(dve.tensor_tensor(picked[:, :], ps4[:, k, :], typed[:, bass.ds((i * 2 + k) * (CB * R16), CB * R16)],
                                                       ALU.mult))
                                link(dve.tensor_reduce(total[:, :], r3(picked), AX.X, ALU.add))
                                dve.wait_ge(gathered[k].sem, gathered[k].at((i + 1) * (16 * CB)))
                                link(dve.tensor_tensor(score[:, chunk], total[:, :], from_src[:, k * CB:(k + 1) * CB], ALU.add))
                                dve.sem_inc(summed[k].sem, 1)

        def relation_sums(acc, weight, typed):
            done = ExitStack()
            with done:
                parts = sb(done, "parts", [P, 3 * SP], BF16)
                rest = sb(done, "rest", [P, SP])
                iota_b = sb(done, "iota_b", [P, P], BF16)
                zeros = sb(done, "zeros", [P, 512], BF16)
                onehot = sb(done, "onehot", [P, 2 * CB * P], BF16)
                wb = sb(done, "wb", [P, 2 * 3 * CB * R16], BF16)
                ps_a = pb(done, "ps_a", [P, 2 * 512])
                chained, split, done_all = signal("rr_chain"), signal("rr_split"), signal("rr_done")
                zeroed = signal("rr_zeroed")
                made, hot, read = ((signal(n + "0"), signal(n + "1")) for n in ("rr_made", "rr_hot", "rr_read"))
                t3 = typed[:, :].rearrange("p (s r) -> p s r", r=R16)
                p3 = parts[:, :].rearrange("p (k s) -> p k s", k=3)
                w5 = wb[:, :].rearrange("p (b k s r) -> p b k s r", b=2, k=3, s=CB)
                one4 = onehot[:, :].rearrange("p (b s n) -> p b s n", b=2, s=CB)
                assert 512 % R16 == 0 and NW * R16 <= 2 * 512
                with nc.Block() as block:
                    @block.gpsimd
                    def _(pool):
                        pool.wait_ge(split.sem, split.at(1))
                        with pool.Fori(0, NPAIR) as i:
                            for b in range(2):
                                chunk = bass.ds((i * 2 + b) * CB, CB)
                                pool.wait_ge(read[b].sem, read[b].at(i))
                                for k in range(3):
                                    last = pool.tensor_tensor(w5[:, b, k], t3[:, chunk, :], p3[:, k, chunk].unsqueeze(2)
                                                              .to_broadcast([P, CB, R16]), ALU.mult)
                                last.then_inc(made[b].sem, 1)

                    @block.tensor
                    def _(pe):
                        pe.wait_ge(zeroed.sem, zeroed.at(1))
                        for c in range(0, NW * R16, 512):
                            n = min(512, NW * R16 - c)
                            last_mm = pe.matmul(ps_a[:, c:c + n], zeros[:, 0:P], zeros[:, 0:n], start=True, stop=True)
                        last_mm.then_inc(zeroed.sem, 1)
                        pe.wait_ge(zeroed.sem, zeroed.at(2))
                        with pe.Fori(0, NPAIR) as i:
                            for b in range(2):
                                _, ws = nc.values_load_multi_w_load_instructions(
                                    window_of[0:1, bass.ds((i * 2 + b) * CP, CP)],
                                    engines=(mybir.EngineType.PE,), min_val=0, max_val=NW - 1)
                                pe.wait_ge(hot[b].sem, hot[b].at(i + 1))
                                pe.wait_ge(made[b].sem, made[b].at(i + 1))
                                for s in range(CB):
                                    for k in range(3):
                                        last_mm = pe.matmul(ps_a[:, bass.ds(ws[s // 2] * R16, R16)], one4[:, b, s, :],
                                                            w5[:, b, k, s, :], start=False, stop=True, skip_group_check=True)
                                last_mm.then_inc(read[b].sem, 1)

                    @block.vector
                    def _(dve):
                        link = chain(dve, chained)
                        dve.memset(zeros[:, :], 0.0).then_inc(zeroed.sem, 1)
                        link(dve.tensor_copy(iota_b[:, :], iota_row[:, :]))
                        link(dve.tensor_copy(p3[:, 0], weight[:, :]))
                        link(dve.tensor_tensor(rest[:, :], weight[:, :], p3[:, 0], ALU.subtract))
                        link(dve.tensor_copy(p3[:, 1], rest[:, :]))
                        link(dve.tensor_tensor(p3[:, 2], rest[:, :], p3[:, 1], ALU.subtract))
                        dve.sem_inc(split.sem, 1)
                        with dve.Fori(0, NPAIR) as i:
                            for b in range(2):
                                dve.wait_ge(read[b].sem, read[b].at(i))
                                for s in range(CB):
                                    last = dve.tensor_scalar(one4[:, b, s, :], iota_b[:, :],
                                                             dloc_e[:, bass.ds((i * 2 + b) * CB + s, 1)], None, ALU.is_equal)
                                last.then_inc(hot[b].sem, 1)
                        for b in range(2):
                            dve.wait_ge(read[b].sem, read[b].at(NPAIR))
                        dve.tensor_copy(acc[:, :], ps_a[:, 0:NW * R16]).then_inc(done_all.sem, 1)
                        dve.wait_ge(done_all.sem, done_all.at(1))

        def relation_finish(acc, rel_b, xnm):
            done = ExitStack()
            with done:
                y = sb(done, "y", [P, NW * D])
                scratch = norm_scratch(done)
                share, present, rel, tmp = (sb(done, n, [P, NW * R16]) for n in ("share", "present", "rel", "tmp"))
                top = sb(done, "top", [P, NW])
                chained, centred, squared = signal("rf_chain"), signal("ln_centred"), signal("ln_squared")
                exp_needed, exp_ready = signal("rf_exp_needed"), signal("rf_exp_ready")
                xnm3 = xnm[:, :].rearrange("p (w c) -> p w c", w=NW)
                r3 = lambda t: t[:, :].rearrange("p (w r) -> p w r", w=NW)
                over = lambda t, n: t[:, :].unsqueeze(2).to_broadcast([P, NW, n])
                with nc.Block() as block:
                    @block.vector
                    def _(dve):
                        link = chain(dve, chained)
                        link(dve.tensor_scalar(present[:, :], acc[:, :], 0.5, None, ALU.is_gt))
                        link(dve.tensor_scalar(share[:, :], acc[:, :], 1e-30, None, ALU.max))
                        link(dve.reciprocal(share[:, :], share[:, :]))
                        link(dve.tensor_tensor(share[:, :], share[:, :], acc[:, :], ALU.mult))
                        link(dve.tensor_tensor(r3(rel), r3(share), xnm3[:, :, R16:2 * R16], ALU.mult))
                        link(dve.tensor_tensor(r3(rel), r3(rel), xnm3[:, :, 0:R16], ALU.add))
                        link(dve.tensor_tensor(r3(rel), r3(rel), rel_b[:, R16:2 * R16].unsqueeze(1)
                                               .to_broadcast([P, NW, R16]), ALU.add))
                        link(dve.tensor_tensor(rel[:, :], rel[:, :], present[:, :], ALU.mult))
                        link(dve.tensor_scalar(tmp[:, :], present[:, :], -1.0, 1e10, ALU.add, ALU.mult))
                        link(dve.tensor_tensor(rel[:, :], rel[:, :], tmp[:, :], ALU.add))
                        link(dve.tensor_reduce(top[:, :], r3(rel), AX.X, ALU.max))
                        link(dve.tensor_tensor(r3(rel), r3(rel), over(top, R16), ALU.subtract))
                        dve.sem_inc(exp_needed.sem, 1)
                        dve.wait_ge(exp_ready.sem, 1)
                        link(dve.tensor_reduce(top[:, :], r3(rel), AX.X, ALU.add))
                        link(dve.reciprocal(top[:, :], top[:, :]))
                        link(dve.tensor_tensor(rel[:, :], rel[:, :], share[:, :], ALU.mult))
                        link(dve.tensor_tensor(r3(rel), r3(rel), over(top, R16), ALU.mult))
                        link(dve.tensor_reduce(top[:, :], r3(rel), AX.X, ALU.add))
                        link(dve.tensor_scalar(top[:, :], top[:, :], 2.0, None, ALU.add))
                        link(dve.tensor_tensor(y[:, :].rearrange("p (w c) -> p w c", w=NW),
                                               x[:, :].rearrange("p (w c) -> p w c", w=NW), over(top, D), ALU.mult))
                        norm_steps(dve, link, scratch, y, x, centred, squared)

                    @block.scalar
                    def _(act_e):
                        act_e.wait_ge(exp_needed.sem, 1)
                        act_e.activation(rel[:, :], rel[:, :], ACT.Exp).then_inc(exp_ready.sem, 1)
                        norm_squares(act_e, scratch, y, centred, squared)
                stage_end(ln_centred=NG, ln_squared=2 * NG)

        def rgcn_project(src, layer, acc):
            done = ExitStack()
            with done:
                w_all = sb(done, "w_all", [P, (R4 + 1) * D])
                b_b = sb(done, "b_b", [P, D])
                y_out = sb(done, "y_out", [P, G * R4 * D])
                root = sb(done, "root", [P, G * D])

                def load(sp, sig):
                    for r in range(R4):
                        sp.dma_start(w_all[:, r * D:(r + 1) * D], a[f"L3_gnn_W{layer}"][r]).then_inc(sig.sem, 16)
                    sp.dma_start(w_all[:, R4 * D:], a[f"L3_gnn_root{layer}"]).then_inc(sig.sem, 16)
                    sp.dma_start(b_b[:, :], a[f"L3_gnn_b{layer}"].partition_broadcast(P)).then_inc(sig.sem, 16)

                def window(dve, y, j):
                    return dve.tensor_tensor(grouped(root)[:, j, :], y[:, R4 * D:], b_b[:, :], ALU.add)

                def act_window(act_e, y, j):
                    return act_e.copy(grouped(y_out)[:, j, :], y[:, 0:R4 * D])

                def group(dve, g, link):
                    link(dve.tensor_copy(grouped_at(acc, g), grouped(root)))

                def stores(g, lo, hi):
                    return [(rel_table.rearrange("(w p) c -> p w c", p=P)[:, bass.ds(g * G + lo, hi - lo), :],
                             grouped(y_out)[:, lo:hi, :])]
                project(src, w_all, (R4 + 1) * D, load, R4 + 2, stores, window, group, 1,
                        act_window=act_window)

        def rgcn_sums(acc):
            done = ExitStack()
            with done:
                idx = sb(done, "idx", [P, 2 * CB], I32)
                yb = sb(done, "yb", [P, 2 * CB * D])
                idx_ready, issuing = signal("rg_idx"), signal("issuing")
                gathered = (signal("rg_gathered0"), signal("rg_gathered1"))
                yb4 = yb[:, :].rearrange("p (k s c) -> p k s c", k=2, s=CB)
                rows = rel_table.rearrange("n (r c) -> (n r) c", c=D)

                def fill(block, read):
                    @block.gpsimd
                    def _(pool):
                        with pool.Fori(0, NPAIR) as i:
                            for k in range(2):
                                pool.wait_ge(read[k].sem, read[k].at(i * CP))
                                pool.tensor_copy(idx[:, k * CB:(k + 1) * CB], src4_i[:, bass.ds((i * 2 + k) * CB, CB)])\
                                    .then_inc(idx_ready.sem, 1)
                                pool.wait_ge(idx_ready.sem, idx_ready.at(i * 2 + k + 1))
                                pool.sem_inc(issuing.sem, 1)
                                for s in range(CB):
                                    pool.indirect_dma_start(
                                        yb4[:, k, s, :], None, rows,
                                        bass.IndirectOffsetOnAxis(ap=idx[:, k * CB + s:k * CB + s + 1], axis=0))\
                                        .then_inc(gathered[k].sem, 16)
                    return [(gathered, 16 * CB)]
                aggregate(acc, D, lambda k, s: yb4[:, k, s, :], fill, scale=ewn_e, clear=False)
                stage_end(rg_idx=NCH, rg_gathered0=16 * CB * NPAIR, rg_gathered1=16 * CB * NPAIR)

        def on_vector(emit):
            sig = signal("ov_chain")
            counts = {}
            with nc.Block() as block:
                @block.vector
                def _(dve):
                    link = chain(dve, sig)
                    emit(dve, link)
                    counts["n"] = link.count[0]
            stage_end(ov_chain=counts["n"])

        tables()
        if STOP == "T": return finish(nc, ctx, signal, x, out)

        for layer in (1, 2):
            total = ACCW + (D if layer == 1 else 0)
            with ExitStack() as conv:
                alpha = sb(conv, "alpha", [P, SP * H])
                with ExitStack() as scoring:
                    qsplit = sb(scoring, "qsplit", [P, NW * 3 * QW], BF16)
                    conv_project(x, layer, qsplit)
                    conv_scores(qsplit, alpha)
                edge_softmax(alpha, H)
                acc = sb(conv, "acc", [P, NW * total])
                if layer == 1:
                    conv_sums(acc, alpha, True, [(x[:, :], skip_rows)])
                    conv_finish(acc, total, x, layer, residual=False)
                else:
                    y = sb(conv, "y", [P, NW * D])
                    conv_sums(acc, alpha, False, [(y[:, :], skip_rows), (x[:, :], a["x"])])
                    conv_finish(acc, total, y, layer, residual=True)
                    layer_norm(y)
        if STOP == "L0": return finish(nc, ctx, signal, x, out)
        mlp_layer()
        with ExitStack() as rel:
            rel_b = sb(rel, "rel_b", [P, 2 * R16])
            xnm = sb(rel, "xnm", [P, NW * 2 * R16])
            score = sb(rel, "score", [P, SP])
            acc = sb(rel, "acc", [P, NW * R16])
            typed = sb(rel, "typed", [P, SP * R16], BF16)
            with ExitStack() as scoring:
                wrel = sb(scoring, "wrel", [P, 4 * R16])
                dsplit = sb(scoring, "dsplit", [P, NW * 3 * R16], BF16)
                relation_weights(wrel, rel_b)
                relation_project(wrel, rel_b, dsplit, xnm)
                relation_scores(dsplit, score, typed)
            edge_softmax(score, R16)
            relation_sums(acc, score, typed)
            relation_finish(acc, rel_b, xnm)
        with ExitStack() as rgcn:
            acc1 = sb(rgcn, "acc1", [P, NW * D])
            acc2 = sb(rgcn, "acc2", [P, NW * D])
            rgcn_project(x, 1, acc1)
            rgcn_sums(acc1)
            on_vector(lambda dve, link: link(dve.tensor_scalar(acc1[:, :], acc1[:, :], 0.0, None, ALU.max)))
            rgcn_project(acc1, 2, acc2)
            rgcn_sums(acc2)
            on_vector(lambda dve, link: link(dve.tensor_tensor(acc2[:, :], acc2[:, :], x[:, :], ALU.add)))
            layer_norm(acc2)
        finish(nc, ctx, signal, x, out)


def finish(nc, ctx, signal, x, out):
    stored = signal("out_stored")
    full = N // P
    with nc.Block() as block:
        @block.sync
        def _(sp):
            sp.dma_start(out[0:full * P, :].rearrange("(w p) c -> p w c", p=P),
                         x[:, 0:full * D].rearrange("p (w c) -> p w c", c=D)).then_inc(stored.sem, 16)
            sp.dma_start(out[full * P:N, :], x[0:N - full * P, full * D:(full + 1) * D]).then_inc(stored.sem, 16)
            sp.wait_ge(stored.sem, 32)

STOP = None

def kernel(**inputs):
    import concourse.bacc as bacc
    from concourse.bass_utils import run_bass_kernel_spmd

    pad = 2 * NTP * P - E

    def by_tile(v, fill):
        v = np.asarray(v)
        return np.concatenate([v, np.full(pad + 2 * P, fill, v.dtype)]).reshape(2 * NTP + 2, P)

    arrays = {}
    xs = np.zeros((NPAD, D), np.float32)
    xs[:N] = np.asarray(inputs["x"])
    arrays["x"] = np.ascontiguousarray(xs.reshape(NW, P, D).transpose(1, 0, 2)).reshape(P, NW * D)
    dst = np.asarray(inputs["dst"])
    outside = np.full(1, NOWHERE, np.int32)
    ints = {"dst": by_tile(dst, NOWHERE), "before": by_tile(np.concatenate([outside, dst[:-1]]), NOWHERE),
            "after": by_tile(np.concatenate([dst[1:], outside]), NOWHERE), "src": by_tile(inputs["src"], 0),
            "et16": by_tile(inputs["edge_type_16"], 0), "et4": by_tile(inputs["edge_type_4"], 0)}
    arrays["int_rows"] = np.concatenate([ints[n] for n in INT_TABLES], axis=1)
    ew = np.asarray(inputs["edge_weight"])
    arrays["ew_rows"] = np.concatenate([ew, np.repeat(ew[-1:], pad + 2 * P)]).reshape(2 * NTP + 2, P)
    last = np.zeros(TC * P, np.int32)
    last[:NTP] = ints["dst"][1:2 * NTP:2, -1]
    arrays["pair_last"] = np.ascontiguousarray(last.reshape(TC, P).T)
    edge_attr = np.zeros(((2 * NTP + 2) * P, D), np.float32)
    edge_attr[:E] = np.asarray(inputs["edge_attr_128"])
    arrays["edge_attr"] = edge_attr
    number = np.full(TC * P, 4 * SP, np.float32)
    number[:NTP] = np.arange(NTP)
    arrays["c_pair_no"] = np.ascontiguousarray(number.reshape(TC, P).T)
    slot = np.arange(SP)
    arrays["c_step_t"] = (slot // 2).astype(np.float32).reshape(P, SB)
    arrays["c_odd_t"] = (slot % 2).astype(np.float32).reshape(P, SB)
    arrays["c_steps_row"] = np.ascontiguousarray(np.broadcast_to((slot // 2).astype(np.float32), (P, SP)))
    arrays["c_iota_row"] = np.ascontiguousarray(np.broadcast_to(np.arange(P, dtype=np.float32), (P, P)))
    arrays["c_iota_col"] = np.arange(P, dtype=np.float32).reshape(P, 1)
    arrays["c_ident"] = np.eye(P, dtype=np.float32)
    for name, v in inputs.items():
        if name.startswith("L"):
            arrays[name] = np.ascontiguousarray(np.asarray(v))
    arrays["L1_gnn_b1"] = np.ascontiguousarray(arrays["L1_gnn_b1"].reshape(2, D).T)
    arrays["edge_embeddings_t"] = np.ascontiguousarray(arrays.pop("L2_gnn_edge_embeddings").T)
    for k in "sr":
        arrays[f"coef_{k}_t"] = np.ascontiguousarray(arrays.pop(f"L2_gnn_coef_{k}").T)

    nc = bacc.Bacc("TRN2", target_bir_lowering=False, num_devices=1)
    a = {name: nc.dram_tensor(f"in_{name}", v.shape, mybir.dt.from_np(v.dtype), kind="ExternalInput").ap()
         for name, v in arrays.items()}
    out = nc.dram_tensor("out_x", (N, D), F32, kind="ExternalOutput").ap()
    gnn_program(nc, a, out)
    result = run_bass_kernel_spmd(nc, [{f"in_{name}": v for name, v in arrays.items()}], core_ids=[0])
    return result.results[0]["out_x"]
```

```python
from contextlib import ExitStack

import concourse.bass as bass
import numpy as np
from concourse import mybir

F32, BF16, I32 = mybir.dt.float32, mybir.dt.bfloat16, mybir.dt.int32
ALU, ACT, AX = mybir.AluOpType, mybir.ActivationFunctionType, mybir.AxisListType

P = 128
N, E, D = 6250, 100000, 128
H, C = 4, 32
R16, R4, RD, NBASIS = 16, 4, 32, 8
NW = -(-N // P)
NPAD = NW * P
NT = -(-E // P)
NTP = -(-NT // 2)
STEPS = NTP + NW - 1
SLOTS = 2 * STEPS
SB = -(-SLOTS // P)
SP = SB * P
CB = 20
CP = CB // 2
NCH = -(-SLOTS // CB)
NCH += NCH % 2
NPAIR = NCH // 2
assert NCH * CB <= SP and CB % 4 == 0
TC = -(-NTP // P)
RP = 56
RC = 8
LAPS = -(-NTP // RP)
TILES = 2 * RP * LAPS
assert RP % RC == 0 and RP >= NW - 1 + RC and RP * LAPS > NTP and STEPS < NPAIR * 2 * CP + 1
G = 7
NG = NW // G
BIG = 1e30
NOWHERE = 1000000
KC = C + 1
KVW = D + H * KC
QW = H * KC
ACCW = D + 2 * H
EPS = 1e-5
INT_TABLES = ("dst", "before", "after", "src", "et16")


FROM_ONE = ("np_turned", "np_made", "np_xt", "np_added", "np_stored0", "np_stored1", "np_evacuated", "np_kept", "sc_summed0", "sc_summed1", "sc_qe_used", "sc_out0",
            "sc_out1", "sc_st0", "sc_st1", "rs_st0", "rs_st1", "ag_read0", "ag_read1", "ag_added", "cs_pv_made0", "cs_pv_made1", "ml_turned", "ml_hidden",
            "ml_made", "ml_xt", "ml_silued", "ml_added", "ml_normed", "ml_based", "rs_summed0", "rs_summed1", "rs_de_made", "rr_read0", "rr_read1", "rs_kept0", "rs_kept1",
            "rg_stepped")


class Signal:

    def __init__(self, sem, base):
        self.sem, self.base = sem, base

    def at(self, n):
        return self.base + n


def gnn_program(nc, a, out):
    ctx = ExitStack()
    signals = {}
    used = {}

    def signal(name):
        if name not in signals:
            signals[name] = Signal(ctx.enter_context(nc.semaphore(name)), 1 if name in FROM_ONE else 0)
        return signals[name]

    def stage_end(**counts):
        for name, n in counts.items():
            signals[name].base += n

    def dram(name, shape, dt):
        return nc.dram_tensor(name, shape, dt).ap()

    def chain(engine, sig, base=0):
        count = [0]

        def link(ins):
            count[0] += 1
            ins.then_inc(sig.sem, 1)
            engine.wait_ge(sig.sem, sig.at(base + count[0]))
        link.count = count
        return link

    kv_table = dram("kv_table", (NPAD, KVW), F32)
    v_steps = dram("v_steps", (P, NCH * CB * D), F32)
    skip_rows = dram("skip_rows", (P, NW * D), F32)
    agg_rows = dram("agg_rows", (P, NW * D), F32)
    dloc_slots = dram("dloc_slots", (1, SP * P), BF16)
    score_table = dram("score_table", (NPAD, R16), F32)
    type_rows = dram("type_rows", (2, P, SP), F32)
    src16_idx = dram("src16_idx", (P, TILES), I32)
    src4_idx = dram("src4_idx", (P, TILES), I32)
    src_score_rows = dram("src_score_rows", (TILES, P), F32)
    rel_table = dram("rel_table", (NPAD, R4 * D), F32)

    with ctx:
        def sb(stack, name, shape, dt=F32):
            used[name] = used.get(name, 0) + 1
            return stack.enter_context(nc.sbuf_tensor(f"{name}_{used[name]}", shape, dt))

        def pb(stack, name, shape, dt=F32):
            used[name] = used.get(name, 0) + 1
            return stack.enter_context(nc.psum_tensor(f"{name}_{used[name]}", shape, dt))

        x = sb(ctx, "x", [P, NW * D])
        ident = sb(ctx, "ident", [P, P])
        iota_row = sb(ctx, "iota_row", [P, P])
        iota_col = sb(ctx, "iota_col", [P, 1])
        ones = sb(ctx, "ones", [P, P])
        window_of = sb(ctx, "window_of", [1, SP // 2], I32)
        pair_of = sb(ctx, "pair_of", [1, SP // 2], I32)
        place_of = sb(ctx, "place_of", [1, SP // 2], I32)
        dloc_e = sb(ctx, "dloc_e", [P, SP])
        ew_e = sb(ctx, "ew_e", [P, SP])
        src_i = sb(ctx, "src_i", [P, SP], I32)
        tile_t_i = sb(ctx, "tile_t_i", [P, SB], I32)
        ewn_e = sb(ctx, "ewn_e", [P, SP])
        reset_t = sb(ctx, "reset_t", [P, SP])
        close_t = sb(ctx, "close_t", [P, SP])
        cumreset_t = sb(ctx, "cumreset_t", [P, SP])
        cumclose_t = sb(ctx, "cumclose_t", [P, SP])
        amask_t = sb(ctx, "amask_t", [P, SP])

        def tables():
            done = ExitStack()
            with done:
                ones_b = sb(done, "ones_b", [P, P], BF16)
                steps_row = sb(done, "steps_row", [P, SP])
                pair_no = sb(done, "pair_no", [P, TC])
                odd_t = sb(done, "odd_t", [P, SB])
                step_t = sb(done, "step_t", [P, SB])
                last_i = sb(done, "last_i", [P, TC], I32)
                lastw_i = sb(done, "lastw_i", [P, TC], I32)
                last = sb(done, "last", [P, TC])
                cmp = sb(done, "cmp", [P, TC * SP], BF16)
                pair_t = sb(done, "pair_t", [P, SB])
                tile_t = sb(done, "tile_t", [P, SB])
                negw_t = sb(done, "negw_t", [P, SB])
                tile_row = sb(done, "tile_row", [1, SP])
                win_row = sb(done, "win_row", [1, SP])
                packed = sb(done, "packed", [P, SB * 5 * P], I32)
                ew_t = sb(done, "ew_t", [P, SP])
                dl = sb(done, "dl", [P, SP])
                act = sb(done, "act", [P, SP])
                tmp = sb(done, "tmp", [P, SP])
                src_t = sb(done, "src_t", [P, SP])
                dl_b = sb(done, "dl_b", [P, SP], BF16)
                et16_tiles = sb(done, "et16_tiles", [P, TILES], I32)
                src_tiles = sb(done, "src_tiles", [P, TILES], I32)
                et16_e = sb(done, "et16_e", [P, SP])
                et16_t = sb(done, "et16_t", [P, SP])
                src16_tiles = sb(done, "src16_tiles", [P, TILES], I32)
                src4_tiles = sb(done, "src4_tiles", [P, TILES], I32)
                et4_tiles = sb(done, "et4_tiles", [P, TILES], I32)
                place = sb(done, "place", [1, SP // 2])
                lap = sb(done, "lap", [1, SP // 2])
                ext = sb(done, "ext", [P, 2])
                ext2 = sb(done, "ext2", [2, 1])
                ext_d = sb(done, "ext_d", [2, 2])
                ext_b = sb(done, "ext_b", [P, 4])
                ps_row = pb(done, "ps_row", [P, 1024])
                ps_t = pb(done, "ps_t", [P, 512])
                ps_e = pb(done, "ps_e", [P, 2 * 1024])
                loaded, gathered, chained, counted, turned, copied, stored, ext_s = (
                    signal(n) for n in ("tb_loaded", "tb_gathered", "tb_chain", "tb_counted",
                                        "tb_turned", "tb_copied", "tb_stored", "tb_ext"))
                idx_ready = signal("tb_idx_ready")
                cmp_v = cmp[:, :].rearrange("p (c s) -> p c s", c=TC)
                pk = packed[:, :].rearrange("p (b f e) -> p b f e", b=SB, f=5)
                blocked = lambda t: t[:, :].rearrange("p (b e) -> p b e", b=SB)
                to_turn = [(dl, dloc_e), (ew_t, ew_e), (et16_t, et16_e), (src_t, src_i)]
                half = SP // 2
                LAYOUT_T = 150
                with nc.Block() as block:
                    @block.sync
                    def _(sp):
                        for name in FROM_ONE:
                            sp.sem_inc(signal(name).sem, 1)
                        loads = [(x[:, :], a["x"]), (ident[:, :], a["c_ident"]), (iota_row[:, :], a["c_iota_row"]),
                                 (iota_col[:, :], a["c_iota_col"]), (steps_row[:, :], a["c_steps_row"]),
                                 (pair_no[:, :], a["c_pair_no"]), (step_t[:, :], a["c_step_t"]),
                                 (odd_t[:, :], a["c_odd_t"]),
                                 (last_i[:, :], a["pair_last"]), (src_tiles[:, :], a["src_tiles"]),
                                 (et4_tiles[:, :], a["et4_tiles"]), (et16_tiles[:, :], a["et16_tiles"])]
                        for to, of in loads:
                            sp.dma_start(to, of).then_inc(loaded.sem, 16)
                        sp.wait_ge(chained.sem, LAYOUT_T)
                        sp.dma_start(dloc_slots.rearrange("o (p e) -> (o p) e", p=P), dl_b[:, :]).then_inc(stored.sem, 16)
                        sp.dma_start(src16_idx, src16_tiles[:, :]).then_inc(stored.sem, 16)
                        sp.dma_start(src4_idx, src4_tiles[:, :]).then_inc(stored.sem, 16)
                        sp.dma_start(type_rows[1], et16_t[:, :]).then_inc(stored.sem, 16)
                        sp.wait_ge(copied.sem, len(to_turn))
                        sp.dma_start(type_rows[0], et16_e[:, :]).then_inc(stored.sem, 16)
                        sp.wait_ge(stored.sem, 16 * 5)

                    @block.vector
                    def _(dve):
                        link = chain(dve, chained)
                        link(dve.memset(ones[:, :], 1.0))
                        link(dve.memset(ones_b[:, :], 1.0))
                        dve.wait_ge(loaded.sem, 16 * 12)
                        link(dve.scalar_tensor_tensor(src4_tiles[:, :], src_tiles[:, :], float(R4), et4_tiles[:, :],
                                                      ALU.mult, ALU.add))
                        link(dve.scalar_tensor_tensor(src16_tiles[:, :], src_tiles[:, :], float(R16), et16_tiles[:, :],
                                                      ALU.mult, ALU.add))
                        link(dve.tensor_scalar(lastw_i[:, :], last_i[:, :], 7, None, ALU.arith_shift_right))
                        link(dve.tensor_copy(last[:, :], lastw_i[:, :]))
                        link(dve.scalar_tensor_tensor(last[:, :], last[:, :], float(NW - 1), pair_no[:, :], ALU.min, ALU.add))
                        for c in range(TC):
                            dve.tensor_scalar(cmp_v[:, c, :], steps_row[:, :], last[:, c:c + 1], None,
                                              ALU.is_gt).then_inc(counted.sem, 1)
                        dve.wait_ge(turned.sem, 1)
                        link(dve.tensor_copy(pair_t[:, :], ps_t[:, 0:SB]))
                        link(dve.scalar_tensor_tensor(tile_t[:, :], pair_t[:, :], 2.0, odd_t[:, :], ALU.mult, ALU.add))
                        dve.tensor_copy(tile_t_i[:, :], tile_t[:, :]).then_inc(idx_ready.sem, 1)
                        link(dve.tensor_tensor(negw_t[:, :], step_t[:, :], pair_t[:, :], ALU.subtract))
                        link(dve.tensor_scalar(negw_t[:, :], negw_t[:, :], float(NW - 1), -float(P), ALU.min, ALU.mult))
                        for h in range(2):
                            dve.tensor_copy(tile_row[:, h * half:(h + 1) * half], ps_row[0:1, h * 512:h * 512 + half])\
                               .then_inc(chained.sem, 1)
                            link.count[0] += 1
                        dve.wait_ge(chained.sem, link.count[0])
                        link(dve.tensor_copy(pair_of[:, :], tile_row[:, 0::2]))
                        link(dve.tensor_copy(place[:, :], tile_row[:, 0::2]))
                        for n in range(1, LAPS):
                            link(dve.tensor_scalar(lap[:, :], tile_row[:, 0::2], float(n * RP), -float(RP), ALU.is_ge, ALU.mult))
                            link(dve.tensor_tensor(place[:, :], place[:, :], lap[:, :], ALU.add))
                        link(dve.tensor_copy(place_of[:, :], place[:, :]))
                        link(dve.tensor_tensor(win_row[:, :], steps_row[0:1, :], tile_row[:, :], ALU.subtract))
                        link(dve.tensor_scalar(win_row[:, :], win_row[:, :], float(NW - 1), None, ALU.min))
                        link(dve.tensor_copy(window_of[:, :], win_row[:, 0::2]))
                        dve.wait_ge(gathered.sem, 16 * 2 * SB)
                        for b in range(SB):
                            link(dve.tensor_scalar(blocked(dl)[:, b, :], pk[:, b, 0, :], negw_t[:, b:b + 1], None, ALU.add))
                        link(dve.tensor_scalar(tmp[:, :], dl[:, :], 0.0, None, ALU.is_ge))
                        link(dve.scalar_tensor_tensor(act[:, :], dl[:, :], P - 0.5, tmp[:, :], ALU.is_le, ALU.mult))
                        link(dve.tensor_scalar(amask_t[:, :], act[:, :], -1.0, BIG, ALU.add, ALU.mult))
                        for other, flag in ((1, reset_t), (2, close_t)):
                            link(dve.tensor_tensor(blocked(tmp), pk[:, :, 0, :], pk[:, :, other, :], ALU.not_equal))
                            link(dve.scalar_tensor_tensor(flag[:, :], tmp[:, :], -BIG, act[:, :], ALU.mult, ALU.mult))
                        link(dve.memset(tmp[:, :], 0.0))
                        link(dve.tensor_tensor_scan(cumreset_t[:, :], tmp[:, :], reset_t[:, :], 0.0, ALU.add, ALU.add))
                        link(dve.tensor_tensor_scan(cumclose_t[:, ::-1], tmp[:, :], close_t[:, ::-1], 0.0, ALU.add, ALU.add))
                        link(dve.scalar_tensor_tensor(dl[:, :], dl[:, :], 1.0, act[:, :], ALU.add, ALU.mult))
                        link(dve.tensor_scalar(dl[:, :], dl[:, :], -1.0, None, ALU.add))
                        link(dve.tensor_copy(dl_b[:, :], dl[:, :]))
                        link(dve.tensor_copy(blocked(src_t), pk[:, :, 3, :]))
                        link(dve.tensor_copy(blocked(et16_t), pk[:, :, 4, :]))
                        link(dve.tensor_reduce(ext[:, 0:1], ew_t[:, :], AX.X, ALU.max))
                        link(dve.tensor_reduce(ext[:, 1:2], ew_t[:, :], AX.X, ALU.min))
                        link(dve.tensor_scalar(ext[:, 1:2], ext[:, 1:2], -1.0, None, ALU.mult))
                        dve.sem_inc(chained.sem, LAYOUT_T - link.count[0])
                        link.count[0] = LAYOUT_T
                        dve.wait_ge(ext_s.sem, 1)
                        link(dve.tensor_reduce(ext2[:, :], ps_t[0:2, 128:256], AX.X, ALU.max))
                        dve.tensor_scalar(ext_d[:, :], ident[0:2, 0:2], ext2[:, :], None, ALU.mult).then_inc(counted.sem, 1)
                        dve.wait_ge(ext_s.sem, 2)
                        link(dve.tensor_copy(ext_b[:, 0:2], ps_t[:, 256:258]))
                        link(dve.tensor_tensor(ext_b[:, 2:3], ext_b[:, 0:1], ext_b[:, 1:2], ALU.add))
                        link(dve.tensor_scalar(ext_b[:, 2:3], ext_b[:, 2:3], 1e-8, None, ALU.add))
                        link(dve.reciprocal(ext_b[:, 3:4], ext_b[:, 2:3]))
                        dve.wait_ge(copied.sem, 2)
                        link(dve.tensor_scalar(ewn_e[:, :], ew_e[:, :], ext_b[:, 1:2], ext_b[:, 3:4], ALU.add, ALU.mult))

                    @block.tensor
                    def _(pe):
                        pe.wait_ge(counted.sem, TC)
                        for h in range(2):
                            for c in range(TC):
                                pe.matmul(ps_row[:, h * 512:h * 512 + half], ones_b[:, :],
                                          cmp_v[:, c, h * half:(h + 1) * half], start=(c == 0), stop=(c == TC - 1))
                        for b in range(SB):
                            for c in range(TC):
                                last_mm = pe.matmul(ps_t[:, b:b + 1], cmp_v[:, c, b::SB], ones_b[:, 0:1],
                                                    start=(c == 0), stop=(c == TC - 1))
                        last_mm.then_inc(turned.sem, 1)
                        pe.wait_ge(chained.sem, LAYOUT_T)
                        pe.transpose(ps_t[0:2, 128:256], ext[:, :], ident[:, :]).then_inc(ext_s.sem, 1)
                        pe.wait_ge(counted.sem, TC + 1)
                        pe.matmul(ps_t[:, 256:258], ones[0:2, :], ext_d[:, :], start=True, stop=True).then_inc(ext_s.sem, 1)
                        for n, (of, _) in enumerate(to_turn):
                            if n >= 2:
                                pe.wait_ge(copied.sem, n - 1)
                            for b in range(SB):
                                at = n % 2 * 1024 + b * P
                                last_mm = pe.transpose(ps_e[:, at:at + P], blocked(of)[:, b, :], ident[:, :])
                            last_mm.then_inc(turned.sem, 1)

                    @block.scalar
                    def _(act_e):
                        for n, (_, to) in enumerate(to_turn):
                            act_e.wait_ge(turned.sem, n + 2)
                            at = n % 2 * 1024
                            act_e.copy(to[:, :].rearrange("e (p b) -> e b p", b=SB),
                                       ps_e[:, at:at + SP].rearrange("e (b p) -> e b p", b=SB)).then_inc(copied.sem, 1)

                    @block.gpsimd
                    def _(pool):
                        pool.wait_ge(idx_ready.sem, 1)
                        for b in range(SB):
                            at = bass.IndirectOffsetOnAxis(ap=tile_t_i[:, b:b + 1], axis=0)
                            pool.indirect_dma_start(pk[:, b, :, :].rearrange("p f e -> p (f e)"), None,
                                                    a["int_rows"], at).then_inc(gathered.sem, 16)
                            pool.indirect_dma_start(blocked(ew_t)[:, b, :], None, a["ew_rows"], at)\
                                .then_inc(gathered.sem, 16)

        def project(src, w_all, cols, load, n_loads, stores, window, group, n_links, first=None,
                    act_window=None, keep=None, relu=False):
            done = ExitStack()
            with done:
                slots = 4 if cols <= 512 else 2
                wide = 2048 // slots
                xg = sb(done, "xg", [P, G * D])
                xt = sb(done, "xt", [P, G * D])
                ps_x = pb(done, "ps_x", [P, 1024])
                ps_y = pb(done, "ps_y", [P, 2048])
                loaded, got, turned, xt_ready, made, added, chained = (
                    signal(n) for n in ("np_loaded", "np_got", "np_turned", "np_xt", "np_made",
                                        "np_added", "np_chain"))
                evacuated, kept, issuing = signal("np_evacuated"), signal("np_kept"), signal("issuing")
                HALVES = ((0, 4), (4, G))
                starts = [lo for lo, _ in HALVES]
                stored = (signal("np_stored0"), signal("np_stored1"))
                results = signal("np_results")
                n_stores = len(stores(0, 0, 1))
                pre = [0]
                with nc.Block() as block:
                    @block.sync
                    def _(sp):
                        load(sp, loaded)
                        with sp.Fori(0, NG) as g:
                            for (lo, hi), sig in zip(HALVES, stored):
                                sp.wait_ge(added.sem, added.at(g * G + hi))
                                sp.sem_inc(issuing.sem, 1)
                                if act_window:
                                    sp.wait_ge(evacuated.sem, evacuated.at(g * G + hi))
                                    sp.sem_inc(issuing.sem, 1)
                                for to, of in stores(g, lo, hi):
                                    sp.dma_start(to, of).then_inc(sig.sem, 16)
                        for sig in stored:
                            sp.wait_ge(sig.sem, sig.at(NG * 16 * n_stores))

                    @block.scalar
                    def _(act_e):
                        def take(g):
                            act_e.wait_ge(turned.sem, turned.at(g + 1))
                            act_e.wait_ge(made.sem, made.at(g * G))
                            act_e.activation(xt[:, :], ps_x[:, 0:G * D], ACT.Relu if relu else ACT.Copy).then_inc(xt_ready.sem, 1)
                            if act_window:
                                for j in range(G):
                                    if j in starts:
                                        sig = stored[starts.index(j)]
                                        act_e.wait_ge(sig.sem, sig.at(g * (16 * n_stores)))
                                    act_e.wait_ge(made.sem, made.at(g * G + j + 1))
                                    at = j % slots * wide
                                    act_window(act_e, ps_y[:, at:at + cols], j).then_inc(evacuated.sem, 1)

                        def store_results(g):
                            if keep:
                                act_e.wait_ge(results.sem, results.at(g + 1))
                                keep(act_e, g).then_inc(kept.sem, 1)
                        take(0)
                        with act_e.Fori(1, NG) as g:
                            take(g)
                            store_results(g - 1)
                        store_results(NG - 1)

                    @block.gpsimd
                    def _(pool):
                        with pool.Fori(0, NG) as g:
                            pool.wait_ge(turned.sem, turned.at(g))
                            pool.tensor_copy(xg[:, :], src[:, bass.ds(g * (G * D), G * D)]).then_inc(got.sem, 1)

                    @block.tensor
                    def _(pe):
                        pe.wait_ge(loaded.sem, loaded.at(16 * n_loads))
                        with pe.Fori(0, NG) as g:
                            pe.wait_ge(got.sem, got.at(g + 1))
                            pe.wait_ge(xt_ready.sem, xt_ready.at(g))
                            for j in range(G):
                                last_mm = pe.transpose(ps_x[:, j * D:(j + 1) * D], xg[:, j * D:(j + 1) * D], ident[:, :])
                            last_mm.then_inc(turned.sem, 1)
                            pe.wait_ge(xt_ready.sem, xt_ready.at(g + 1))
                            for j in range(G):
                                pe.wait_ge(added.sem, added.at(g * G + max(j - slots + 1, 0)))
                                if act_window:
                                    pe.wait_ge(evacuated.sem, evacuated.at(g * G + max(j - slots + 1, 0)))
                                for c in range(0, cols, 512):
                                    n = min(512, cols - c)
                                    at = j % slots * wide + c
                                    last_mm = pe.matmul(ps_y[:, at:at + n], xt[:, j * D:(j + 1) * D], w_all[:, c:c + n],
                                                        start=True, stop=True)
                                last_mm.then_inc(made.sem, 1)

                    @block.vector
                    def _(dve):
                        dve.wait_ge(loaded.sem, loaded.at(16 * n_loads))
                        if first:
                            link = chain(dve, chained)
                            first(dve, link)
                            pre[0] = link.count[0]
                        with dve.Fori(0, NG) as g:
                            for j in range(G):
                                if j in starts:
                                    sig = stored[starts.index(j)]
                                    dve.wait_ge(sig.sem, sig.at(g * (16 * n_stores)))
                                dve.wait_ge(made.sem, made.at(g * G + j + 1))
                                at = j % slots * wide
                                window(dve, ps_y[:, at:at + cols], j).then_inc(added.sem, 1)
                            dve.wait_ge(added.sem, added.at((g + 1) * G))
                            if group:
                                if keep:
                                    dve.wait_ge(kept.sem, kept.at(g))
                                link = chain(dve, chained, g * n_links + pre[0])
                                group(dve, g, link)
                                assert link.count[0] == n_links
                                dve.sem_inc(results.sem, 1)
                stage_end(np_evacuated=NW if act_window else 0, np_results=NG if group else 0, np_kept=NG if keep else 0,
                          np_loaded=16 * n_loads, np_got=NG, np_turned=NG, np_xt=NG, np_made=NW, np_added=NW,
                          np_stored0=16 * n_stores * NG, np_stored1=16 * n_stores * NG, np_chain=pre[0] + n_links * NG)

        def split3(dve, link, value, rest, parts):
            p3 = parts[:, :].rearrange("p (k g c) -> p k g c", k=3, g=G)
            link(dve.tensor_copy(p3[:, 0], grouped(value)))
            link(dve.tensor_tensor(grouped(rest), grouped(value), p3[:, 0], ALU.subtract))
            link(dve.tensor_copy(p3[:, 1], grouped(rest)))
            link(dve.tensor_tensor(p3[:, 2], grouped(rest), p3[:, 1], ALU.subtract))

        def grouped(t):
            return t[:, :].rearrange("p (g c) -> p g c", g=G)

        def in_heads(ap):
            return ap.rearrange("p (h c) -> p h c", h=H)

        def conv_project(src, layer, qsplit):
            done = ExitStack()
            with done:
                w_all = sb(done, "w_all", [P, 4 * D])
                b_all = sb(done, "b_all", [P, 4 * D])
                we_b = sb(done, "we_b", [P, D])
                kv_out = sb(done, "kv_out", [P, G * KVW])
                sq_out = sb(done, "sq_out", [P, G * 2 * D])
                qx = sb(done, "qx", [P, G * QW])
                rest = sb(done, "rest", [P, G * QW])
                parts = sb(done, "parts", [P, 3 * G * QW], BF16)
                tmp = sb(done, "tmp", [P, G * D])
                kv3, sq3 = grouped(kv_out), grouped(sq_out)
                qx4 = qx[:, :].rearrange("p (g h c) -> p g h c", g=G, h=H)
                tmp4 = tmp[:, :].rearrange("p (g h c) -> p g h c", g=G, h=H)
                q3 = qsplit[:, :].rearrange("p (w k c) -> p w k c", k=3, c=QW)

                def load(sp, sig):
                    for n, k in enumerate(("v", "s", "q", "k")):
                        sp.dma_start(w_all[:, n * D:(n + 1) * D], a[f"L0_gnn_W{k}{layer}"]).then_inc(sig.sem, 16)
                        sp.dma_start(b_all[:, n * D:(n + 1) * D],
                                     a[f"L0_gnn_b{k}{layer}"].partition_broadcast(P)).then_inc(sig.sem, 16)
                    sp.dma_start(we_b[:, :], a[f"L0_gnn_We{layer}"][0, :].partition_broadcast(P)).then_inc(sig.sem, 16)

                def first(dve, link):
                    link(dve.memset(kv_out[:, :], 0.0))

                def window(dve, y, j):
                    dve.tensor_tensor(kv3[:, j, 0:D], y[:, 0:D], b_all[:, 0:D], ALU.add)
                    dve.tensor_tensor(sq3[:, j, :], y[:, D:3 * D], b_all[:, D:3 * D], ALU.add)
                    return dve.tensor_tensor(in_heads(kv3[:, j, D:KVW])[:, :, 0:C], in_heads(y[:, 3 * D:4 * D]),
                                             in_heads(b_all[:, 3 * D:4 * D]), ALU.add)

                def group(dve, g, link):
                    link(dve.tensor_scalar(qx4[:, :, :, 0:C], sq3[:, :, D:2 * D].rearrange("p g (h c) -> p g h c", h=H),
                                           float(C) ** -0.5, None, ALU.mult))
                    link(dve.tensor_tensor(tmp4, qx4[:, :, :, 0:C],
                                           in_heads(we_b[:, :]).unsqueeze(1).to_broadcast([P, G, H, C]), ALU.mult))
                    link(dve.tensor_reduce(qx4[:, :, :, C], tmp4, AX.X, ALU.add))
                    split3(dve, link, qx, rest, parts)

                def keep(act_e, g):
                    return act_e.copy(q3[:, bass.ds(g * G, G), :, :],
                                            parts[:, :].rearrange("p (k g c) -> p g k c", k=3, g=G))

                def stores(g, lo, hi):
                    return [(kv_table.rearrange("(w p) c -> p w c", p=P)[:, bass.ds(g * G + lo, hi - lo), :], kv3[:, lo:hi, :]),
                            (skip_rows.rearrange("p (w c) -> p w c", c=D)[:, bass.ds(g * G + lo, hi - lo), :],
                             sq3[:, lo:hi, 0:D])]
                project(src, w_all, 4 * D, load, 9, stores, window, group, 7, first, keep=keep)

        def conv_scores(qsplit, alpha):
            done = ExitStack()
            with done:
                kv = sb(done, "kv", [P, 2 * CB * KVW])
                idx = sb(done, "idx", [P, 2 * CB], I32)
                dl_row = sb(done, "dl_row", [P, 2 * CB * P], BF16)
                st = sb(done, "st", [P, 2 * CB * P], BF16)
                prod = sb(done, "prod", [P, CB * QW])
                ps_q = pb(done, "ps_q", [P, 2 * 1024])
                idx_ready, ew_in, qe_made, qe_used = (
                    signal(n) for n in ("sc_idx", "sc_ew_in", "sc_qe_made", "sc_qe_used"))
                st_made = (signal("sc_st0"), signal("sc_st1"))
                issuing = signal("issuing")
                values_out = (signal("sc_out0"), signal("sc_out1"))
                gathered, dl_in, spilled, summed = (
                    (signal(n + "0"), signal(n + "1")) for n in ("sc_gathered", "sc_dl_in", "sc_spilled", "sc_summed"))
                kv4 = kv[:, :].rearrange("p (k s c) -> p k s c", k=2, s=CB)
                st4 = st[:, :].rearrange("p (k s e) -> p k s e", k=2, s=CB)
                dl3 = dl_row[:, :].rearrange("p (k n) -> p k n", k=2)
                prod3 = prod[:, :].rearrange("p (s c) -> p s c", s=CB)
                ps4 = ps_q[:, :].rearrange("p (b s c) -> p b s c", b=2, s=4)
                al3 = alpha[:, :].rearrange("p (s h) -> p s h", h=H)
                q_of = lambda w, part: qsplit[:, bass.ds(w * (3 * QW) + part * QW, QW)]
                GQ = CB // 4
                with nc.Block() as block:
                    @block.gpsimd
                    def _(pool):
                        with pool.Fori(0, NPAIR) as i:
                            for k in range(2):
                                pool.wait_ge(summed[k].sem, summed[k].at(i))
                                pool.wait_ge(values_out[k].sem, values_out[k].at(i))
                                pool.tensor_copy(idx[:, k * CB:(k + 1) * CB], src_i[:, bass.ds((i * 2 + k) * CB, CB)])\
                                    .then_inc(idx_ready.sem, 1)
                                pool.wait_ge(idx_ready.sem, idx_ready.at(i * 2 + k + 1))
                                pool.sem_inc(issuing.sem, 1)
                                for s in range(CB):
                                    pool.indirect_dma_start(
                                        kv4[:, k, s, :], None, kv_table,
                                        bass.IndirectOffsetOnAxis(ap=idx[:, k * CB + s:k * CB + s + 1], axis=0))\
                                        .then_inc(gathered[k].sem, 16)

                    @block.sync
                    def _(sp):
                        with sp.Fori(0, NPAIR) as i:
                            for k in range(2):
                                sp.wait_ge(gathered[k].sem, gathered[k].at((i + 1) * (16 * CB)))
                                sp.dma_start(v_steps.rearrange("p (s c) -> p s c", c=D)[:, bass.ds((i * 2 + k) * CB, CB), :],
                                             kv4[:, k, :, 0:D]).then_inc(spilled[k].sem, 16)
                                sp.wait_ge(spilled[k].sem, spilled[k].at((i + 1) * 16))
                                sp.sem_inc(values_out[k].sem, 1)

                    @block.scalar
                    def _(act_e):
                        with act_e.Fori(0, NPAIR) as i:
                            for k in range(2):
                                act_e.wait_ge(st_made[k].sem, st_made[k].at(i))
                                act_e.dma_start(dl3[:, k, :], dloc_slots[0, bass.ds((i * 2 + k) * (CB * P), CB * P)]
                                                .partition_broadcast(P)).then_inc(dl_in[k].sem, 16)
                            for k in range(2):
                                act_e.wait_ge(gathered[k].sem, gathered[k].at((i + 1) * (16 * CB)))
                                act_e.copy(kv4[:, k, :, D:KVW].rearrange("p s (h c) -> p s h c", h=H)[:, :, :, C],
                                           ew_e[:, bass.ds((i * 2 + k) * CB, CB)].unsqueeze(2).to_broadcast([P, CB, H]))\
                                    .then_inc(ew_in.sem, 1)

                    @block.tensor
                    def _(pe):
                        with pe.Fori(0, NPAIR) as i:
                            for k in range(2):
                                pe.wait_ge(st_made[k].sem, st_made[k].at(i + 1))
                                _, ws = nc.values_load_multi_w_load_instructions(
                                    window_of[0:1, bass.ds((i * 2 + k) * CP, CP)],
                                    engines=(mybir.EngineType.PE,), min_val=0, max_val=NW - 1)
                                for q in range(GQ):
                                    n = 2 * GQ * i + k * GQ + q
                                    if k * GQ + q >= 2:
                                        pe.wait_ge(qe_used.sem, qe_used.at(n - 1))
                                    else:
                                        pe.wait_ge(qe_used.sem, qe_used.at(2 * GQ * i))
                                    for s in range(4):
                                        for part in range(3):
                                            last_mm = pe.matmul(ps4[:, (k * GQ + q) % 2, s, 0:QW], st4[:, k, q * 4 + s, :],
                                                                q_of(ws[(q * 4 + s) // 2], part), start=(part == 0), stop=(part == 2))
                                    last_mm.then_inc(qe_made.sem, 1)

                    @block.vector
                    def _(dve):
                        dve.memset(alpha[:, NCH * CB * H:], 0.0)
                        with dve.Fori(0, NPAIR) as i:
                            for k in range(2):
                                dve.wait_ge(dl_in[k].sem, dl_in[k].at((i + 1) * 16))
                                dve.wait_ge(qe_used.sem, qe_used.at(2 * GQ * i))
                                dve.tensor_scalar(st4[:, k].rearrange("p s e -> p (s e)"), dl3[:, k, :], iota_col[:, :],
                                                  None, ALU.is_equal).then_inc(st_made[k].sem, 1)
                                dve.wait_ge(ew_in.sem, ew_in.at(i * 2 + k + 1))
                                dve.wait_ge(summed[1 - k].sem, summed[1 - k].at(i + k))
                                for q in range(GQ):
                                    dve.wait_ge(qe_made.sem, qe_made.at(2 * GQ * i + k * GQ + q + 1))
                                    dve.tensor_tensor(prod3[:, q * 4:q * 4 + 4, :], ps4[:, (k * GQ + q) % 2, :, 0:QW],
                                                      kv4[:, k, q * 4:q * 4 + 4, D:KVW], ALU.mult).then_inc(qe_used.sem, 1)
                                dve.wait_ge(qe_used.sem, qe_used.at(2 * GQ * i + (k + 1) * GQ))
                                dve.tensor_reduce(al3[:, bass.ds((i * 2 + k) * CB, CB), :],
                                                  prod3.rearrange("p s (h c) -> p s h c", h=H),
                                                  AX.X, ALU.add).then_inc(summed[k].sem, 1)
                stage_end(sc_idx=NCH, sc_gathered0=16 * CB * NPAIR, sc_gathered1=16 * CB * NPAIR, sc_ew_in=NCH,
                          sc_dl_in0=16 * NPAIR, sc_dl_in1=16 * NPAIR, sc_st0=NPAIR, sc_st1=NPAIR, sc_qe_made=NCH * GQ,
                          sc_qe_used=NCH * GQ, sc_summed0=NPAIR, sc_summed1=NPAIR, sc_out0=NPAIR, sc_out1=NPAIR, sc_spilled0=16 * NPAIR, sc_spilled1=16 * NPAIR)

        def edge_softmax(score, lanes, more_t=None, et16_t=None):
            done = ExitStack()
            by_relation = lanes == R16
            heads = 1 if by_relation else H
            with done:
                a_t = sb(done, "a_t", [P, heads * SP])
                f_t = sb(done, "f_t", [P, lanes * SP])
                U = 4
                first_t = [sb(done, "first_t", [P, SP]) for _ in range(U)]
                second_t = [sb(done, "second_t", [P, SP]) for _ in range(U)]
                m_t = sb(done, "m_t", [P, SP])
                ends = sb(done, "ends", [P, lanes])
                totals = sb(done, "totals", [P, lanes])
                ends_r = sb(done, "ends_r", [lanes, P])
                tot_r = sb(done, "tot_r", [lanes, P])
                carry_r = sb(done, "carry_r", [lanes, P + 1])
                carry = sb(done, "carry", [P, lanes])
                ps_a = pb(done, "ps_a", [P, 2 * 1024])
                ps_c = pb(done, "ps_c", [P, 512])
                turned_in, taken, chained, turned, out_turned, out_copied, weighed = (
                    signal(n) for n in ("sm_turned_in", "sm_taken", "sm_chain", "sm_turned", "sm_out_turned",
                                        "sm_out_copied", "sm_weighed"))
                ready = signal("sm_ready")
                s3 = score[:, :].rearrange("e (s h) -> e s h", h=heads)
                a3 = a_t[:, :].rearrange("p (h s) -> p h s", h=heads)
                lane_of = lambda t, r: t[:, bass.ds(r * SP, SP)]
                with nc.Block() as block:
                    @block.tensor
                    def _(pe):
                        for h in range(heads):
                            if h >= 2:
                                pe.wait_ge(taken.sem, taken.at(h - 1))
                            for b in range(SB):
                                at = h % 2 * 1024 + b * P
                                last_mm = pe.transpose(ps_a[:, at:at + P], s3[:, b::SB, h], ident[:, :])
                            last_mm.then_inc(turned_in.sem, 1)
                        for back in range(2):
                            pe.wait_ge(ready.sem, ready.at(2 * back + 1))
                            pe.transpose(ps_c[0:lanes, 0:P], ends[:, :], ident[:, :])
                            pe.transpose(ps_c[0:lanes, P:2 * P], totals[:, :], ident[:, :]).then_inc(turned.sem, 1)
                            pe.wait_ge(ready.sem, ready.at(2 * back + 2))
                            lo = 1 if back else 0
                            pe.transpose(ps_c[:, 2 * P:2 * P + lanes], carry_r[:, lo:lo + P], ident[0:lanes, 0:lanes])\
                              .then_inc(turned.sem, 1)
                        for h in range(heads):
                            pe.wait_ge(weighed.sem, weighed.at(h + 1))
                            if h >= 2:
                                pe.wait_ge(out_copied.sem, out_copied.at(h - 1))
                            for b in range(SB):
                                at = h % 2 * 1024 + b * P
                                last_mm = pe.transpose(ps_a[:, at:at + P], a3[:, h, b * P:(b + 1) * P], ident[:, :])
                            last_mm.then_inc(out_turned.sem, 1)

                    @block.vector
                    def _(dve):
                        count = [0]

                        def link(ins):
                            count[0] += 1
                            ins.then_inc(chained.sem, 1)
                            dve.wait_ge(chained.sem, chained.at(count[0]))

                        def lane_loop(per_lane, body, serial=False):
                            start = count[0]
                            with dve.Fori(0, lanes // U) as i:
                                to_do = [body(i * U + u, u) for u in range(U)]
                                issued = 0
                                for j in range(per_lane):
                                    for u in range(U):
                                        needs = issued if serial and j == per_lane - 1 else issued - U + 1
                                        if needs > 0:
                                            dve.wait_ge(chained.sem, chained.at(i * (per_lane * U) + (start + needs)))
                                        to_do[u][j]().then_inc(chained.sem, 1)
                                        issued += 1
                                dve.wait_ge(chained.sem, chained.at(i * (per_lane * U) + (start + issued)))
                            count[0] = start + per_lane * lanes

                        for h in range(heads):
                            dve.wait_ge(turned_in.sem, turned_in.at(h + 1))
                            dve.tensor_tensor(a3[:, h, :], ps_a[:, h % 2 * 1024:h % 2 * 1024 + SP], amask_t[:, :], ALU.add)\
                               .then_inc(taken.sem, 1)
                        dve.wait_ge(taken.sem, taken.at(heads))
                        if more_t:
                            link(dve.tensor_tensor(a_t[:, :], a_t[:, :], more_t[:, :], ALU.add))

                        def forward(r, u):
                            of = []
                            if not by_relation:
                                scores = lane_of(a_t, r)
                            else:
                                far, scores = first_t[u][:, :], second_t[u][:, :]
                                of = [lambda: dve.tensor_scalar(far, et16_t[:, :], iota_row[:, bass.ds(r, 1)], -BIG,
                                                                ALU.not_equal, ALU.mult),
                                      lambda: dve.tensor_tensor(scores, far, a_t[:, :], ALU.add)]
                            return of + [lambda: dve.tensor_tensor_scan(lane_of(f_t, r), reset_t[:, :], scores, -BIG,
                                                                        ALU.add, ALU.max)]
                        lane_loop(3 if by_relation else 1, forward)

                        def carries(back, cum):
                            f3 = f_t[:, :].rearrange("p (l s) -> p l s", l=lanes)
                            edge = 0 if back else SP - 1
                            link(dve.tensor_copy(ends[:, :], f3[:, :, edge]))
                            link(dve.tensor_copy(totals[:, :], cum[:, edge:edge + 1].to_broadcast([P, lanes])))
                            dve.sem_inc(ready.sem, 1)
                            dve.wait_ge(turned.sem, turned.at(2 * back + 1))
                            link(dve.tensor_copy(ends_r[:, :], ps_c[0:lanes, 0:P]))
                            link(dve.tensor_copy(tot_r[:, :], ps_c[0:lanes, P:2 * P]))
                            link(dve.memset(carry_r[:, :], -BIG))
                            if back:
                                link(dve.tensor_tensor_scan(carry_r[:, 0:P][:, ::-1], tot_r[:, ::-1], ends_r[:, ::-1], -BIG,
                                                            ALU.add, ALU.max))
                            else:
                                link(dve.tensor_tensor_scan(carry_r[:, 1:P + 1], tot_r[:, :], ends_r[:, :], -BIG,
                                                            ALU.add, ALU.max))
                            dve.sem_inc(ready.sem, 1)
                            dve.wait_ge(turned.sem, turned.at(2 * back + 2))
                            link(dve.tensor_copy(carry[:, :], ps_c[:, 2 * P:2 * P + lanes]))

                        carries(0, cumreset_t)

                        def backward(r, u):
                            f, whole, back = lane_of(f_t, r), first_t[u], second_t[u]
                            return [lambda: dve.scalar_tensor_tensor(whole[:, :], cumreset_t[:, :], carry[:, bass.ds(r, 1)], f,
                                                                     ALU.add, ALU.max),
                                    lambda: dve.tensor_tensor_scan(back[:, ::-1], close_t[:, ::-1], whole[:, ::-1], -BIG,
                                                                   ALU.add, ALU.max),
                                    lambda: dve.tensor_scalar(f, back[:, :], 0.0, None, ALU.add)]
                        lane_loop(3, backward)
                        carries(1, cumclose_t)

                        def maxima(r):
                            f = lane_of(f_t, r)
                            return lambda: dve.scalar_tensor_tensor(f, cumclose_t[:, :], carry[:, bass.ds(r, 1)], f,
                                                                    ALU.add, ALU.max)
                        if by_relation:
                            link(dve.memset(m_t[:, :], 0.0))

                            def pick(r, u):
                                own = first_t[u][:, :]
                                return [maxima(r),
                                        lambda: dve.scalar_tensor_tensor(own, et16_t[:, :], iota_row[:, bass.ds(r, 1)],
                                                                         lane_of(f_t, r), ALU.is_equal, ALU.mult),
                                        lambda: dve.tensor_tensor(m_t[:, :], m_t[:, :], own, ALU.add)]
                            lane_loop(3, pick, serial=True)
                            link(dve.tensor_tensor(a_t[:, :], a_t[:, :], m_t[:, :], ALU.subtract))
                        else:
                            def subtract(r, u):
                                return [maxima(r),
                                        lambda: dve.tensor_tensor(lane_of(a_t, r), lane_of(a_t, r), lane_of(f_t, r), ALU.subtract)]
                            lane_loop(2, subtract)
                        link(dve.tensor_scalar(a_t[:, :], a_t[:, :], 0.0, None, ALU.min))
                        dve.sem_inc(ready.sem, 1)
                        edge_softmax.linked = count[0]

                    @block.scalar
                    def _(act_e):
                        act_e.wait_ge(ready.sem, ready.at(5))
                        for h in range(heads):
                            act_e.activation(a3[:, h, :], a3[:, h, :], ACT.Exp).then_inc(weighed.sem, 1)
                        for h in range(heads):
                            act_e.wait_ge(out_turned.sem, out_turned.at(h + 1))
                            act_e.copy(s3.rearrange("e (p b) h -> e b p h", b=SB)[:, :, :, h],
                                       ps_a[:, h % 2 * 1024:h % 2 * 1024 + SP].rearrange("e (b p) -> e b p", b=SB))\
                                 .then_inc(out_copied.sem, 1)
                stage_end(sm_turned_in=heads, sm_taken=heads, sm_chain=edge_softmax.linked, sm_turned=4,
                          sm_out_turned=heads, sm_out_copied=heads, sm_weighed=heads, sm_ready=5)

        def aggregate(acc, width, rhs, fill, scale=None, extra=None, extra_width=0, clear=True, ring=None, shared=None):
            done = ExitStack()
            with done:
                RING, AHEAD = 4, 3
                BANKS = 8
                LC = 4
                LS = LC * CP
                OWN = (0, 3, 6, 9) if shared else tuple(range(CP))
                given = [m for m in range(CP) if m not in OWN]
                assert LC * len(OWN) % RING == 0 and LS % BANKS == 0 and NCH % LC == 0
                lent = sb(done, "lent", [P, 2 * len(given) * 2 * P]) if given else None
                lent5 = lent[:, :].rearrange("p (k m j n) -> p k m j n", k=2, m=len(given), j=2) if given else None
                onehot = sb(done, "onehot", [P, RING * 2 * P])
                ps_s = pb(done, "ps_s", [P, BANKS * 512])
                hot, added, cleared = signal("ag_hot"), signal("ag_added"), signal("ag_cleared")
                read = (signal("ag_read0"), signal("ag_read1"))
                total = width + extra_width
                lent_ready = (signal("ag_lent0"), signal("ag_lent1"))
                lent_chain = signal("ag_lent_chain")
                one = lambda m, j: onehot[:, (m % RING * 2 + j) * P:(m % RING * 2 + j + 1) * P]

                def step_of(q):
                    return q // len(OWN) * CP + OWN[q % len(OWN)]
                if ring:
                    ring_rows, pairs_in, stepped = ring

                def wait_step(engine, i, n):
                    if ring:
                        engine.wait_ge(stepped.sem, stepped.at(i * LS + n + 1))
                    elif n < 0:
                        engine.wait_ge(read[1].sem, read[1].at(i * (LS // 2)))
                    else:
                        c, k = divmod(n // CP, 2)
                        engine.wait_ge(read[k].sem, read[k].at(i * (LS // 2) + c * CP + n % CP + 1))

                def taken(n):
                    return stepped if ring else read[n // CP % 2]
                with nc.Block() as block:
                    filled = fill(block, read)

                    @block.tensor
                    def _(pe):
                        with pe.Fori(0, NCH // LC) as i:
                            for n in range(LS):
                                c, m = divmod(n, CP)
                                c, k = divmod(c, 2)
                                if m == 0:
                                    for sig, per in filled:
                                        pe.wait_ge(sig[k].sem, sig[k].at(i * (LC // 2 * per) + (c + 1) * per))
                                    if ring:
                                        _, ts = nc.values_load_multi_w_load_instructions(
                                            pair_of[0:1, bass.ds(i * LS + n, CP)],
                                            engines=(mybir.EngineType.PE,), min_val=0, max_val=NTP)
                                        _, places = nc.values_load_multi_w_load_instructions(
                                            place_of[0:1, bass.ds(i * LS + n, CP)],
                                            engines=(mybir.EngineType.PE,), min_val=0, max_val=RP - 1)
                                if ring:
                                    pe.wait_ge(pairs_in.sem, pairs_in.at(ts[m] + 1))
                                if m in OWN:
                                    q = n // CP * len(OWN) + OWN.index(m)
                                    pe.wait_ge(hot.sem, hot.at(i * (LC * len(OWN)) + q + 1))
                                    hots = [one(q, j) for j in range(2)]
                                else:
                                    pe.wait_ge(lent_ready[k].sem, lent_ready[k].at(i * (LC // 2) + c + 1))
                                    hots = [lent5[:, k, given.index(m), j, :] for j in range(2)]
                                pe.wait_ge(added.sem, added.at(i * LS + max(n - BANKS + 1, 0)))
                                to = ps_s[:, n % BANKS * 512:n % BANKS * 512 + total]
                                if extra:
                                    for j in range(2):
                                        pe.matmul(to[:, width:total], hots[j], extra(k, 2 * m + j),
                                                  start=(j == 0), stop=(j == 1))
                                for j in range(2):
                                    rows = ring_rows(places[m], j) if ring else rhs(k, 2 * m + j)
                                    last_mm = pe.matmul(to[:, 0:width], hots[j], rows, start=(j == 0), stop=(j == 1))
                                last_mm.then_inc(taken(n).sem, 1)

                    @block.vector
                    def _(dve):
                        def make_onehots(i, q):
                            for j in range(2):
                                cell = bass.ds(i * (2 * LS) + step_of(q) * 2 + j, 1)
                                if scale is None:
                                    last = dve.tensor_scalar(one(q, j), iota_row[:, :], dloc_e[:, cell], None, ALU.is_equal)
                                else:
                                    last = dve.tensor_scalar(one(q, j), iota_row[:, :], dloc_e[:, cell], scale[:, cell],
                                                             ALU.is_equal, ALU.mult)
                            last.then_inc(hot.sem, 1)
                        for q in range(AHEAD):
                            make_onehots(0, q)
                        if clear:
                            dve.memset(acc[:, :], 0.0).then_inc(cleared.sem, 1)
                            dve.wait_ge(cleared.sem, cleared.at(1))
                        with dve.Fori(0, NCH // LC) as i:
                            for n in range(LS):
                                m = n % CP
                                if m == 0:
                                    _, ws = nc.values_load_multi_w_load_instructions(
                                        window_of[0:1, bass.ds(i * LS + n, CP)],
                                        engines=(mybir.EngineType.DVE,), min_val=0, max_val=NW - 1)
                                if m in OWN:
                                    q = n // CP * len(OWN) + OWN.index(m)
                                    wait_step(dve, i, step_of(q - 1))
                                    make_onehots(i, q + AHEAD)
                                wait_step(dve, i, n)
                                dve.wait_ge(added.sem, added.at(i * LS + n))
                                at = acc[:, bass.ds(ws[m] * total, total)]
                                dve.tensor_tensor(at, at, ps_s[:, n % BANKS * 512:n % BANKS * 512 + total], ALU.add)\
                                   .then_inc(added.sem, 1)

                    if shared:
                        @block.scalar
                        def _(act_e):
                            first, last = shared
                            first(act_e)
                            with act_e.Fori(0, NPAIR) as i:
                                for k in range(2):
                                    act_e.wait_ge(read[k].sem, read[k].at(i * CP))
                                    for m, step in enumerate(given):
                                        for j in range(2):
                                            cell = bass.ds(i * (4 * CP) + (k * CP + step) * 2 + j, 1)
                                            ins = act_e.activation(lent5[:, k, m, j, :], iota_row[:, :], ACT.Abs,
                                                                   scale=-1.0, bias=dloc_e[:, cell])
                                    ins.then_inc(lent_chain.sem, 1)
                                    act_e.wait_ge(lent_chain.sem, lent_chain.at(i * 2 + k + 1))
                                    whole = lent5[:, k].rearrange("p m j n -> p (m j n)")
                                    act_e.activation(whole, whole, ACT.Relu, scale=-1.0, bias=ones[:, 0:1])\
                                         .then_inc(lent_ready[k].sem, 1)
                            last(act_e)
                steps = NCH * CP
                hots_made = NCH * len(OWN) + AHEAD
                if shared:
                    stage_end(ag_lent0=NPAIR, ag_lent1=NPAIR, ag_lent_chain=NCH)
                in_turn = 0 if ring else NPAIR * CP
                stage_end(ag_hot=hots_made, ag_read0=in_turn, ag_read1=in_turn, ag_added=steps,
                          ag_cleared=1 if clear else 0)

        def conv_sums(acc, weight, with_edges, fetch):
            done = ExitStack()
            with done:
                vb = sb(done, "vb", [P, 2 * CB * D])
                pv = sb(done, "pv", [P, 2 * CB * ACCW])
                eb = sb(done, "eb", [P, 2 * CB * D]) if with_edges else None
                v_in, pv_made, e_in = ((signal(n + "0"), signal(n + "1")) for n in ("cs_v_in", "cs_pv_made", "cs_e_in"))
                vb4 = vb[:, :].rearrange("p (k s c) -> p k s c", k=2, s=CB)
                pv4 = pv[:, :].rearrange("p (k s c) -> p k s c", k=2, s=CB)
                eb4 = eb[:, :].rearrange("p (k s c) -> p k s c", k=2, s=CB) if with_edges else None
                w3 = weight[:, :].rearrange("p (s h) -> p s h", h=H)
                per_pv = 6
                fetched = signal("cs_fetched")

                def fill(block, read):
                    @block.sync
                    def _(sp):
                        with sp.Fori(0, NPAIR) as i:
                            for k in range(2):
                                sp.wait_ge(pv_made[k].sem, pv_made[k].at(i * per_pv))
                                sp.dma_start(vb4[:, k], v_steps.rearrange("p (s c) -> p s c", c=D)
                                             [:, bass.ds((i * 2 + k) * CB, CB), :]).then_inc(v_in[k].sem, 16)
                                if with_edges:
                                    sp.wait_ge(read[k].sem, read[k].at(i * CP))
                                    _, ts = nc.values_load_multi_w_load_instructions(
                                        pair_of[0:1, bass.ds((i * 2 + k) * CP, CP)],
                                        engines=(mybir.EngineType.SP,), min_val=0, max_val=NTP)
                                    for m in range(CP):
                                        sp.dma_start(eb4[:, k, 2 * m:2 * m + 2, :],
                                                     a["edge_attr"][bass.ds(ts[m] * (2 * P), 2 * P), :]
                                                     .rearrange("(j e) c -> e j c", j=2)).then_inc(e_in[k].sem, 16)

                    @block.gpsimd
                    def _(pool):
                        with pool.Fori(0, NPAIR) as i:
                            for k in range(2):
                                pool.wait_ge(read[k].sem, read[k].at(i * CP))
                                pool.wait_ge(v_in[k].sem, v_in[k].at((i + 1) * 16))
                                chunk = bass.ds((i * 2 + k) * CB, CB)
                                for h in range(H):
                                    pool.tensor_tensor(pv4[:, k, :, h * C:(h + 1) * C], vb4[:, k, :, h * C:(h + 1) * C],
                                                       w3[:, chunk, h:h + 1].to_broadcast([P, CB, C]), ALU.mult)\
                                        .then_inc(pv_made[k].sem, 1)
                                pool.tensor_copy(pv4[:, k, :, D:D + H], w3[:, chunk, :]).then_inc(pv_made[k].sem, 1)
                                pool.tensor_tensor(pv4[:, k, :, D + H:ACCW], w3[:, chunk, :],
                                                   ew_e[:, chunk].unsqueeze(2).to_broadcast([P, CB, H]), ALU.mult)\
                                    .then_inc(pv_made[k].sem, 1)
                    return [(pv_made, per_pv)] + ([(e_in, 16 * CP)] if with_edges else [])

                def begin_fetch(act_e):
                    for to, of in fetch:
                        act_e.dma_start(to, of).then_inc(fetched.sem, 16)

                def end_fetch(act_e):
                    act_e.wait_ge(fetched.sem, fetched.at(16 * len(fetch)))
                aggregate(acc, ACCW, lambda k, s: pv4[:, k, s, :], fill, shared=(begin_fetch, end_fetch),
                          extra=(lambda k, s: eb4[:, k, s, :]) if with_edges else None, extra_width=D if with_edges else 0)
                stage_end(cs_v_in0=16 * NPAIR, cs_v_in1=16 * NPAIR, cs_pv_made0=per_pv * NPAIR,
                          cs_pv_made1=per_pv * NPAIR, cs_fetched=16 * len(fetch))
                if with_edges:
                    stage_end(cs_e_in0=16 * CP * NPAIR, cs_e_in1=16 * CP * NPAIR)

        def conv_finish(acc, total, y, layer, residual):
            done = ExitStack()
            with done:
                we_b = sb(done, "we_b", [P, D])
                rec = sb(done, "rec", [P, NW * H])
                pe_ = sb(done, "pe_", [P, NW * H])
                loaded, chained, stored = signal("cf_loaded"), signal("cf_chain"), signal("cf_stored")
                acc3 = acc[:, :].rearrange("p (w c) -> p w c", w=NW)
                y3 = y[:, :].rearrange("p (w c) -> p w c", w=NW)
                rec3 = rec[:, :].rearrange("p (w h) -> p w h", h=H)
                pe3 = pe_[:, :].rearrange("p (w h) -> p w h", h=H)
                counts = {}
                with nc.Block() as block:
                    @block.sync
                    def _(sp):
                        sp.dma_start(we_b[:, :], a[f"L0_gnn_We{layer}"][0, :].partition_broadcast(P)).then_inc(loaded.sem, 16)
                        if total > ACCW:
                            sp.dma_start(agg_rows.rearrange("p (w c) -> p w c", w=NW), acc3[:, :, ACCW:total])\
                              .then_inc(stored.sem, 16)
                            sp.wait_ge(stored.sem, stored.at(16))

                    @block.vector
                    def _(dve):
                        link = chain(dve, chained)
                        link(dve.tensor_scalar(rec3, acc3[:, :, D:D + H], 1e-30, None, ALU.max))
                        link(dve.reciprocal(rec[:, :], rec[:, :]))
                        link(dve.tensor_tensor(pe3, acc3[:, :, D + H:ACCW], rec3, ALU.mult))
                        dve.wait_ge(loaded.sem, loaded.at(16))
                        for h in range(H):
                            part, to = acc3[:, :, h * C:(h + 1) * C], y3[:, :, h * C:(h + 1) * C]
                            link(dve.tensor_tensor(part, part, rec3[:, :, h:h + 1].to_broadcast([P, NW, C]), ALU.mult))
                            link(dve.tensor_tensor(to, to, part, ALU.add))
                            link(dve.tensor_tensor(part, pe3[:, :, h:h + 1].to_broadcast([P, NW, C]),
                                                   we_b[:, h * C:(h + 1) * C].unsqueeze(1).to_broadcast([P, NW, C]), ALU.mult))
                            link(dve.tensor_tensor(to, to, part, ALU.add))
                        if residual:
                            link(dve.tensor_tensor(y[:, :], y[:, :], x[:, :], ALU.add))
                        counts["chain"] = link.count[0]
                stage_end(cf_loaded=16, cf_chain=counts["chain"], cf_stored=16 if total > ACCW else 0)

        def norm_steps(dve, link, scratch, y, to, centred, squared):
            _, mean, var, eps = scratch
            link(dve.memset(eps[:, :], EPS))
            for g in range(NG):
                ws = slice(g * G, (g + 1) * G)
                link(dve.tensor_reduce(mean[:, ws], y[:, g * G * D:(g + 1) * G * D].rearrange("p (w c) -> p w c", c=D),
                                       AX.X, ALU.add))
                link(dve.tensor_scalar(mean[:, ws], mean[:, ws], -1.0 / D, None, ALU.mult))
                dve.sem_inc(centred.sem, 1)
            for g in range(NG):
                ws = slice(g * G, (g + 1) * G)
                dve.wait_ge(squared.sem, squared.at(2 * (g + 1)))
                link(dve.reciprocal(var[:, ws], var[:, ws]))
                for w in range(g * G, (g + 1) * G):
                    last = dve.tensor_scalar(to[:, w * D:(w + 1) * D], y[:, w * D:(w + 1) * D], mean[:, w:w + 1],
                                             var[:, w:w + 1], ALU.add, ALU.mult)
                link(last)

        def norm_squares(act_e, scratch, y, centred, squared):
            sq, mean, var, eps = scratch
            for g in range(NG):
                act_e.wait_ge(centred.sem, centred.at(g + 1))
                for w in range(g * G, (g + 1) * G):
                    last = act_e.activation(sq[:, w * D:(w + 1) * D], y[:, w * D:(w + 1) * D], ACT.Square,
                                            bias=mean[:, w:w + 1], accum_out=var[:, w:w + 1])
                last.then_inc(squared.sem, 1)
                act_e.wait_ge(squared.sem, squared.at(2 * g + 1))
                ws = slice(g * G, (g + 1) * G)
                act_e.activation(var[:, ws], var[:, ws], ACT.Sqrt, bias=eps[:, :], scale=1.0 / D).then_inc(squared.sem, 1)

        def norm_scratch(stack):
            return (sb(stack, "ln_sq", [P, NW * D]), sb(stack, "ln_mean", [P, NW]), sb(stack, "ln_var", [P, NW]),
                    sb(stack, "ln_eps", [P, 1]))

        def norm_group(dve, link, y, sq, sums, squares, to, std_needed, std_ready, n):
            over = lambda t: t[:, :].unsqueeze(2).to_broadcast([P, G, D])
            link(dve.tensor_reduce(sums[:, :], y, AX.X, ALU.add))
            link(dve.scalar_tensor_tensor(y, over(sums), -1.0 / D, y, ALU.mult, ALU.add))
            link(dve.tensor_tensor(sq, y, y, ALU.mult))
            link(dve.tensor_reduce(squares[:, :], sq, AX.X, ALU.add))
            link(dve.tensor_scalar(squares[:, :], squares[:, :], 1.0 / D, EPS, ALU.mult, ALU.add))
            dve.sem_inc(std_needed.sem, 1)
            dve.wait_ge(std_ready.sem, std_ready.at(n))
            link(dve.reciprocal(squares[:, :], squares[:, :]))
            link(dve.tensor_tensor(to, y, over(squares), ALU.mult))

        def layer_norm(y):
            done = ExitStack()
            with done:
                scratch = norm_scratch(done)
                chained, centred, squared = signal("ln_chain"), signal("ln_centred"), signal("ln_squared")
                counts = {}
                with nc.Block() as block:
                    @block.vector
                    def _(dve):
                        link = chain(dve, chained)
                        norm_steps(dve, link, scratch, y, x, centred, squared)
                        counts["chain"] = link.count[0]

                    @block.scalar
                    def _(act_e):
                        norm_squares(act_e, scratch, y, centred, squared)
                stage_end(ln_chain=counts["chain"], ln_centred=NG, ln_squared=2 * NG)

        def mlp_layer():
            done = ExitStack()
            with done:
                w1 = sb(done, "w1", [P, 2 * 2 * D])
                w2 = sb(done, "w2", [P, 2 * D])
                b1 = sb(done, "b1", [P, 2])
                b2_b = sb(done, "b2_b", [P, D])
                gamma_b = sb(done, "gamma_b", [P, D])
                beta_b = sb(done, "beta_b", [P, D])
                xg = sb(done, "xg", [P, 2 * G * D])
                xt = sb(done, "xt", [P, 2 * G * D])
                ht = sb(done, "ht", [P, 2 * G * D])
                base = sb(done, "base", [P, G * D])
                y = sb(done, "y", [P, G * D])
                sq = sb(done, "sq", [P, G * D])
                sums, squares = sb(done, "sums", [P, G]), sb(done, "squares", [P, G])
                ps_x = pb(done, "ps_x", [P, 1024])
                ps_h = pb(done, "ps_h", [P, 4 * 512])
                ps_y = pb(done, "ps_y", [P, 1024])
                (loaded, got_x, got_agg, turned, xt_ready, hidden, silued, made, added, chained, based, normed) = (
                    signal(n) for n in ("ml_loaded", "ml_got_x", "ml_got_agg", "ml_turned", "ml_xt", "ml_hidden", "ml_silued",
                                        "ml_made", "ml_added", "ml_chain", "ml_based", "ml_normed"))
                needed, ready = signal("ln_needed"), signal("ln_ready")
                GD = G * D
                HALF = GD // 2
                LINKS = 16
                by_window = lambda t: t[:, :].unsqueeze(1).to_broadcast([P, G, D])
                with nc.Block() as block:
                    @block.sync
                    def _(sp):
                        loads = [(w1[:, 0:2 * D], a["L1_gnn_W1"][0:D, :]),
                                 (w1[:, 2 * D:4 * D], a["L1_gnn_W1"][D:2 * D, :]), (w2[:, 0:D], a["L1_gnn_W2"][0:D, :]),
                                 (w2[:, D:2 * D], a["L1_gnn_W2"][D:2 * D, :]), (b1[:, :], a["L1_gnn_b1"]),
                                 (b2_b[:, :], a["L1_gnn_b2"].partition_broadcast(P)),
                                 (gamma_b[:, :], a["L1_gnn_ln_gamma"].partition_broadcast(P)),
                                 (beta_b[:, :], a["L1_gnn_ln_beta"].partition_broadcast(P))]
                        for to, of in loads:
                            sp.dma_start(to, of).then_inc(loaded.sem, 16)
                        with sp.Fori(0, NG) as g:
                            sp.wait_ge(turned.sem, turned.at(g * 2))
                            sp.dma_start(xg[:, GD:2 * GD], agg_rows[:, bass.ds(g * GD, GD)]).then_inc(got_agg.sem, 16)

                    @block.gpsimd
                    def _(pool):
                        pool.wait_ge(loaded.sem, 16 * 8)
                        with pool.Fori(0, NG) as g:
                            pool.wait_ge(turned.sem, turned.at(g * 2))
                            pool.wait_ge(based.sem, based.at(g))
                            pool.tensor_copy(xg[:, 0:GD], x[:, bass.ds(g * GD, GD)]).then_inc(got_x.sem, 1)
                            pool.wait_ge(got_x.sem, got_x.at(g + 1))
                            pool.wait_ge(normed.sem, normed.at(g))
                            pool.tensor_tensor(grouped(base), xg[:, 0:GD].rearrange("p (g c) -> p g c", g=G),
                                               by_window(beta_b), ALU.add).then_inc(based.sem, 1)

                    @block.scalar
                    def _(act_e):
                        act_e.wait_ge(loaded.sem, 16 * 8)

                        def root(n):
                            act_e.wait_ge(needed.sem, needed.at(n))
                            act_e.activation(squares[:, :], squares[:, :], ACT.Sqrt).then_inc(ready.sem, 1)

                        def group(g, roots_too):
                            for n in range(2):
                                act_e.wait_ge(turned.sem, turned.at(g * 2 + n + 1))
                                act_e.wait_ge(hidden.sem, hidden.at(g * 4))
                                act_e.copy(xt[:, n * GD:(n + 1) * GD], ps_x[:, 0:GD]).then_inc(xt_ready.sem, 1)
                            if roots_too:
                                root(g * 2 - 1)
                            for n in range(4):
                                j, half = divmod(n, 2)
                                act_e.wait_ge(hidden.sem, hidden.at(g * 4 + n + 1))
                                act_e.wait_ge(made.sem, made.at(g))
                                act_e.activation(ht[:, j * GD + half * HALF:j * GD + (half + 1) * HALF],
                                                 ps_h[:, n * 512:n * 512 + HALF], ACT.Silu, bias=b1[:, j:j + 1])\
                                     .then_inc(silued.sem, 1)
                            if roots_too:
                                root(g * 2)
                        group(0, False)
                        with act_e.Fori(1, NG) as g:
                            group(g, True)
                        root(2 * NG - 1)
                        root(2 * NG)

                    @block.tensor
                    def _(pe):
                        def turn(g, n):
                            if n == 0:
                                pe.wait_ge(got_x.sem, got_x.at(g + 1))
                            else:
                                pe.wait_ge(got_agg.sem, got_agg.at((g + 1) * 16))
                            pe.wait_ge(xt_ready.sem, xt_ready.at(g * 2 + n))
                            for j in range(G):
                                at = n * GD + j * D
                                last_mm = pe.transpose(ps_x[:, j * D:(j + 1) * D], xg[:, at:at + D], ident[:, :])
                            last_mm.then_inc(turned.sem, 1)

                        def products(g, more):
                            pe.wait_ge(xt_ready.sem, xt_ready.at(g * 2 + 2))
                            pe.wait_ge(silued.sem, silued.at(g * 4))
                            for n in range(4):
                                j, half = divmod(n, 2)
                                for k in range(2):
                                    last_mm = pe.matmul(ps_h[:, n * 512:n * 512 + HALF],
                                                        w1[:, k * 2 * D + j * D:k * 2 * D + (j + 1) * D],
                                                        xt[:, k * GD + half * HALF:k * GD + (half + 1) * HALF],
                                                        start=(k == 0), stop=(k == 1))
                                last_mm.then_inc(hidden.sem, 1)
                            if more:
                                turn(g + 1, 0)
                            pe.wait_ge(silued.sem, silued.at(g * 4 + 4))
                            pe.wait_ge(added.sem, added.at(g))
                            for w in range(G):
                                for j in range(2):
                                    last_mm = pe.matmul(ps_y[:, w * D:(w + 1) * D], ht[:, j * GD + w * D:j * GD + (w + 1) * D],
                                                        w2[:, j * D:(j + 1) * D], start=(j == 0), stop=(j == 1))
                            last_mm.then_inc(made.sem, 1)
                            if more:
                                turn(g + 1, 1)
                        pe.wait_ge(loaded.sem, 16 * 8)
                        for n in range(2):
                            turn(0, n)
                        with pe.Fori(0, NG - 1) as g:
                            products(g, True)
                        products(NG - 1, False)

                    @block.vector
                    def _(dve):
                        dve.wait_ge(loaded.sem, 16 * 8)
                        with dve.Fori(0, NG) as g:
                            link = chain(dve, chained, g * LINKS)
                            dve.wait_ge(made.sem, made.at(g + 1))
                            dve.tensor_tensor(grouped(y), ps_y[:, 0:GD].rearrange("p (g c) -> p g c", g=G),
                                              by_window(b2_b), ALU.add).then_inc(added.sem, 1)
                            dve.wait_ge(added.sem, added.at(g + 1))
                            norm_group(dve, link, grouped(y), grouped(sq), sums, squares, grouped(y), needed, ready, g * 2 + 1)
                            link(dve.tensor_tensor(grouped(y), grouped(y), by_window(gamma_b), ALU.mult))
                            dve.wait_ge(based.sem, based.at(g + 1))
                            dve.tensor_tensor(y[:, :], y[:, :], base[:, :], ALU.add).then_inc(normed.sem, 1)
                            dve.wait_ge(normed.sem, normed.at(g + 1))
                            link(dve.tensor_tensor(y[:, :], y[:, :], x[:, bass.ds(g * GD, GD)], ALU.add))
                            norm_group(dve, link, grouped(y), grouped(sq), sums, squares, grouped_at(x, g), needed, ready,
                                       g * 2 + 2)
                            assert link.count[0] == LINKS
                stage_end(ln_needed=2 * NG, ln_ready=2 * NG)

        def grouped_at(t, g):
            return t[:, bass.ds(g * (G * D), G * D)].rearrange("p (g c) -> p g c", g=G)

        def relation_weights(wrel, rel_b, tables_back):
            done = ExitStack()
            with done:
                basis = sb(done, "basis", [NBASIS, 2 * (2 * D + RD)])
                coef = sb(done, "coef", [NBASIS, 2 * R16])
                emb = sb(done, "emb", [RD, R16])
                bias_b = sb(done, "bias_b", [P, 2 * R16])
                prod = sb(done, "prod", [RD, 2 * R16])
                ps_w = pb(done, "ps_w", [P, 512])
                ps_r = pb(done, "ps_r", [P, 512])
                loaded, made, chained = signal("rw_loaded"), signal("rw_made"), signal("rw_chain")
                IN = 2 * D + RD
                with nc.Block() as block:
                    @block.sync
                    def _(sp):
                        loads = [(emb[:, :], a["edge_embeddings_t"])]
                        loads += [(to[:, :], of) for to, of in tables_back]
                        for n, k in enumerate("sr"):
                            loads += [(basis[:, n * IN:(n + 1) * IN], a[f"L2_gnn_basis_{k}"]),
                                      (coef[:, n * R16:(n + 1) * R16], a[f"coef_{k}_t"]),
                                      (bias_b[:, n * R16:(n + 1) * R16], a[f"L2_gnn_b_{k}"].partition_broadcast(P))]
                        for to, of in loads:
                            sp.dma_start(to, of).then_inc(loaded.sem, 16)

                    @block.tensor
                    def _(pe):
                        pe.wait_ge(loaded.sem, 16 * 10)
                        for n in range(2):
                            c = coef[:, n * R16:(n + 1) * R16]
                            for m in range(2):
                                at = (2 * n + m) * R16
                                pe.matmul(ps_w[:, at:at + R16], basis[:, n * IN + m * D:n * IN + (m + 1) * D], c,
                                          start=True, stop=True)
                            last_mm = pe.matmul(ps_r[0:RD, n * R16:(n + 1) * R16], basis[:, n * IN + 2 * D:(n + 1) * IN], c,
                                                start=True, stop=True)
                        last_mm.then_inc(made.sem, 1)
                        pe.wait_ge(chained.sem, 3)
                        pe.matmul(ps_w[:, 256:256 + 2 * R16], ones[0:RD, :], prod[:, :], start=True, stop=True)\
                          .then_inc(made.sem, 1)

                    @block.vector
                    def _(dve):
                        link = chain(dve, chained)
                        dve.wait_ge(made.sem, 1)
                        link(dve.tensor_copy(wrel[:, :], ps_w[:, 0:4 * R16]))
                        for n in range(2):
                            link(dve.tensor_tensor(prod[:, n * R16:(n + 1) * R16], ps_r[0:RD, n * R16:(n + 1) * R16],
                                                   emb[:, :], ALU.mult))
                        dve.wait_ge(made.sem, 2)
                        link(dve.tensor_tensor(rel_b[:, :], ps_w[:, 256:256 + 2 * R16], bias_b[:, :], ALU.add))

        def relation_project(wrel, rel_b, dsplit, xnm):
            done = ExitStack()
            with done:
                s_out = sb(done, "s_out", [P, G * R16])
                d_out = sb(done, "d_out", [P, G * R16])
                nm_out = sb(done, "nm_out", [P, G * 2 * R16])
                rest = sb(done, "rest", [P, G * R16])
                parts = sb(done, "parts", [P, 3 * G * R16], BF16)
                d3 = dsplit[:, :].rearrange("p (w k c) -> p w k c", k=3, c=R16)

                def window(dve, y, j):
                    dve.tensor_copy(grouped(s_out)[:, j, :], y[:, 0:R16])
                    dve.tensor_tensor(grouped(d_out)[:, j, :], y[:, R16:2 * R16], rel_b[:, 0:R16], ALU.add)
                    return dve.tensor_copy(grouped(nm_out)[:, j, :], y[:, 2 * R16:4 * R16])

                def group(dve, g, link):
                    split3(dve, link, d_out, rest, parts)
                    link(dve.tensor_copy(xnm[:, bass.ds(g * (G * 2 * R16), G * 2 * R16)], nm_out[:, :]))

                def keep(act_e, g):
                    return act_e.copy(d3[:, bass.ds(g * G, G), :, :],
                                            parts[:, :].rearrange("p (k g c) -> p g k c", k=3, g=G))

                def stores(g, lo, hi):
                    return [(score_table.rearrange("(w p) c -> p w c", p=P)[:, bass.ds(g * G + lo, hi - lo), :],
                             grouped(s_out)[:, lo:hi, :])]
                project(x, wrel, 4 * R16, lambda sp, sig: None, 0, stores, window, group, 5, keep=keep)

        def relation_scores(dsplit, score, src_t, typed, src16_tiles, et16_e):
            done = ExitStack()
            with done:
                CT = 28
                ROUNDS = TILES // (2 * CT)
                TB = 112
                assert TILES % (2 * CT) == 0 and TILES % TB == 0 and TILES // TB * P <= 1024
                idx = sb(done, "idx", [P, 2 * CT], I32)
                from_src = sb(done, "from_src", [P, 2 * CT])
                src_scores = sb(done, "src_scores", [P, TILES])
                src_rows = sb(done, "src_rows", [TB, TILES // TB * P])
                dl_row = sb(done, "dl_row", [P, 2 * CB * P], BF16)
                st = sb(done, "st", [P, 2 * CB * P], BF16)
                picked = sb(done, "picked", [P, CB * R16])
                ps_d = pb(done, "ps_d", [P, 2 * 512])
                ps_r = pb(done, "ps_r", [P, 2 * 512])
                idx_ready, de_made, chained, turned, copied, stored, back = (signal(n) for n in (
                    "rs_idx", "rs_de_made", "rs_chain", "rs_turned", "rs_copied", "rs_stored", "rs_back"))
                st_made = (signal("rs_st0"), signal("rs_st1"))
                issuing = signal("issuing")
                kept = (signal("rs_kept0"), signal("rs_kept1"))
                gathered, dl_in, summed = ((signal(n + "0"), signal(n + "1")) for n in ("rs_gathered", "rs_dl_in", "rs_summed"))
                st4 = st[:, :].rearrange("p (k s e) -> p k s e", k=2, s=CB)
                dl3 = dl_row[:, :].rearrange("p (k n) -> p k n", k=2)
                r3 = lambda t: t[:, :].rearrange("p (s r) -> p s r", r=R16)
                ps4 = ps_d[:, :].rearrange("p (k c) -> p k c", k=2)[:, :, 0:CB * R16]
                flat_scores = score_table.rearrange("n (r o) -> (n r) o", o=1)
                with nc.Block() as block:
                    @block.gpsimd
                    def _(pool):
                        with pool.Fori(0, ROUNDS) as i:
                            for k in range(2):
                                pool.wait_ge(kept[k].sem, kept[k].at(i))
                                pool.tensor_copy(idx[:, k * CT:(k + 1) * CT], src16_tiles[:, bass.ds((i * 2 + k) * CT, CT)])\
                                    .then_inc(idx_ready.sem, 1)
                                pool.wait_ge(idx_ready.sem, idx_ready.at(i * 2 + k + 1))
                                pool.sem_inc(issuing.sem, 1)
                                for s in range(k * CT, (k + 1) * CT):
                                    pool.indirect_dma_start(
                                        from_src[:, s:s + 1], None, flat_scores,
                                        bass.IndirectOffsetOnAxis(ap=idx[:, s:s + 1], axis=0)).then_inc(gathered[k].sem, 16)
                        pool.wait_ge(stored.sem, 16)
                        for b in range(SB):
                            pool.indirect_dma_start(src_t[:, b * P:(b + 1) * P], None, src_score_rows,
                                                    bass.IndirectOffsetOnAxis(ap=tile_t_i[:, b:b + 1], axis=0))\
                                .then_inc(back.sem, 16)
                        pool.wait_ge(back.sem, 16 * SB)

                    @block.sync
                    def _(sp):
                        with sp.Fori(0, NPAIR) as i:
                            for k in range(2):
                                sp.wait_ge(st_made[k].sem, st_made[k].at(i))
                                sp.dma_start(dl3[:, k, :], dloc_slots[0, bass.ds((i * 2 + k) * (CB * P), CB * P)]
                                             .partition_broadcast(P)).then_inc(dl_in[k].sem, 16)
                        sp.wait_ge(copied.sem, 1)
                        sp.dma_start(src_score_rows.rearrange("(b t) e -> t b e", t=TB),
                                     src_rows[:, :].rearrange("t (b e) -> t b e", e=P)).then_inc(stored.sem, 16)

                    @block.scalar
                    def _(act_e):
                        with act_e.Fori(0, ROUNDS) as i:
                            for k in range(2):
                                act_e.wait_ge(gathered[k].sem, gathered[k].at((i + 1) * (16 * CT)))
                                act_e.copy(src_scores[:, bass.ds((i * 2 + k) * CT, CT)], from_src[:, k * CT:(k + 1) * CT])\
                                    .then_inc(kept[k].sem, 1)
                        act_e.wait_ge(turned.sem, 1)
                        act_e.copy(src_rows[:, :], ps_r[0:TB, 0:TILES // TB * P]).then_inc(copied.sem, 1)

                    @block.tensor
                    def _(pe):
                        with pe.Fori(0, NPAIR) as i:
                            for k in range(2):
                                pe.wait_ge(st_made[k].sem, st_made[k].at(i + 1))
                                pe.wait_ge(summed[k].sem, summed[k].at(i))
                                _, ws = nc.values_load_multi_w_load_instructions(
                                    window_of[0:1, bass.ds((i * 2 + k) * CP, CP)],
                                    engines=(mybir.EngineType.PE,), min_val=0, max_val=NW - 1)
                                for s in range(CB):
                                    for part in range(3):
                                        last_mm = pe.matmul(ps4[:, k, s * R16:(s + 1) * R16], st4[:, k, s, :],
                                                            dsplit[:, bass.ds(ws[s // 2] * (3 * R16) + part * R16, R16)],
                                                            start=(part == 0), stop=(part == 2))
                                last_mm.then_inc(de_made.sem, 1)
                        for k in range(2):
                            pe.wait_ge(kept[k].sem, kept[k].at(ROUNDS))
                        for b in range(TILES // TB):
                            last_mm = pe.transpose(ps_r[0:TB, b * P:(b + 1) * P], src_scores[:, b * TB:(b + 1) * TB], ident[:, :])
                        last_mm.then_inc(turned.sem, 1)

                    @block.vector
                    def _(dve):
                        dve.memset(score[:, NCH * CB:], 0.0)
                        L = 3
                        with dve.Fori(0, NPAIR) as i:
                            for k in range(2):
                                link = chain(dve, chained, i * (2 * L) + k * L)
                                chunk = bass.ds((i * 2 + k) * CB, CB)
                                dve.wait_ge(dl_in[k].sem, dl_in[k].at((i + 1) * 16))
                                dve.wait_ge(de_made.sem, de_made.at(i * 2))
                                dve.tensor_scalar(st4[:, k].rearrange("p s e -> p (s e)"), dl3[:, k, :], iota_col[:, :],
                                                  None, ALU.is_equal).then_inc(st_made[k].sem, 1)
                                link(dve.tensor_tensor(r3(typed)[:, chunk, :], et16_e[:, chunk].unsqueeze(2).to_broadcast([P, CB, R16]),
                                                       iota_row[:, 0:R16].unsqueeze(1).to_broadcast([P, CB, R16]),
                                                       ALU.is_equal))
                                dve.wait_ge(de_made.sem, de_made.at(i * 2 + k + 1))
                                link(dve.tensor_tensor(picked[:, :], ps4[:, k, :], typed[:, bass.ds((i * 2 + k) * (CB * R16), CB * R16)],
                                                       ALU.mult))
                                link(dve.tensor_reduce(score[:, chunk], r3(picked), AX.X, ALU.add))
                                dve.sem_inc(summed[k].sem, 1)

        def relation_sums(acc, weight, typed):
            done = ExitStack()
            with done:
                parts = sb(done, "parts", [P, 3 * SP], BF16)
                rest = sb(done, "rest", [P, SP])
                iota_b = sb(done, "iota_b", [P, P], BF16)
                zeros = sb(done, "zeros", [P, 512], BF16)
                onehot = sb(done, "onehot", [P, 2 * CB * P], BF16)
                wb = sb(done, "wb", [P, 2 * 3 * CB * R16], BF16)
                ps_a = pb(done, "ps_a", [P, 2 * 512])
                chained, split, done_all = signal("rr_chain"), signal("rr_split"), signal("rr_done")
                zeroed = signal("rr_zeroed")
                made, hot, read = ((signal(n + "0"), signal(n + "1")) for n in ("rr_made", "rr_hot", "rr_read"))
                t3 = typed[:, :].rearrange("p (s r) -> p s r", r=R16)
                p3 = parts[:, :].rearrange("p (k s) -> p k s", k=3)
                w5 = wb[:, :].rearrange("p (b k s r) -> p b k s r", b=2, k=3, s=CB)
                one4 = onehot[:, :].rearrange("p (b s n) -> p b s n", b=2, s=CB)
                assert 512 % R16 == 0 and NW * R16 <= 2 * 512
                with nc.Block() as block:
                    @block.gpsimd
                    def _(pool):
                        pool.wait_ge(split.sem, split.at(1))
                        with pool.Fori(0, NPAIR) as i:
                            for b in range(2):
                                chunk = bass.ds((i * 2 + b) * CB, CB)
                                pool.wait_ge(read[b].sem, read[b].at(i))
                                for k in range(3):
                                    last = pool.tensor_tensor(w5[:, b, k], t3[:, chunk, :], p3[:, k, chunk].unsqueeze(2)
                                                              .to_broadcast([P, CB, R16]), ALU.mult)
                                last.then_inc(made[b].sem, 1)

                    @block.tensor
                    def _(pe):
                        pe.wait_ge(zeroed.sem, zeroed.at(1))
                        for c in range(0, NW * R16, 512):
                            n = min(512, NW * R16 - c)
                            last_mm = pe.matmul(ps_a[:, c:c + n], zeros[:, 0:P], zeros[:, 0:n], start=True, stop=True)
                        last_mm.then_inc(zeroed.sem, 1)
                        pe.wait_ge(zeroed.sem, zeroed.at(2))
                        with pe.Fori(0, NPAIR) as i:
                            for b in range(2):
                                _, ws = nc.values_load_multi_w_load_instructions(
                                    window_of[0:1, bass.ds((i * 2 + b) * CP, CP)],
                                    engines=(mybir.EngineType.PE,), min_val=0, max_val=NW - 1)
                                pe.wait_ge(hot[b].sem, hot[b].at(i + 1))
                                pe.wait_ge(made[b].sem, made[b].at(i + 1))
                                for s in range(CB):
                                    for k in range(3):
                                        last_mm = pe.matmul(ps_a[:, bass.ds(ws[s // 2] * R16, R16)], one4[:, b, s, :],
                                                            w5[:, b, k, s, :], start=False, stop=True, skip_group_check=True)
                                last_mm.then_inc(read[b].sem, 1)

                    @block.vector
                    def _(dve):
                        link = chain(dve, chained)
                        dve.memset(zeros[:, :], 0.0).then_inc(zeroed.sem, 1)
                        link(dve.tensor_copy(iota_b[:, :], iota_row[:, :]))
                        link(dve.tensor_copy(p3[:, 0], weight[:, :]))
                        link(dve.tensor_tensor(rest[:, :], weight[:, :], p3[:, 0], ALU.subtract))
                        link(dve.tensor_copy(p3[:, 1], rest[:, :]))
                        link(dve.tensor_tensor(p3[:, 2], rest[:, :], p3[:, 1], ALU.subtract))
                        dve.sem_inc(split.sem, 1)
                        with dve.Fori(0, NPAIR) as i:
                            for b in range(2):
                                dve.wait_ge(read[b].sem, read[b].at(i))
                                for s in range(CB):
                                    last = dve.tensor_scalar(one4[:, b, s, :], iota_b[:, :],
                                                             dloc_e[:, bass.ds((i * 2 + b) * CB + s, 1)], None, ALU.is_equal)
                                last.then_inc(hot[b].sem, 1)
                        for b in range(2):
                            dve.wait_ge(read[b].sem, read[b].at(NPAIR))
                        dve.tensor_copy(acc[:, :], ps_a[:, 0:NW * R16]).then_inc(done_all.sem, 1)
                        dve.wait_ge(done_all.sem, done_all.at(1))

        def relation_finish(acc, rel_b, xnm):
            done = ExitStack()
            with done:
                y = sb(done, "y", [P, NW * D])
                scratch = norm_scratch(done)
                share, present, rel, tmp = (sb(done, n, [P, NW * R16]) for n in ("share", "present", "rel", "tmp"))
                top = sb(done, "top", [P, NW])
                chained, centred, squared = signal("rf_chain"), signal("ln_centred"), signal("ln_squared")
                exp_needed, exp_ready = signal("rf_exp_needed"), signal("rf_exp_ready")
                xnm3 = xnm[:, :].rearrange("p (w c) -> p w c", w=NW)
                r3 = lambda t: t[:, :].rearrange("p (w r) -> p w r", w=NW)
                over = lambda t, n: t[:, :].unsqueeze(2).to_broadcast([P, NW, n])
                with nc.Block() as block:
                    @block.vector
                    def _(dve):
                        link = chain(dve, chained)
                        link(dve.tensor_scalar(present[:, :], acc[:, :], 0.5, None, ALU.is_gt))
                        link(dve.tensor_scalar(share[:, :], acc[:, :], 1e-30, None, ALU.max))
                        link(dve.reciprocal(share[:, :], share[:, :]))
                        link(dve.tensor_tensor(share[:, :], share[:, :], acc[:, :], ALU.mult))
                        link(dve.tensor_tensor(r3(rel), r3(share), xnm3[:, :, R16:2 * R16], ALU.mult))
                        link(dve.tensor_tensor(r3(rel), r3(rel), xnm3[:, :, 0:R16], ALU.add))
                        link(dve.tensor_tensor(r3(rel), r3(rel), rel_b[:, R16:2 * R16].unsqueeze(1)
                                               .to_broadcast([P, NW, R16]), ALU.add))
                        link(dve.tensor_tensor(rel[:, :], rel[:, :], present[:, :], ALU.mult))
                        link(dve.tensor_scalar(tmp[:, :], present[:, :], -1.0, 1e10, ALU.add, ALU.mult))
                        link(dve.tensor_tensor(rel[:, :], rel[:, :], tmp[:, :], ALU.add))
                        link(dve.tensor_reduce(top[:, :], r3(rel), AX.X, ALU.max))
                        link(dve.tensor_tensor(r3(rel), r3(rel), over(top, R16), ALU.subtract))
                        dve.sem_inc(exp_needed.sem, 1)
                        dve.wait_ge(exp_ready.sem, 1)
                        link(dve.tensor_reduce(top[:, :], r3(rel), AX.X, ALU.add))
                        link(dve.reciprocal(top[:, :], top[:, :]))
                        link(dve.tensor_tensor(rel[:, :], rel[:, :], share[:, :], ALU.mult))
                        link(dve.tensor_tensor(r3(rel), r3(rel), over(top, R16), ALU.mult))
                        link(dve.tensor_reduce(top[:, :], r3(rel), AX.X, ALU.add))
                        link(dve.tensor_scalar(top[:, :], top[:, :], 2.0, None, ALU.add))
                        link(dve.tensor_tensor(y[:, :].rearrange("p (w c) -> p w c", w=NW),
                                               x[:, :].rearrange("p (w c) -> p w c", w=NW), over(top, D), ALU.mult))
                        norm_steps(dve, link, scratch, y, x, centred, squared)

                    @block.scalar
                    def _(act_e):
                        act_e.wait_ge(exp_needed.sem, 1)
                        act_e.activation(rel[:, :], rel[:, :], ACT.Exp).then_inc(exp_ready.sem, 1)
                        norm_squares(act_e, scratch, y, centred, squared)
                stage_end(ln_centred=NG, ln_squared=2 * NG)

        def rgcn_project(src, layer, acc, src4_tiles):
            done = ExitStack()
            with done:
                w_all = sb(done, "w_all", [P, (R4 + 1) * D])
                b_b = sb(done, "b_b", [P, D])
                y_out = sb(done, "y_out", [P, G * R4 * D])
                root = sb(done, "root", [P, G * D])

                def load(sp, sig):
                    for r in range(R4):
                        sp.dma_start(w_all[:, r * D:(r + 1) * D], a[f"L3_gnn_W{layer}"][r]).then_inc(sig.sem, 16)
                    sp.dma_start(w_all[:, R4 * D:], a[f"L3_gnn_root{layer}"]).then_inc(sig.sem, 16)
                    sp.dma_start(src4_tiles[:, :], src4_idx).then_inc(sig.sem, 16)
                    sp.dma_start(b_b[:, :], a[f"L3_gnn_b{layer}"].partition_broadcast(P)).then_inc(sig.sem, 16)

                def window(dve, y, j):
                    return dve.tensor_tensor(grouped(root)[:, j, :], y[:, R4 * D:], b_b[:, :], ALU.add)

                def act_window(act_e, y, j):
                    return act_e.copy(grouped(y_out)[:, j, :], y[:, 0:R4 * D])

                def group(dve, g, link):
                    if layer == 2:
                        link(dve.tensor_tensor(grouped_at(acc, g), grouped_at(x, g), grouped(root), ALU.add))
                    else:
                        link(dve.tensor_copy(grouped_at(acc, g), grouped(root)))

                def stores(g, lo, hi):
                    return [(rel_table.rearrange("(w p) c -> p w c", p=P)[:, bass.ds(g * G + lo, hi - lo), :],
                             grouped(y_out)[:, lo:hi, :])]
                project(src, w_all, (R4 + 1) * D, load, R4 + 3, stores, window, group, 1,
                        act_window=act_window, relu=layer == 2)

        def rgcn_sums(acc, src4_tiles):
            done = ExitStack()
            with done:
                idx = sb(done, "idx", [P, 2 * RP], I32)
                rows_in = sb(done, "rows_in", [P, 2 * RP * D])
                idx_ready, issuing, pairs_in, stepped = (signal(n) for n in ("rg_idx", "issuing", "rg_pairs_in", "rg_stepped"))
                gathered = [signal(f"rg_gathered{c}") for c in range(RP // RC)]
                rows3 = rows_in[:, :].rearrange("p (t c) -> p t c", c=D)
                table = rel_table.rearrange("n (r c) -> (n r) c", c=D)

                def fill(block, read):
                    @block.gpsimd
                    def _(pool):
                        def once_round(i, again):
                            for c in range(RP // RC):
                                pair = i * RP + c * RC
                                if again:
                                    pool.wait_ge(stepped.sem, stepped.at(pair))
                                places = slice(c * 2 * RC, (c + 1) * 2 * RC)
                                pool.tensor_copy(idx[:, places], src4_tiles[:, bass.ds(pair * 2, 2 * RC)])\
                                    .then_inc(idx_ready.sem, 1)
                                pool.wait_ge(idx_ready.sem, idx_ready.at(i * (RP // RC) + c + 1))
                                pool.sem_inc(issuing.sem, 1)
                                for t in range(places.start, places.stop):
                                    pool.indirect_dma_start(
                                        rows3[:, t, :], None, table,
                                        bass.IndirectOffsetOnAxis(ap=idx[:, t:t + 1], axis=0)).then_inc(gathered[c].sem, 16)
                        once_round(0, False)
                        with pool.Fori(1, LAPS) as i:
                            once_round(i, True)

                    @block.sync
                    def _(sp):
                        with sp.Fori(0, LAPS) as i:
                            for c in range(RP // RC):
                                sp.wait_ge(gathered[c].sem, gathered[c].at((i + 1) * (16 * 2 * RC)))
                                sp.sem_inc(pairs_in.sem, RC)
                    return []
                aggregate(acc, D, None, fill, scale=ewn_e, clear=False,
                          ring=(lambda place, j: rows_in[:, bass.ds(place * (2 * D) + j * D, D)], pairs_in, stepped))
                stage_end(rg_idx=LAPS * (RP // RC), rg_pairs_in=LAPS * RP, rg_stepped=NCH * CP,
                          **{f"rg_gathered{c}": 16 * 2 * RC * LAPS for c in range(RP // RC)})

        tables()

        for layer in (1, 2):
            total = ACCW + (D if layer == 1 else 0)
            with ExitStack() as conv:
                alpha = sb(conv, "alpha", [P, SP * H])
                with ExitStack() as scoring:
                    qsplit = sb(scoring, "qsplit", [P, NW * 3 * QW], BF16)
                    conv_project(x, layer, qsplit)
                    conv_scores(qsplit, alpha)
                edge_softmax(alpha, H)
                acc = sb(conv, "acc", [P, NW * total])
                if layer == 1:
                    conv_sums(acc, alpha, True, [(x[:, :], skip_rows)])
                    conv_finish(acc, total, x, layer, residual=False)
                else:
                    y = sb(conv, "y", [P, NW * D])
                    conv_sums(acc, alpha, False, [(y[:, :], skip_rows), (x[:, :], a["x"])])
                    conv_finish(acc, total, y, layer, residual=True)
                    layer_norm(y)
        mlp_layer()
        with ExitStack() as rel:
            rel_b = sb(rel, "rel_b", [P, 2 * R16])
            et16_e = sb(rel, "et16_e", [P, SP])
            et16_t = sb(rel, "et16_t", [P, SP])
            xnm = sb(rel, "xnm", [P, NW * 2 * R16])
            score = sb(rel, "score", [P, SP])
            src_t = sb(rel, "src_t", [P, SP])
            acc = sb(rel, "acc", [P, NW * R16])
            typed = sb(rel, "typed", [P, SP * R16], BF16)
            with ExitStack() as scoring:
                src16_tiles = sb(scoring, "src16_tiles", [P, TILES], I32)
                wrel = sb(scoring, "wrel", [P, 4 * R16])
                dsplit = sb(scoring, "dsplit", [P, NW * 3 * R16], BF16)
                relation_weights(wrel, rel_b, ((src16_tiles, src16_idx), (et16_e, type_rows[0]), (et16_t, type_rows[1])))
                relation_project(wrel, rel_b, dsplit, xnm)
                relation_scores(dsplit, score, src_t, typed, src16_tiles, et16_e)
            edge_softmax(score, R16, src_t, et16_t)
            relation_sums(acc, score, typed)
            relation_finish(acc, rel_b, xnm)
        with ExitStack() as rgcn:
            src4_tiles = sb(rgcn, "src4_tiles", [P, TILES], I32)
            acc1 = sb(rgcn, "acc1", [P, NW * D])
            acc2 = sb(rgcn, "acc2", [P, NW * D])
            rgcn_project(x, 1, acc1, src4_tiles)
            rgcn_sums(acc1, src4_tiles)
            rgcn_project(acc1, 2, acc2, src4_tiles)
            rgcn_sums(acc2, src4_tiles)
            layer_norm(acc2)
        finish(nc, ctx, signal, x, out)


def finish(nc, ctx, signal, x, out):
    stored = signal("out_stored")
    full = N // P
    with nc.Block() as block:
        @block.sync
        def _(sp):
            sp.dma_start(out[0:full * P, :].rearrange("(w p) c -> p w c", p=P),
                         x[:, 0:full * D].rearrange("p (w c) -> p w c", c=D)).then_inc(stored.sem, 16)
            sp.dma_start(out[full * P:N, :], x[0:N - full * P, full * D:(full + 1) * D]).then_inc(stored.sem, 16)
            sp.wait_ge(stored.sem, 32)


def kernel(**inputs):
    import concourse.bacc as bacc
    from concourse.bass_utils import run_bass_kernel_spmd

    pad = 2 * NTP * P - E

    def by_tile(v, fill):
        v = np.asarray(v)
        return np.concatenate([v, np.full(pad + 2 * P, fill, v.dtype)]).reshape(2 * NTP + 2, P)

    arrays = {}
    xs = np.zeros((NPAD, D), np.float32)
    xs[:N] = np.asarray(inputs["x"])
    arrays["x"] = np.ascontiguousarray(xs.reshape(NW, P, D).transpose(1, 0, 2)).reshape(P, NW * D)
    dst = np.asarray(inputs["dst"])
    outside = np.full(1, NOWHERE, np.int32)
    ints = {"dst": by_tile(dst, NOWHERE), "before": by_tile(np.concatenate([outside, dst[:-1]]), NOWHERE),
            "after": by_tile(np.concatenate([dst[1:], outside]), NOWHERE), "src": by_tile(inputs["src"], 0),
            "et16": by_tile(inputs["edge_type_16"], 0)}
    for name, v in (("src_tiles", ints["src"]), ("et4_tiles", by_tile(inputs["edge_type_4"], 0)),
                    ("et16_tiles", ints["et16"])):
        tiles = np.zeros((TILES, P), v.dtype)
        tiles[:len(v)] = v
        arrays[name] = np.ascontiguousarray(tiles.T)
    arrays["int_rows"] = np.concatenate([ints[n] for n in INT_TABLES], axis=1)
    ew = np.asarray(inputs["edge_weight"])
    arrays["ew_rows"] = np.concatenate([ew, np.repeat(ew[-1:], pad + 2 * P)]).reshape(2 * NTP + 2, P)
    last = np.zeros(TC * P, np.int32)
    last[:NTP] = ints["dst"][1:2 * NTP:2, -1]
    arrays["pair_last"] = np.ascontiguousarray(last.reshape(TC, P).T)
    edge_attr = np.zeros(((2 * NTP + 2) * P, D), np.float32)
    edge_attr[:E] = np.asarray(inputs["edge_attr_128"])
    arrays["edge_attr"] = edge_attr
    number = np.full(TC * P, 4 * SP, np.float32)
    number[:NTP] = np.arange(NTP)
    arrays["c_pair_no"] = np.ascontiguousarray(number.reshape(TC, P).T)
    slot = np.arange(SP)
    arrays["c_step_t"] = (slot // 2).astype(np.float32).reshape(P, SB)
    arrays["c_odd_t"] = (slot % 2).astype(np.float32).reshape(P, SB)
    arrays["c_steps_row"] = np.ascontiguousarray(np.broadcast_to((slot // 2).astype(np.float32), (P, SP)))
    arrays["c_iota_row"] = np.ascontiguousarray(np.broadcast_to(np.arange(P, dtype=np.float32), (P, P)))
    arrays["c_iota_col"] = np.arange(P, dtype=np.float32).reshape(P, 1)
    arrays["c_ident"] = np.eye(P, dtype=np.float32)
    for name, v in inputs.items():
        if name.startswith("L"):
            arrays[name] = np.ascontiguousarray(np.asarray(v))
    arrays["L1_gnn_b1"] = np.ascontiguousarray(arrays["L1_gnn_b1"].reshape(2, D).T)
    arrays["edge_embeddings_t"] = np.ascontiguousarray(arrays.pop("L2_gnn_edge_embeddings").T)
    for k in "sr":
        arrays[f"coef_{k}_t"] = np.ascontiguousarray(arrays.pop(f"L2_gnn_coef_{k}").T)

    nc = bacc.Bacc("TRN2", target_bir_lowering=False, num_devices=1)
    a = {name: nc.dram_tensor(f"in_{name}", v.shape, mybir.dt.from_np(v.dtype), kind="ExternalInput").ap()
         for name, v in arrays.items()}
    out = nc.dram_tensor("out_x", (N, D), F32, kind="ExternalOutput").ap()
    gnn_program(nc, a, out)
    result = run_bass_kernel_spmd(nc, [{f"in_{name}": v for name, v in arrays.items()}], core_ids=[0])
    return result.results[0]["out_x"]
```
